# Optimizing a Trainium2 kernel written in Bass

```python
import numpy as np
import jax
import jax.numpy as jnp

def _softmax(x, axis=-1):
    return jax.nn.softmax(x, axis=axis)

def _gelu(x):
    return jax.nn.gelu(x, approximate=True)

def _silu(x):
    return jax.nn.silu(x)

def _sigmoid(x):
    return jax.nn.sigmoid(x)

def _layernorm(x, axis=-1, eps=1e-05):
    m = jnp.mean(x, axis=axis, keepdims=True)
    v = jnp.var(x, axis=axis, keepdims=True)
    return (x - m) / jnp.sqrt(v + eps)

def _scatter_add(tgt, idx, src, axis=0):
    return tgt.at[idx].add(src)

def _segment_sum(src, seg, n):
    return jax.ops.segment_sum(src, seg, n)
kernel_name = 'mk_hybrid_d2_jaxref_r8_6a91c1'

def setup_inputs(seed: int=0):
    np.random.seed(seed)
    _w = jnp.asarray

    def _L0_attn_a_setup():
        import jax, jax.numpy as jnp
        import numpy as np
        EPS = 1e-06
        N_HEADS, N_KV_HEADS = (16, 4)
        HYBRID_RATIO = 0.5
        ROPE_BASE = 10000.0

        def rms(x, w):
            return x * jax.lax.rsqrt(jnp.mean(x * x, axis=-1, keepdims=True) + EPS) * w

        def rotate_half(x):
            x1, x2 = jnp.split(x, 2, axis=-1)
            return jnp.concatenate((-x2, x1), axis=-1)
        key = jax.random.key(seed)
        ks = jax.random.split(key, 20)
        B, L, D = (2, 128, 128)
        N = 128
        R = 64
        hd = D // N_HEADS
        F = 4 * D
        rn = lambda k, s, sc=0.02: jax.random.normal(k, s, jnp.float32) * sc
        return {'x': jax.random.normal(ks[0], (B, L, D), jnp.float32), 'norm_attn_w': jnp.ones((D,), jnp.float32), 'Wq': rn(ks[1], (D, D)), 'Wk': rn(ks[2], (D, N_KV_HEADS * hd)), 'Wv': rn(ks[3], (D, N_KV_HEADS * hd)), 'Wo': rn(ks[4], (D, D)), 'qn_w': jnp.ones((hd,), jnp.float32), 'kn_w': jnp.ones((hd,), jnp.float32), 'ssm_norm_w': jnp.ones((D,), jnp.float32), 'Wx': rn(ks[5], (D, R + 2 * N)), 'Wdt': rn(ks[6], (R, D)), 'bdt': jnp.zeros((D,), jnp.float32), 'A_log': rn(ks[7], (D, N), 0.1), 'Dp': jnp.ones((D,), jnp.float32), 'Wsel': rn(ks[8], (D, D)), 'bsel': jnp.zeros((D,), jnp.float32), 'sel_gate': jnp.ones((D,), jnp.float32), 'Wimp': rn(ks[9], (D, N)), 'bimp': jnp.zeros((N,), jnp.float32), 'Wg': rn(ks[10], (D, D)), 'bg': jnp.zeros((D,), jnp.float32), 'Wout': rn(ks[11], (D, D)), 'norm_ffn_w': jnp.ones((D,), jnp.float32), 'W1': rn(ks[12], (D, 2 * F)), 'W2': rn(ks[13], (F, D))}
    _L0_attn_a_in = _L0_attn_a_setup()

    def _L0_attn_b_setup():
        import jax, jax.numpy as jnp
        import numpy as np
        B, N, D, H = (4, 256, 128, 16)
        DH = D // H
        EPS = 1e-05
        key = jax.random.key(seed)
        k1, k2, k3, k4 = jax.random.split(key, 4)
        return {'x': jax.random.normal(k1, (B, N, D), dtype=jnp.float32), 'g_ln': jnp.ones((D,), dtype=jnp.float32), 'Wq': jax.random.normal(k2, (D, D), dtype=jnp.float32) * 0.02, 'Wkv': jax.random.normal(k3, (D, 2 * D), dtype=jnp.float32) * 0.02, 'Wo': jax.random.normal(k4, (D, D), dtype=jnp.float32) * 0.02}
    _L0_attn_b_in = _L0_attn_b_setup()

    def _L0_ffn_setup():
        import jax, jax.numpy as jnp
        import numpy as np
        DIM = 128
        DEPTH = 2
        HEADS = 8
        DIM_HEAD = 64
        WINDOW = 64
        INNER = HEADS * DIM_HEAD
        HID = int(DIM * 4 * 2 / 3)
        B, N = (2, 1024)
        QK_SCALE = 8.0

        def shift_token(t):
            t1, t2 = jnp.split(t, 2, axis=-1)
            t2 = jnp.pad(t2, ((0, 0), (1, 0), (0, 0)))[:, :-1]
            return jnp.concatenate([t1, t2], axis=-1)

        def l2norm(t):
            return t / jnp.clip(jnp.linalg.norm(t, axis=-1, keepdims=True), 1e-12)

        def rotate_half(x):
            x1, x2 = jnp.split(x, 2, axis=-1)
            return jnp.concatenate([-x2, x1], axis=-1)

        def rotary_xpos(q, k):
            n = q.shape[-2]
            half_idx = jnp.arange(0, DIM_HEAD, 2, dtype=jnp.float32)
            inv_freq = 1.0 / 10000.0 ** (half_idx / DIM_HEAD)
            t = jnp.arange(n, dtype=jnp.float32)
            freqs = t[:, None] * inv_freq[None, :]
            freqs = jnp.concatenate([freqs, freqs], axis=-1)
            base = (half_idx + 0.4 * DIM_HEAD) / (1.4 * DIM_HEAD)
            power = (t - n // 2) / float(WINDOW // 2)
            scale = base[None, :] ** power[:, None]
            scale = jnp.concatenate([scale, scale], axis=-1)
            cos, sin = (jnp.cos(freqs), jnp.sin(freqs))
            q = q * cos * scale + rotate_half(q) * sin * scale
            k = k * cos / scale + rotate_half(k) * sin / scale
            return (q, k)

        def local_attention(q, k, v):
            b, h, n, d = q.shape
            w = n // WINDOW
            bq = q.reshape(b, h, w, WINDOW, d) * QK_SCALE
            bk = k.reshape(b, h, w, WINDOW, d)
            bv = v.reshape(b, h, w, WINDOW, d)

            def look_around(t):
                p = jnp.pad(t, ((0, 0), (0, 0), (1, 0), (0, 0), (0, 0)))
                return jnp.concatenate([p[:, :, :w], p[:, :, 1:]], axis=3)
            bk, bv = (look_around(bk), look_around(bv))
            bt = jnp.arange(n).reshape(w, WINDOW)
            btp = jnp.pad(bt, ((1, 0), (0, 0)), constant_values=-1)
            btk = jnp.concatenate([btp[:w], btp[1:]], axis=1)
            sim = jnp.einsum('bhwid,bhwjd->bhwij', bq, bk)
            i = bt[:, :, None]
            j = btk[:, None, :]
            mask = (i < j) | (i > j + WINDOW) | (j == -1)
            sim = jnp.where(mask, -jnp.finfo(sim.dtype).max, sim)
            attn = jax.nn.softmax(sim, axis=-1)
            out = jnp.einsum('bhwij,bhwjd->bhwid', attn, bv)
            return out.reshape(b, h, n, d)

        def _layer(x, wqkv, qs, ksc, wo, lg, lb, w1, b1, w2, b2):
            b, n, _ = x.shape
            h = shift_token(x)
            qkv = h @ wqkv
            q, k, v = jnp.split(qkv, 3, axis=-1)
            to_heads = lambda t: t.reshape(b, n, HEADS, DIM_HEAD).transpose(0, 2, 1, 3)
            q, k, v = (to_heads(q), to_heads(k), to_heads(v))
            q = l2norm(q) * qs
            k = l2norm(k) * ksc
            q, k = rotary_xpos(q, k)
            o = local_attention(q, k, v)
            o = o.transpose(0, 2, 1, 3).reshape(b, n, INNER)
            x = x + o @ wo
            h = shift_token(x)
            mu = h.mean(-1, keepdims=True)
            var = h.var(-1, keepdims=True)
            h = (h - mu) / jnp.sqrt(var + 1e-05) * lg + lb
            h = h @ w1 + b1
            a, g = jnp.split(h, 2, axis=-1)
            h = a * jax.nn.gelu(g, approximate=False)
            x = x + h @ w2 + b2
            return x
        key = jax.random.key(seed)
        ks = jax.random.split(key, 6)
        return {'x': jax.random.normal(ks[0], (B, N, DIM), jnp.float32), 'wqkv': jax.random.normal(ks[1], (DEPTH, DIM, 3 * INNER), jnp.float32) * 0.02, 'q_scale': jnp.ones((DEPTH, DIM_HEAD), jnp.float32), 'k_scale': jnp.ones((DEPTH, DIM_HEAD), jnp.float32), 'wo': jax.random.normal(ks[2], (DEPTH, INNER, DIM), jnp.float32) * 0.02, 'ln_g': jnp.ones((DEPTH, DIM), jnp.float32), 'ln_b': jnp.zeros((DEPTH, DIM), jnp.float32), 'w1': jax.random.normal(ks[3], (DEPTH, DIM, 2 * HID), jnp.float32) * 0.02, 'b1': jnp.zeros((DEPTH, 2 * HID), jnp.float32), 'w2': jax.random.normal(ks[4], (DEPTH, HID, DIM), jnp.float32) * 0.02, 'b2': jnp.zeros((DEPTH, DIM), jnp.float32)}
    _L0_ffn_in = _L0_ffn_setup()

    def _L1_attn_a_setup():
        import jax, jax.numpy as jnp
        import numpy as np
        B, N, D = (2, 256, 128)
        H = 16
        HD = D // H
        ROPE_BASE = 10000.0

        def _rotate_half(t):
            t = t.reshape(*t.shape[:-1], -1, 2)
            x1, x2 = (t[..., 0], t[..., 1])
            return jnp.stack((-x2, x1), axis=-1).reshape(*t.shape[:-2], -1)

        def _apply_rope(t, cos, sin):
            return t * cos + _rotate_half(t) * sin
        key = jax.random.key(seed)
        ks = jax.random.split(key, 5)
        s = 0.02
        return {'x': jax.random.normal(ks[0], (B, N, D), dtype=jnp.float32), 'qkv_w': jax.random.normal(ks[1], (3 * D, D), dtype=jnp.float32) * s, 'qkv_b': jax.random.normal(ks[2], (3 * D,), dtype=jnp.float32) * s, 'proj_w': jax.random.normal(ks[3], (D, D), dtype=jnp.float32) * s, 'proj_b': jax.random.normal(ks[4], (D,), dtype=jnp.float32) * s}
    _L1_attn_a_in = _L1_attn_a_setup()

    def _L1_attn_b_setup():
        import jax, jax.numpy as jnp
        import numpy as np
        DIM = 128
        H = 16
        DH = DIM // H
        NF = 64
        EPS = 1e-06
        key = jax.random.key(seed)
        ks = jax.random.split(key, 10)
        B, L = (4, 512)
        s = 1.0 / np.sqrt(DIM)
        x = jax.random.normal(ks[0], (B, L, DIM), dtype=jnp.float32)
        Wq = jax.random.normal(ks[1], (DIM, DIM), dtype=jnp.float32) * s
        Wk = jax.random.normal(ks[2], (DIM, DIM), dtype=jnp.float32) * s
        Wv = jax.random.normal(ks[3], (DIM, DIM), dtype=jnp.float32) * s
        Wo = jax.random.normal(ks[4], (DIM, DIM), dtype=jnp.float32) * s
        bq = jax.random.normal(ks[5], (DIM,), dtype=jnp.float32) * s
        bk = jax.random.normal(ks[6], (DIM,), dtype=jnp.float32) * s
        bv = jax.random.normal(ks[7], (DIM,), dtype=jnp.float32) * s
        bo = jax.random.normal(ks[8], (DIM,), dtype=jnp.float32) * s
        Wrf = jax.random.normal(ks[9], (1, H, DH, NF), dtype=jnp.float32)
        return {'x': x, 'Wq': Wq, 'bq': bq, 'Wk': Wk, 'bk': bk, 'Wv': Wv, 'bv': bv, 'Wo': Wo, 'bo': bo, 'Wrf': Wrf}
    _L1_attn_b_in = _L1_attn_b_setup()

    def _L1_ffn_setup():
        import jax, jax.numpy as jnp
        import numpy as np
        B, S, D, F, E = (2, 256, 128, 512, 8)
        LN_EPS = 1e-05

        def _layer_norm(x, gamma, beta):
            mu = jnp.mean(x, axis=-1, keepdims=True)
            var = jnp.mean(jnp.square(x - mu), axis=-1, keepdims=True)
            return (x - mu) * jax.lax.rsqrt(var + LN_EPS) * gamma + beta
        key = jax.random.key(seed)
        ks = jax.random.split(key, 8)

        def xavier(k, shape):
            fan_in, fan_out = (shape[-1], shape[-2])
            a = jnp.sqrt(6.0 / (fan_in + fan_out))
            return jax.random.uniform(k, shape, jnp.float32, -a, a)
        return {'tgt': jax.random.normal(ks[0], (B, S, D), jnp.float32), 'Wr': xavier(ks[1], (E, D)), 'br': jnp.zeros((E,), jnp.float32), 'W1': xavier(ks[2], (E, F, D)), 'b1': jnp.zeros((E, F), jnp.float32), 'W2': xavier(ks[3], (E, D, F)), 'b2': jnp.zeros((E, D), jnp.float32), 'gamma': jnp.ones((D,), jnp.float32), 'beta': jnp.zeros((D,), jnp.float32)}
    _L1_ffn_in = _L1_ffn_setup()
    _d = {'L0_attn_a_x': _L0_attn_a_in['x'], 'L0_attn_a_norm_attn_w': _L0_attn_a_in['norm_attn_w'], 'L0_attn_a_Wq': _L0_attn_a_in['Wq'], 'L0_attn_a_Wk': _L0_attn_a_in['Wk'], 'L0_attn_a_Wv': _L0_attn_a_in['Wv'], 'L0_attn_a_Wo': _L0_attn_a_in['Wo'], 'L0_attn_a_qn_w': _L0_attn_a_in['qn_w'], 'L0_attn_a_kn_w': _L0_attn_a_in['kn_w'], 'L0_attn_a_ssm_norm_w': _L0_attn_a_in['ssm_norm_w'], 'L0_attn_a_Wx': _L0_attn_a_in['Wx'], 'L0_attn_a_Wdt': _L0_attn_a_in['Wdt'], 'L0_attn_a_bdt': _L0_attn_a_in['bdt'], 'L0_attn_a_A_log': _L0_attn_a_in['A_log'], 'L0_attn_a_Dp': _L0_attn_a_in['Dp'], 'L0_attn_a_Wsel': _L0_attn_a_in['Wsel'], 'L0_attn_a_bsel': _L0_attn_a_in['bsel'], 'L0_attn_a_sel_gate': _L0_attn_a_in['sel_gate'], 'L0_attn_a_Wimp': _L0_attn_a_in['Wimp'], 'L0_attn_a_bimp': _L0_attn_a_in['bimp'], 'L0_attn_a_Wg': _L0_attn_a_in['Wg'], 'L0_attn_a_bg': _L0_attn_a_in['bg'], 'L0_attn_a_Wout': _L0_attn_a_in['Wout'], 'L0_attn_a_norm_ffn_w': _L0_attn_a_in['norm_ffn_w'], 'L0_attn_a_W1': _L0_attn_a_in['W1'], 'L0_attn_a_W2': _L0_attn_a_in['W2'], 'L0_attn_b_g_ln': _L0_attn_b_in['g_ln'], 'L0_attn_b_Wq': _L0_attn_b_in['Wq'], 'L0_attn_b_Wkv': _L0_attn_b_in['Wkv'], 'L0_attn_b_Wo': _L0_attn_b_in['Wo'], 'L0_ffn_wqkv': _L0_ffn_in['wqkv'], 'L0_ffn_q_scale': _L0_ffn_in['q_scale'], 'L0_ffn_k_scale': _L0_ffn_in['k_scale'], 'L0_ffn_wo': _L0_ffn_in['wo'], 'L0_ffn_ln_g': _L0_ffn_in['ln_g'], 'L0_ffn_ln_b': _L0_ffn_in['ln_b'], 'L0_ffn_w1': _L0_ffn_in['w1'], 'L0_ffn_b1': _L0_ffn_in['b1'], 'L0_ffn_w2': _L0_ffn_in['w2'], 'L0_ffn_b2': _L0_ffn_in['b2'], 'L1_attn_a_qkv_w': _L1_attn_a_in['qkv_w'], 'L1_attn_a_qkv_b': _L1_attn_a_in['qkv_b'], 'L1_attn_a_proj_w': _L1_attn_a_in['proj_w'], 'L1_attn_a_proj_b': _L1_attn_a_in['proj_b'], 'L1_attn_b_Wq': _L1_attn_b_in['Wq'], 'L1_attn_b_bq': _L1_attn_b_in['bq'], 'L1_attn_b_Wk': _L1_attn_b_in['Wk'], 'L1_attn_b_bk': _L1_attn_b_in['bk'], 'L1_attn_b_Wv': _L1_attn_b_in['Wv'], 'L1_attn_b_bv': _L1_attn_b_in['bv'], 'L1_attn_b_Wo': _L1_attn_b_in['Wo'], 'L1_attn_b_bo': _L1_attn_b_in['bo'], 'L1_attn_b_Wrf': _L1_attn_b_in['Wrf'], 'L1_ffn_Wr': _L1_ffn_in['Wr'], 'L1_ffn_br': _L1_ffn_in['br'], 'L1_ffn_W1': _L1_ffn_in['W1'], 'L1_ffn_b1': _L1_ffn_in['b1'], 'L1_ffn_W2': _L1_ffn_in['W2'], 'L1_ffn_b2': _L1_ffn_in['b2'], 'L1_ffn_gamma': _L1_ffn_in['gamma'], 'L1_ffn_beta': _L1_ffn_in['beta']}
    _x0 = _d['L0_attn_a_x']
    _d['L0_attn_a_x'] = jax.random.normal(jax.random.fold_in(jax.random.key(seed), 1), (16, 256, 128), dtype=_x0.dtype)
    del _x0
    return _d

def reference(L0_attn_a_x, L0_attn_a_norm_attn_w, L0_attn_a_Wq, L0_attn_a_Wk, L0_attn_a_Wv, L0_attn_a_Wo, L0_attn_a_qn_w, L0_attn_a_kn_w, L0_attn_a_ssm_norm_w, L0_attn_a_Wx, L0_attn_a_Wdt, L0_attn_a_bdt, L0_attn_a_A_log, L0_attn_a_Dp, L0_attn_a_Wsel, L0_attn_a_bsel, L0_attn_a_sel_gate, L0_attn_a_Wimp, L0_attn_a_bimp, L0_attn_a_Wg, L0_attn_a_bg, L0_attn_a_Wout, L0_attn_a_norm_ffn_w, L0_attn_a_W1, L0_attn_a_W2, L0_attn_b_g_ln, L0_attn_b_Wq, L0_attn_b_Wkv, L0_attn_b_Wo, L0_ffn_wqkv, L0_ffn_q_scale, L0_ffn_k_scale, L0_ffn_wo, L0_ffn_ln_g, L0_ffn_ln_b, L0_ffn_w1, L0_ffn_b1, L0_ffn_w2, L0_ffn_b2, L1_attn_a_qkv_w, L1_attn_a_qkv_b, L1_attn_a_proj_w, L1_attn_a_proj_b, L1_attn_b_Wq, L1_attn_b_bq, L1_attn_b_Wk, L1_attn_b_bk, L1_attn_b_Wv, L1_attn_b_bv, L1_attn_b_Wo, L1_attn_b_bo, L1_attn_b_Wrf, L1_ffn_Wr, L1_ffn_br, L1_ffn_W1, L1_ffn_b1, L1_ffn_W2, L1_ffn_b2, L1_ffn_gamma, L1_ffn_beta):

    def _L0_attn_a_ref(x, norm_attn_w, Wq, Wk, Wv, Wo, qn_w, kn_w, ssm_norm_w, Wx, Wdt, bdt, A_log, Dp, Wsel, bsel, sel_gate, Wimp, bimp, Wg, bg, Wout, norm_ffn_w, W1, W2):
        import jax, jax.numpy as jnp
        import numpy as np
        EPS = 1e-06
        N_HEADS, N_KV_HEADS = (16, 4)
        HYBRID_RATIO = 0.5
        ROPE_BASE = 10000.0

        def rms(x, w):
            return x * jax.lax.rsqrt(jnp.mean(x * x, axis=-1, keepdims=True) + EPS) * w

        def rotate_half(x):
            x1, x2 = jnp.split(x, 2, axis=-1)
            return jnp.concatenate((-x2, x1), axis=-1)
        B, L, D = x.shape
        H, KVH = (N_HEADS, N_KV_HEADS)
        hd = D // H
        R = Wdt.shape[0]
        N = A_log.shape[1]
        xa = rms(x, norm_attn_w)
        q = (xa @ Wq).reshape(B, L, H, hd).transpose(0, 2, 1, 3)
        k = (xa @ Wk).reshape(B, L, KVH, hd).transpose(0, 2, 1, 3)
        v = (xa @ Wv).reshape(B, L, KVH, hd).transpose(0, 2, 1, 3)
        q = rms(q, qn_w)
        k = rms(k, kn_w)
        inv_freq = 1.0 / ROPE_BASE ** (jnp.arange(0, hd, 2, dtype=jnp.float32) / hd)
        freqs = jnp.arange(L, dtype=jnp.float32)[:, None] * inv_freq[None, :]
        emb = jnp.concatenate((freqs, freqs), axis=-1)
        cos, sin = (jnp.cos(emb), jnp.sin(emb))
        q = q * cos + rotate_half(q) * sin
        k = k * cos + rotate_half(k) * sin
        n_rep = H // KVH
        k = jnp.repeat(k, n_rep, axis=1)
        v = jnp.repeat(v, n_rep, axis=1)
        scores = jnp.einsum('bhqd,bhkd->bhqk', q, k) / jnp.sqrt(jnp.float32(hd))
        attn = jax.nn.softmax(scores, axis=-1)
        attn = jnp.einsum('bhqk,bhkd->bhqd', attn, v)
        attn_out = attn.transpose(0, 2, 1, 3).reshape(B, L, D) @ Wo
        xn = rms(x, ssm_norm_w)
        xp = xn @ Wx
        dr, Bs, Cs = (xp[..., :R], xp[..., R:R + N], xp[..., R + N:])
        sel = jax.nn.sigmoid((xn @ Wsel + bsel) * sel_gate)
        xn = xn * sel
        imp = jax.nn.sigmoid(xn @ Wimp + bimp)
        delta = jax.nn.softplus(dr @ Wdt + bdt)
        A = -jnp.exp(A_log)
        gate = jax.nn.sigmoid(xn @ Wg + bg)
        xn = xn * gate
        Bs = Bs * imp
        Cs = Cs * imp

        def step(h, inputs):
            dt, bt, ct, xt = inputs
            dA = jnp.exp(dt[:, :, None] * A)
            h = dA * h + dt[:, :, None] * bt[:, None, :] * xt[:, :, None]
            y = jnp.sum(h * ct[:, None, :], axis=-1)
            return (h, y)
        h0 = jnp.zeros((B, D, N), x.dtype)
        seq = (delta.transpose(1, 0, 2), Bs.transpose(1, 0, 2), Cs.transpose(1, 0, 2), xn.transpose(1, 0, 2))
        _, ys = jax.lax.scan(step, h0, seq)
        y = ys.transpose(1, 0, 2)
        ssm_out = (y + x * Dp) @ Wout
        x1 = x + HYBRID_RATIO * attn_out + (1.0 - HYBRID_RATIO) * ssm_out
        xf = rms(x1, norm_ffn_w)
        u = xf @ W1
        a, g = jnp.split(u, 2, axis=-1)
        ff = jax.nn.silu(a) * g @ W2
        return x1 + ff

    def _L0_attn_b_ref(x, g_ln, Wq, Wkv, Wo):
        import jax, jax.numpy as jnp
        import numpy as np
        B, N, D, H = (4, 256, 128, 16)
        DH = D // H
        EPS = 1e-05
        mu = jnp.mean(x, axis=-1, keepdims=True)
        var = jnp.mean(jnp.square(x - mu), axis=-1, keepdims=True)
        xn = (x - mu) * jax.lax.rsqrt(var + EPS) * g_ln
        b, n, d = xn.shape
        q = (xn @ Wq).reshape(b, n, H, DH).transpose(0, 2, 1, 3)
        kv = xn @ Wkv
        k, v = jnp.split(kv, 2, axis=-1)
        k = k.reshape(b, n, H, DH).transpose(0, 2, 1, 3)
        v = v.reshape(b, n, H, DH).transpose(0, 2, 1, 3)
        scale = DH ** (-0.5)
        dots = jnp.einsum('bhid,bhjd->bhij', q, k) * scale
        mask_value = -jnp.finfo(dots.dtype).max
        causal = jnp.triu(jnp.ones((n, n), dtype=bool), k=1)
        dots = jnp.where(causal, mask_value, dots)
        attn = jax.nn.softmax(dots.astype(jnp.float32), axis=-1).astype(dots.dtype)
        out = jnp.einsum('bhij,bhjd->bhid', attn, v)
        out = out.transpose(0, 2, 1, 3).reshape(b, n, d)
        return out @ Wo

    def _L0_ffn_ref(x, wqkv, q_scale, k_scale, wo, ln_g, ln_b, w1, b1, w2, b2):
        import jax, jax.numpy as jnp
        import numpy as np
        DIM = 128
        DEPTH = 2
        HEADS = 8
        DIM_HEAD = 64
        WINDOW = 64
        INNER = HEADS * DIM_HEAD
        HID = int(DIM * 4 * 2 / 3)
        B, N = (2, 1024)
        QK_SCALE = 8.0

        def shift_token(t):
            t1, t2 = jnp.split(t, 2, axis=-1)
            t2 = jnp.pad(t2, ((0, 0), (1, 0), (0, 0)))[:, :-1]
            return jnp.concatenate([t1, t2], axis=-1)

        def l2norm(t):
            return t / jnp.clip(jnp.linalg.norm(t, axis=-1, keepdims=True), 1e-12)

        def rotate_half(x):
            x1, x2 = jnp.split(x, 2, axis=-1)
            return jnp.concatenate([-x2, x1], axis=-1)

        def rotary_xpos(q, k):
            n = q.shape[-2]
            half_idx = jnp.arange(0, DIM_HEAD, 2, dtype=jnp.float32)
            inv_freq = 1.0 / 10000.0 ** (half_idx / DIM_HEAD)
            t = jnp.arange(n, dtype=jnp.float32)
            freqs = t[:, None] * inv_freq[None, :]
            freqs = jnp.concatenate([freqs, freqs], axis=-1)
            base = (half_idx + 0.4 * DIM_HEAD) / (1.4 * DIM_HEAD)
            power = (t - n // 2) / float(WINDOW // 2)
            scale = base[None, :] ** power[:, None]
            scale = jnp.concatenate([scale, scale], axis=-1)
            cos, sin = (jnp.cos(freqs), jnp.sin(freqs))
            q = q * cos * scale + rotate_half(q) * sin * scale
            k = k * cos / scale + rotate_half(k) * sin / scale
            return (q, k)

        def local_attention(q, k, v):
            b, h, n, d = q.shape
            w = n // WINDOW
            bq = q.reshape(b, h, w, WINDOW, d) * QK_SCALE
            bk = k.reshape(b, h, w, WINDOW, d)
            bv = v.reshape(b, h, w, WINDOW, d)

            def look_around(t):
                p = jnp.pad(t, ((0, 0), (0, 0), (1, 0), (0, 0), (0, 0)))
                return jnp.concatenate([p[:, :, :w], p[:, :, 1:]], axis=3)
            bk, bv = (look_around(bk), look_around(bv))
            bt = jnp.arange(n).reshape(w, WINDOW)
            btp = jnp.pad(bt, ((1, 0), (0, 0)), constant_values=-1)
            btk = jnp.concatenate([btp[:w], btp[1:]], axis=1)
            sim = jnp.einsum('bhwid,bhwjd->bhwij', bq, bk)
            i = bt[:, :, None]
            j = btk[:, None, :]
            mask = (i < j) | (i > j + WINDOW) | (j == -1)
            sim = jnp.where(mask, -jnp.finfo(sim.dtype).max, sim)
            attn = jax.nn.softmax(sim, axis=-1)
            out = jnp.einsum('bhwij,bhwjd->bhwid', attn, bv)
            return out.reshape(b, h, n, d)

        def _layer(x, wqkv, qs, ksc, wo, lg, lb, w1, b1, w2, b2):
            b, n, _ = x.shape
            h = shift_token(x)
            qkv = h @ wqkv
            q, k, v = jnp.split(qkv, 3, axis=-1)
            to_heads = lambda t: t.reshape(b, n, HEADS, DIM_HEAD).transpose(0, 2, 1, 3)
            q, k, v = (to_heads(q), to_heads(k), to_heads(v))
            q = l2norm(q) * qs
            k = l2norm(k) * ksc
            q, k = rotary_xpos(q, k)
            o = local_attention(q, k, v)
            o = o.transpose(0, 2, 1, 3).reshape(b, n, INNER)
            x = x + o @ wo
            h = shift_token(x)
            mu = h.mean(-1, keepdims=True)
            var = h.var(-1, keepdims=True)
            h = (h - mu) / jnp.sqrt(var + 1e-05) * lg + lb
            h = h @ w1 + b1
            a, g = jnp.split(h, 2, axis=-1)
            h = a * jax.nn.gelu(g, approximate=False)
            x = x + h @ w2 + b2
            return x
        for l in range(DEPTH):
            x = _layer(x, wqkv[l], q_scale[l], k_scale[l], wo[l], ln_g[l], ln_b[l], w1[l], b1[l], w2[l], b2[l])
        return x

    def _L1_attn_a_ref(x, qkv_w, qkv_b, proj_w, proj_b):
        import jax, jax.numpy as jnp
        import numpy as np
        B, N, D = (2, 256, 128)
        H = 16
        HD = D // H
        ROPE_BASE = 10000.0

        def _rotate_half(t):
            t = t.reshape(*t.shape[:-1], -1, 2)
            x1, x2 = (t[..., 0], t[..., 1])
            return jnp.stack((-x2, x1), axis=-1).reshape(*t.shape[:-2], -1)

        def _apply_rope(t, cos, sin):
            return t * cos + _rotate_half(t) * sin
        b, n, d = x.shape
        scale = HD ** (-0.5)
        qkv = x @ qkv_w.T + qkv_b
        qkv = qkv.reshape(b, n, 3, H, HD)
        qkv = jnp.transpose(qkv, (2, 0, 3, 1, 4))
        q, k, v = (qkv[0], qkv[1], qkv[2])
        inv_freq = 1.0 / ROPE_BASE ** (jnp.arange(0, HD, 2, dtype=jnp.float32) / HD)
        freqs = jnp.arange(n, dtype=jnp.float32)[:, None] * inv_freq[None, :]
        freqs = jnp.repeat(freqs, 2, axis=-1)
        cos, sin = (jnp.cos(freqs), jnp.sin(freqs))
        q = _apply_rope(q, cos, sin)
        k = _apply_rope(k, cos, sin)
        scores = jnp.einsum('bhid,bhjd->bhij', q, k) * scale
        causal = jnp.triu(jnp.ones((n, n), dtype=bool), k=1)
        scores = jnp.where(causal, -jnp.inf, scores)
        attn = jax.nn.softmax(scores, axis=-1)
        out = jnp.einsum('bhij,bhjd->bhid', attn, v)
        out = jnp.transpose(out, (0, 2, 1, 3)).reshape(b, n, d)
        return out @ proj_w.T + proj_b

    def _L1_attn_b_ref(x, Wq, bq, Wk, bk, Wv, bv, Wo, bo, Wrf):
        import jax, jax.numpy as jnp
        import numpy as np
        DIM = 128
        H = 16
        DH = DIM // H
        NF = 64
        EPS = 1e-06
        B, L, _ = x.shape
        W0 = Wrf[0]

        def split_heads(y):
            return y.reshape(B, L, H, DH).transpose(0, 2, 1, 3)
        q = split_heads(x @ Wq.T + bq)
        k = split_heads(x @ Wk.T + bk)
        v = split_heads(x @ Wv.T + bv)
        logits = jnp.einsum('bhld,hdf->bhlf', k, W0) - 0.5 * jnp.sum(k * k, axis=-1, keepdims=True)
        alpha = jax.nn.softmax(logits.reshape(B, H, L * NF), axis=2)
        alpha = alpha.reshape(B, H, L, NF)
        N = jnp.einsum('bhlf,bhld->bhfd', alpha, v)
        D = jnp.sum(alpha, axis=2)
        phi = jax.nn.softmax(jnp.einsum('bhld,hdf->bhlf', q, W0), axis=-1)
        num = jnp.einsum('bhlf,bhfd->bhld', phi, N)
        den = jnp.einsum('bhlf,bhf->bhl', phi, D)
        out = num / (den[..., None] + EPS)
        ctx = out.transpose(0, 2, 1, 3).reshape(B, L, DIM)
        return ctx @ Wo.T + bo

    def _L1_ffn_ref(tgt, Wr, br, W1, b1, W2, b2, gamma, beta):
        import jax, jax.numpy as jnp
        import numpy as np
        B, S, D, F, E = (2, 256, 128, 512, 8)
        LN_EPS = 1e-05

        def _layer_norm(x, gamma, beta):
            mu = jnp.mean(x, axis=-1, keepdims=True)
            var = jnp.mean(jnp.square(x - mu), axis=-1, keepdims=True)
            return (x - mu) * jax.lax.rsqrt(var + LN_EPS) * gamma + beta
        logits = jnp.einsum('bsd,ed->bse', tgt, Wr) + br
        top_v, top_i = jax.lax.top_k(logits, 2)
        top_w = jax.nn.softmax(top_v, axis=-1)
        n_exp = logits.shape[-1]
        router_w = jnp.sum(jax.nn.one_hot(top_i, n_exp, dtype=top_w.dtype) * top_w[..., None], axis=-2)
        h = jnp.einsum('bsd,efd->bsef', tgt, W1) + b1
        h = jax.nn.relu(h)
        o = jnp.einsum('bsef,edf->bsed', h, W2) + b2
        tgt2 = jnp.einsum('bsed,bse->bsd', o, router_w)
        return _layer_norm(tgt + tgt2, gamma, beta)
    x = L0_attn_a_x
    x = x + _L0_attn_a_ref(_layernorm(x, axis=-1), L0_attn_a_norm_attn_w, L0_attn_a_Wq, L0_attn_a_Wk, L0_attn_a_Wv, L0_attn_a_Wo, L0_attn_a_qn_w, L0_attn_a_kn_w, L0_attn_a_ssm_norm_w, L0_attn_a_Wx, L0_attn_a_Wdt, L0_attn_a_bdt, L0_attn_a_A_log, L0_attn_a_Dp, L0_attn_a_Wsel, L0_attn_a_bsel, L0_attn_a_sel_gate, L0_attn_a_Wimp, L0_attn_a_bimp, L0_attn_a_Wg, L0_attn_a_bg, L0_attn_a_Wout, L0_attn_a_norm_ffn_w, L0_attn_a_W1, L0_attn_a_W2)
    x = x + _L0_ffn_ref(_layernorm(x, axis=-1), L0_ffn_wqkv, L0_ffn_q_scale, L0_ffn_k_scale, L0_ffn_wo, L0_ffn_ln_g, L0_ffn_ln_b, L0_ffn_w1, L0_ffn_b1, L0_ffn_w2, L0_ffn_b2)
    x = x + _L0_attn_b_ref(_layernorm(x, axis=-1), L0_attn_b_g_ln, L0_attn_b_Wq, L0_attn_b_Wkv, L0_attn_b_Wo)
    x = x + _L0_ffn_ref(_layernorm(x, axis=-1), L0_ffn_wqkv, L0_ffn_q_scale, L0_ffn_k_scale, L0_ffn_wo, L0_ffn_ln_g, L0_ffn_ln_b, L0_ffn_w1, L0_ffn_b1, L0_ffn_w2, L0_ffn_b2)
    x = x + _L1_attn_a_ref(_layernorm(x, axis=-1), L1_attn_a_qkv_w, L1_attn_a_qkv_b, L1_attn_a_proj_w, L1_attn_a_proj_b)
    x = x + _L1_ffn_ref(_layernorm(x, axis=-1), L1_ffn_Wr, L1_ffn_br, L1_ffn_W1, L1_ffn_b1, L1_ffn_W2, L1_ffn_b2, L1_ffn_gamma, L1_ffn_beta)
    x = x + _L1_attn_b_ref(_layernorm(x, axis=-1), L1_attn_b_Wq, L1_attn_b_bq, L1_attn_b_Wk, L1_attn_b_bk, L1_attn_b_Wv, L1_attn_b_bv, L1_attn_b_Wo, L1_attn_b_bo, L1_attn_b_Wrf)
    x = x + _L1_ffn_ref(_layernorm(x, axis=-1), L1_ffn_Wr, L1_ffn_br, L1_ffn_W1, L1_ffn_b1, L1_ffn_W2, L1_ffn_b2, L1_ffn_gamma, L1_ffn_beta)
    return x

_drawn_inputs = setup_inputs


def setup_inputs(seed=0):
    import zlib

    import numpy as np

    out = dict(_drawn_inputs(seed))
    spreads = {'L0_attn_a_norm_attn_w': (1.0, 0.6),
     'L0_attn_a_qn_w': (1.0, 0.6),
     'L0_attn_a_kn_w': (1.0, 0.6),
     'L0_attn_a_ssm_norm_w': (1.0, 0.6),
     'L0_attn_a_bdt': (0.0, 0.8),
     'L0_attn_a_Dp': (1.0, 0.6),
     'L0_attn_a_bsel': (0.0, 0.8),
     'L0_attn_a_sel_gate': (1.0, 0.6),
     'L0_attn_a_bimp': (0.0, 0.8),
     'L0_attn_a_bg': (0.0, 0.8),
     'L0_attn_a_norm_ffn_w': (1.0, 0.6),
     'L0_attn_b_g_ln': (1.0, 0.6),
     'L0_ffn_q_scale': (1.0, 0.6),
     'L0_ffn_k_scale': (1.0, 0.6),
     'L0_ffn_ln_g': (1.0, 0.6),
     'L0_ffn_ln_b': (0.0, 0.8),
     'L0_ffn_b1': (0.0, 0.8),
     'L0_ffn_b2': (0.0, 0.29),
     'L1_ffn_br': (0.0, 1.3),
     'L1_ffn_b1': (0.0, 1.125),
     'L1_ffn_b2': (0.0, 1.0),
     'L1_ffn_gamma': (1.0, 0.6),
     'L1_ffn_beta': (0.0, 0.683)}
    factors = {'L0_attn_a_Wq': 8.0,
     'L0_attn_a_Wk': 8.0,
     'L0_attn_a_Wv': 8.0,
     'L0_attn_a_Wo': 8.0,
     'L0_attn_a_Wx': 8.0,
     'L0_attn_a_Wdt': 8.0,
     'L0_attn_a_A_log': 8.0,
     'L0_attn_a_Wsel': 8.0,
     'L0_attn_a_Wimp': 8.0,
     'L0_attn_a_Wg': 8.0,
     'L0_attn_a_W1': 6.626,
     'L0_attn_a_W2': 6.649,
     'L0_attn_b_Wq': 8.0,
     'L0_attn_b_Wkv': 8.0,
     'L0_attn_b_Wo': 8.0,
     'L0_ffn_w1': 4.435,
     'L0_ffn_w2': 4.508,
     'L1_attn_a_qkv_w': 8.0,
     'L1_attn_a_qkv_b': 8.0,
     'L1_attn_a_proj_w': 8.0,
     'L1_attn_a_proj_b': 42.095,
     'L1_attn_b_bq': 31.216,
     'L1_attn_b_bk': 31.052,
     'L1_attn_b_bv': 10.635,
     'L1_attn_b_bo': 10.071,
     'L1_attn_b_Wq': 3.89,
     'L1_attn_b_Wk': 2.927,
     'L1_attn_b_Wrf': 3.65}
    for name, (base, spread) in spreads.items():
        noise = np.random.default_rng([zlib.crc32(name.encode()), seed]).standard_normal(out[name].shape)
        drawn = base * np.exp(spread * noise) if base else spread * noise
        out[name] = jnp.asarray(drawn.astype(out[name].dtype))
    for name, factor in factors.items():
        out[name] = (out[name] * factor).astype(out[name].dtype)
    return out
```

```python
from contextlib import ExitStack

import numpy as np

import concourse.bass as bass
from concourse import mybir

F32 = mybir.dt.float32
BF16 = mybir.dt.bfloat16
U32 = mybir.dt.uint32
ACT = mybir.ActivationFunctionType
ALU = mybir.AluOpType
AX_X = mybir.AxisListType.X

BATCH, SEQ, DIM = 16, 256, 128
TOKENS = BATCH * SEQ
TILE = 512
TILES = TOKENS // TILE
HEADS, HEAD_DIM = 16, 8
VCOLS = HEAD_DIM + 1
NEG = -1.0e30

EXP_LN = "natural_log_exp_and_others"
GELU_SET = "gelu_and_others"
SILU_SET = "silu_and_others"
SIGMOID_SET = "sigmoid_and_others"


class Steps:

    def __init__(self, k, role, steps, trips):
        self.sem, self.base = k.shared(role, len(steps) * (trips + 1))
        self.place = {s: n for n, s in enumerate(steps)}
        self.count = len(steps)
        assert len(self.place) == self.count

    def at(self, trip, step):
        return trip * self.count + (self.base + self.count + self.place[step] + 1)

    def before(self, trip, step):
        return trip * self.count + (self.base + self.place[step] + 1)

    def prime(self, eng):
        eng.sem_inc(self.sem, self.count)


class Count:

    def __init__(self, k, role, total):
        self.sem, self.base = k.shared(role, total)

    def at(self, n):
        return self.base + n


class Region:

    def __init__(self, tensor, columns):
        self.tensor, self.columns, self.used = tensor, columns, 0

    def reset(self):
        self.used = 0

    def take(self, columns):
        at = self.used
        self.used += columns
        assert self.used <= self.columns, (self.used, self.columns)
        return self.tensor[:, at:at + columns]

    def take_bf16(self, columns):
        return self.take((columns + 1) // 2).bitcast(BF16)


class Core:

    def __init__(self, nc, ctx):
        self.nc, self.ctx = nc, ctx
        self.roles = {}

    def sb(self, name, shape, dt=F32):
        return self.ctx.enter_context(self.nc.sbuf_tensor(name, shape, dt))

    def sem(self, name):
        return self.ctx.enter_context(self.nc.semaphore(name))

    def shared(self, role, total):
        if role not in self.roles:
            self.roles[role] = [self.sem(role), 0]
        sem, base = self.roles[role]
        self.roles[role][1] = base + total
        return sem, base


def tok(i, width, extra=0):
    return bass.ds(i * width + extra, width)


def copy_dram_stage(k, name, pairs):
    landed = [Count(k, f"landed{n}", 16) for n in range(len(pairs))]
    with k.nc.Block() as block:
        @block.sync
        def _(sp):
            for n, (dst, src) in enumerate(pairs):
                sp.dma_start(dst, src).then_inc(landed[n].sem, 16)
            for n in range(len(pairs)):
                sp.wait_ge(landed[n].sem, landed[n].at(16))


def norm_stage(k, name, src, outs, center, eps):
    nc = k.nc
    U = 4
    us, trips = range(U), TILES // U
    pe_s = Steps(k, "sums", [f"{s}{u}" for s in (["center", "var"] if center else ["var"]) for u in us], trips)
    act_s = Steps(k, "roots", [f"sq{u}" for u in us] + [f"{s}{u}" for u in us for s in ("ln", "exp")], trips)
    biased = any(b is not None for _, _, b in outs)
    dve_s = Steps(k, "scaled", [f"{s}{u}" for u in us for s in (("z", "b") if biased else ("z",))], trips)
    k.arena.reset()
    sq = [k.arena.take(TILE) for _ in us]
    rs = [k.arena.take(TILE) for _ in us]
    pre = [k.arena.take(TILE) for _ in us]
    cbank = [k.psum[:, u, :] for u in us]
    vbank = [k.psum[:, U + u, :] for u in us]
    with nc.Block() as block:
        @block.tensor
        def _(pe):
            pe_s.prime(pe)
            with pe.Fori(0, trips) as i:
                if center:
                    for u in us:
                        pe.wait_ge(dve_s.sem, dve_s.before(i, f"z{u}"))
                        pe.matmul(cbank[u], k.c["center"], src[:, bass.ds(i * (U * TILE) + u * TILE, TILE)],
                                  start=True, stop=True).then_inc(pe_s.sem, 1)
                for u in us:
                    pe.wait_ge(act_s.sem, act_s.at(i, f"sq{u}"))
                    pe.wait_ge(act_s.sem, act_s.before(i, f"ln{u}"))
                    pe.matmul(vbank[u], k.c["mean"], sq[u], start=True, stop=True).then_inc(pe_s.sem, 1)

        @block.scalar
        def _(act):
            act_s.prime(act)
            act.preload_act_table_set(EXP_LN)
            with act.Fori(0, trips) as i:
                for u in us:
                    if center:
                        act.wait_ge(pe_s.sem, pe_s.at(i, f"center{u}"))
                    act.wait_ge(pe_s.sem, pe_s.before(i, f"var{u}"))
                    inp = cbank[u] if center else src[:, bass.ds(i * (U * TILE) + u * TILE, TILE)]
                    act.activation(sq[u], inp, ACT.Square).then_inc(act_s.sem, 1)
                for u in us:
                    act.wait_ge(pe_s.sem, pe_s.at(i, f"var{u}"))
                    act.wait_ge(dve_s.sem, dve_s.before(i, f"z{u}"))
                    act.activation(rs[u], vbank[u], ACT.Ln, bias=k.c[eps]).then_inc(act_s.sem, 1)
                    act.wait_ge(act_s.sem, act_s.at(i, f"ln{u}"))
                    act.activation(rs[u], rs[u], ACT.Exp, scale=-0.5).then_inc(act_s.sem, 1)

        @block.vector
        def _(dve):
            dve_s.prime(dve)
            with dve.Fori(0, trips) as i:
                for u in us:
                    dve.wait_ge(act_s.sem, act_s.at(i, f"exp{u}"))
                    cols = bass.ds(i * (U * TILE) + u * TILE, TILE)
                    for dst, w, b in outs:
                        to = pre[u] if b is not None else dst[:, cols]
                        c = cbank[u] if center else src[:, cols]
                        if w is None:
                            last = dve.tensor_tensor(to, c, rs[u], ALU.mult)
                        else:
                            last = dve.scalar_tensor_tensor(out=to, in0=c, scalar=w, in1=rs[u],
                                                            op0=ALU.mult, op1=ALU.mult)
                    last.then_inc(dve_s.sem, 1)
                    if biased:
                        dve.wait_ge(dve_s.sem, dve_s.at(i, f"z{u}"))
                        dve.tensor_scalar(outs[0][0][:, cols], pre[u], outs[0][2], None, ALU.add)\
                            .then_inc(dve_s.sem, 1)


def project_stage(k, name, src, wq, wk, wv, q, kk, v, bq=None, bk=None, qn=None, kn=None, rope=None, eps=None,
                  bv_row=None):
    nc = k.nc
    normed, rotary = qn is not None, rope is not None
    sides = ["q", "k"]
    pe_steps = ["q", "k", "v"]
    act_steps = ["copy"]
    dve_steps = ["vcopy"]
    pool_steps = []
    for s in sides:
        if normed:
            act_steps += [f"sq_{s}"]
        else:
            act_steps += [f"id_{s}"]
    for s in sides:
        if normed:
            pe_steps += [f"mean_{s}"]
            act_steps += [f"ln_{s}", f"exp_{s}"]
            dve_steps += [f"nrm_{s}"]
    for s in sides:
        if rotary:
            pe_steps += [f"rot_{s}"]
            dve_steps += [f"sin_{s}", f"add_{s}"]
            pool_steps += [f"cos_{s}"]
    pe_s = Steps(k, "products", pe_steps, TILES)
    act_s = Steps(k, "lookups", act_steps, TILES)
    dve_s = Steps(k, "vectors", dve_steps, TILES)
    pool_s = Steps(k, "cosines", pool_steps, TILES) if rotary else None
    k.arena.used = k.arena_kept
    zt = k.arena.take(TILE)
    sq = {s: k.arena.take(TILE) for s in sides}
    rs = {s: k.arena.take(TILE) for s in sides}
    flat = {s: k.arena.take(TILE) for s in sides}
    cosd = {s: k.arena.take(TILE) for s in sides}
    bank = {"q": k.psum[:, 0, :], "k": k.psum[:, 1, :], "v": k.psum[:, 2, :], "mean_q": k.psum[:, 3, :],
            "mean_k": k.psum[:, 4, :], "rot_q": k.psum[:, 5, :], "rot_k": k.psum[:, 6, :]}
    weight = {"q": wq, "k": wk}
    bias = {"q": bq, "k": bk}
    norm_w = {"q": qn, "k": kn}
    dst = {"q": q, "k": kk}

    def two(ap):
        return ap.rearrange("p (b t) -> p b t", b=2)

    def both(table):
        return table.unsqueeze(1).to_broadcast([128, 2, SEQ])

    def bank_read(s):
        return (dve_s, f"nrm_{s}") if normed else (act_s, f"id_{s}")

    with nc.Block() as block:
        @block.tensor
        def _(pe):
            pe_s.prime(pe)
            with pe.Fori(0, TILES) as i:
                for s in sides:
                    r, step = bank_read(s)
                    pe.wait_ge(r.sem, r.before(i, step))
                    pe.matmul(bank[s], weight[s], src[:, tok(i, TILE)], start=True, stop=True).then_inc(pe_s.sem, 1)
                pe.wait_ge(act_s.sem, act_s.at(i, "copy"))
                pe.wait_ge(dve_s.sem, dve_s.before(i, "vcopy"))
                for j in range(4):
                    last = pe.matmul(bank["v"][:, j * 128:(j + 1) * 128], zt[:, j * 128:(j + 1) * 128], wv,
                                     start=True, stop=bv_row is None)
                    if bv_row is not None:
                        last = pe.matmul(bank["v"][:, j * 128:(j + 1) * 128], k.c["ones"][0:1, :], bv_row,
                                         start=False, stop=True)
                last.then_inc(pe_s.sem, 1)
                if normed:
                    for s in sides:
                        pe.wait_ge(act_s.sem, act_s.at(i, f"sq_{s}"))
                        pe.wait_ge(act_s.sem, act_s.before(i, f"ln_{s}"))
                        pe.matmul(bank[f"mean_{s}"], k.c["head_mean"], sq[s], start=True, stop=True)\
                            .then_inc(pe_s.sem, 1)
                if rotary:
                    for s in sides:
                        r, step = (dve_s, f"nrm_{s}") if normed else (act_s, f"id_{s}")
                        pe.wait_ge(r.sem, r.at(i, step))
                        pe.wait_ge(dve_s.sem, dve_s.before(i, f"sin_{s}"))
                        pe.matmul(bank[f"rot_{s}"], rope[0], flat[s], start=True, stop=True).then_inc(pe_s.sem, 1)

        @block.scalar
        def _(act):
            act_s.prime(act)
            act.preload_act_table_set(EXP_LN)
            with act.Fori(0, TILES) as i:
                act.wait_ge(pe_s.sem, pe_s.before(i, "v"))
                act.copy(zt, src[:, tok(i, TILE)]).then_inc(act_s.sem, 1)
                for s in sides:
                    act.wait_ge(pe_s.sem, pe_s.at(i, s))
                    if normed:
                        act.wait_ge(pe_s.sem, pe_s.before(i, f"mean_{s}"))
                        act.activation(sq[s], bank[s], ACT.Square).then_inc(act_s.sem, 1)
                        continue
                    if rotary:
                        act.wait_ge(pe_s.sem, pe_s.before(i, f"rot_{s}"))
                        act.wait_ge(pool_s.sem, pool_s.before(i, f"cos_{s}"))
                    to = flat[s] if rotary else dst[s][:, bass.ds(i * TILE + SEQ, TILE)]
                    act.activation(to, bank[s], ACT.Identity, bias=bias[s] if bias[s] is not None else 0.0)\
                        .then_inc(act_s.sem, 1)
                if normed:
                    for s in sides:
                        act.wait_ge(pe_s.sem, pe_s.at(i, f"mean_{s}"))
                        act.wait_ge(dve_s.sem, dve_s.before(i, f"{'add' if rotary else 'nrm'}_{s}"))
                        act.activation(rs[s], bank[f"mean_{s}"], ACT.Ln, bias=k.c[eps]).then_inc(act_s.sem, 1)
                        act.wait_ge(act_s.sem, act_s.at(i, f"ln_{s}"))
                        act.activation(rs[s], rs[s], ACT.Exp, scale=-0.5).then_inc(act_s.sem, 1)

        @block.vector
        def _(dve):
            dve_s.prime(dve)
            with dve.Fori(0, TILES) as i:
                dve.wait_ge(pe_s.sem, pe_s.at(i, "v"))
                vt = v[:, bass.ds(i * 4 + 2, 4), :].rearrange("p t (h c) -> p t h c", c=VCOLS)[:, :, :, 0:HEAD_DIM]
                bv4 = bank["v"].rearrange("p (t h c) -> p t h c", t=4, c=HEAD_DIM)
                dve.tensor_copy(vt, bv4).then_inc(dve_s.sem, 1)
                if normed:
                    for s in sides:
                        dve.wait_ge(act_s.sem, act_s.at(i, f"exp_{s}"))
                        if rotary:
                            dve.wait_ge(pe_s.sem, pe_s.before(i, f"rot_{s}"))
                            dve.wait_ge(pool_s.sem, pool_s.before(i, f"cos_{s}"))
                        dve.scalar_tensor_tensor(out=flat[s], in0=bank[s], scalar=norm_w[s], in1=rs[s],
                                                 op0=ALU.mult, op1=ALU.mult).then_inc(dve_s.sem, 1)
                if rotary:
                    for s in sides:
                        dve.wait_ge(pe_s.sem, pe_s.at(i, f"rot_{s}"))
                        dve.wait_ge(dve_s.sem, dve_s.before(i, f"add_{s}"))
                        if normed:
                            dve.wait_ge(pe_s.sem, pe_s.at(i, f"mean_{s}"))
                        dve.tensor_tensor(two(rs[s]) if not normed else two(rs[s]), two(bank[f"rot_{s}"]),
                                          both(rope[2]), ALU.mult).then_inc(dve_s.sem, 1)
                        dve.wait_ge(dve_s.sem, dve_s.at(i, f"sin_{s}"))
                        dve.wait_ge(pool_s.sem, pool_s.at(i, f"cos_{s}"))
                        dve.tensor_tensor(dst[s][:, bass.ds(i * TILE + SEQ, TILE)], cosd[s], rs[s], ALU.add)\
                            .then_inc(dve_s.sem, 1)

        if rotary:
            @block.gpsimd
            def _(pool):
                pool_s.prime(pool)
                with pool.Fori(0, TILES) as i:
                    for s in sides:
                        r, step = (dve_s, f"nrm_{s}") if normed else (act_s, f"id_{s}")
                        pool.wait_ge(r.sem, r.at(i, step))
                        pool.wait_ge(dve_s.sem, dve_s.before(i, f"add_{s}"))
                        pool.tensor_tensor(two(cosd[s]), two(flat[s]), both(rope[1]), ALU.mult)\
                            .then_inc(pool_s.sem, 1)


def attention_stage(k, name, q, kk, v, out, causal, scale, bv=None):
    nc = k.nc
    pairs = range(HEADS // 2)
    last_pair = HEADS // 2 - 1
    order = [("shift", 0)]
    for p in range(1, HEADS // 2):
        order += [("s", p), ("max", p - 1), ("pv", p - 1)]
    order += [("max", last_pair), ("pv", last_pair), ("mt", 0), ("raw", 0), ("ot", 0)]
    pe_steps = []
    for what, p in order:
        if what != "raw":
            pe_steps += [f"s{p}_0", f"s{p}_1"] if what in ("s", "shift") else \
                [what] if what in ("ot", "mt") else [f"{what}{p}"]
    act_steps = [f"e{p}_{c}" for p in range(last_pair) for c in range(2)] + \
        ["qcopy", f"e{last_pair}_0", f"e{last_pair}_1", "kcopy", "ot"]
    dve_steps = ["qcopy", "km0", "km1"]
    for p in range(HEADS // 2 - 2):
        dve_steps += [f"max{p}", f"km{p + 2}"]
    dve_steps += [f"max{last_pair - 1}", f"max{last_pair}", "recip", "norm", "shift"]
    pool_steps = [f"qm{p}" for p in range(1, HEADS // 2)] + ["qm0"]
    pe_s = Steps(k, "products", pe_steps, BATCH + 1)
    act_s = Steps(k, "exponentials", act_steps, BATCH + 1)
    dve_s = Steps(k, "vectors", dve_steps, BATCH + 1)
    pool_s = Steps(k, "queries", pool_steps, BATCH + 1)
    k.arena.used = k.arena_kept
    kf = k.arena.take(SEQ)
    qf = k.arena.take(SEQ)
    qb = k.arena.take_bf16(SEQ)
    km = [k.arena.take_bf16(2 * SEQ).rearrange("p (h t) -> p h t", h=2) for _ in range(2)]
    qm = [k.arena.take(2 * SEQ).rearrange("p (h t) -> p h t", h=2) for _ in range(2)]
    prob = [k.arena.take(4 * SEQ).rearrange("p (c h t) -> p c h t", c=2, h=2) for _ in range(2)]
    mx = k.arena.take(2 * HEADS).rearrange("p (c h) -> p c h", c=2)
    shift = k.shift
    recip = k.arena.take(2 * HEADS).rearrange("p (c h) -> p c h", c=2)
    ob = k.arena.take(SEQ).rearrange("p (c f) -> p c f", c=2)
    mbank = [k.psum[:, 2 * u:2 * u + 2, :].rearrange("p c (h t) -> p c h t", h=2) for u in range(2)]
    sbank = [k.psum[:, 4 + u, :].rearrange("p (h t) -> p h t", h=2) for u in range(2)]
    obank = k.psum[:, 6, 0:2 * HEADS * VCOLS].rearrange("p (c h d) -> p c h d", c=2, h=HEADS)
    tbank, mtbank = k.psum[:, 7, :], k.psum[:, 0, 0:SEQ]
    ident, identb = k.c["ident"], k.cb["ident"]
    trips = BATCH + 1
    filled = Count(k, "filled", 3)
    with nc.Block() as block:
        @block.vector
        def _(dve):
            dve.memset(kf, 0.0).then_inc(filled.sem, 1)
            dve.memset(qf, 0.0).then_inc(filled.sem, 1)
            dve.memset(qm[0].rearrange("p h t -> p (h t)"), 0.0).then_inc(filled.sem, 1)
            dve.wait_ge(filled.sem, filled.at(3))

    with nc.Block() as block:
        @block.tensor
        def _(pe):
            pe_s.prime(pe)

            def maxima(i, p):
                pe.wait_ge(dve_s.sem, dve_s.at(i, f"km{p}"))
                if p >= 2:
                    pe.wait_ge(dve_s.sem, dve_s.at(i, f"max{p - 2}"))
                for c in range(2):
                    n = 128 if causal and c == 0 else SEQ
                    last = pe.matmul(mbank[p % 2][:, c, :, 0:n], qb[:, c * 128:(c + 1) * 128],
                                     km[p % 2][:, :, 0:n], start=True, stop=True)
                    if causal:
                        for h in range(2):
                            last = pe.matmul(mbank[p % 2][:, c, h, c * 128:(c + 1) * 128], identb,
                                             k.cb["causal_qk"], start=False, stop=True, skip_group_check=True)
                last.then_inc(pe_s.sem, 1)

            first = [0, 128 if causal else 0]

            def raw(p, c):
                pe.matmul(sbank[c][:, :, first[c]:SEQ], kf[:, c * 128:(c + 1) * 128],
                          qm[p % 2][:, :, first[c]:SEQ], start=True, stop=True)
                if causal:
                    for h in range(2):
                        pe.matmul(sbank[c][:, h, c * 128:(c + 1) * 128], identb, k.cb["causal_kq"],
                                  start=False, stop=True, skip_group_check=True)

            def shifts(p):
                for c in range(2):
                    for h in range(2):
                        last = pe.matmul(sbank[c][:, h, first[c]:SEQ], k.cb["pick_head"][:, 2 * p + h, :],
                                         shift[:, first[c]:SEQ], start=False, stop=True, skip_group_check=True)
                    last.then_inc(pe_s.sem, 1)

            def scores(i, p):
                pe.wait_ge(pool_s.sem, pool_s.at(i, f"qm{p}"))
                for c in range(2):
                    pe.wait_ge(act_s.sem, act_s.at(i, f"e{p - 1}_{c}"))
                    raw(p, c)
                shifts(p)

            def first_raw(i):
                pe.wait_ge(pool_s.sem, pool_s.at(i, "qm0"))
                pe.wait_ge(act_s.sem, act_s.at(i, "kcopy"))
                raw(0, 0)
                raw(0, 1)

            def first_shifts(i):
                pe.wait_ge(dve_s.sem, dve_s.before(i, "shift"))
                shifts(0)

            def values(i, p):
                pe.wait_ge(act_s.sem, act_s.at(i, f"e{p}_1"))
                for h in range(2):
                    head = 2 * p + h
                    for c in range(2):
                        kts = [0] if causal and c == 0 else [0, 1]
                        for kt in kts:
                            vt = v[:, bass.ds(i * 2 + kt, 1), head * VCOLS:(head + 1) * VCOLS]
                            last = pe.matmul(obank[:, c, head, :], prob[p % 2][:, kt, h, c * 128:(c + 1) * 128],
                                             vt.rearrange("p a c -> p (a c)"),
                                             start=(kt == kts[0]), stop=(kt == kts[-1]))
                last.then_inc(pe_s.sem, 1)

            def turn_out(i):
                pe.wait_ge(dve_s.sem, dve_s.at(i, "norm"))
                pe.wait_ge(act_s.sem, act_s.before(i, "ot"))
                for c in range(2):
                    last = pe.transpose(tbank[:, SEQ + c * 128:SEQ + (c + 1) * 128], ob[:, c, :], ident)
                last.then_inc(pe_s.sem, 1)

            def turn_maxima(i):
                pe.wait_ge(dve_s.sem, dve_s.at(i, f"max{last_pair}"))
                for c in range(2):
                    last = pe.transpose(mtbank[0:HEADS, c * 128:(c + 1) * 128], mx[:, c, :], ident)
                last.then_inc(pe_s.sem, 1)

            raw(0, 0)
            raw(0, 1)
            with pe.Fori(0, trips) as i:
                for what, p in order:
                    if what == "shift":
                        first_shifts(i)
                    elif what == "raw":
                        first_raw(i)
                    elif what == "s":
                        scores(i, p)
                    elif what == "pv":
                        values(i, p)
                    elif what == "max":
                        maxima(i, p)
                    elif what == "ot":
                        turn_out(i)
                    else:
                        turn_maxima(i)

        @block.scalar
        def _(act):
            act_s.prime(act)
            act.preload_act_table_set(EXP_LN)
            with act.Fori(0, trips) as i:
                for p in pairs:
                    if p == last_pair:
                        act.wait_ge(pool_s.sem, pool_s.at(i, f"qm{last_pair}"))
                        act.copy(qf, q[:, bass.ds(i * SEQ + SEQ, SEQ)]).then_inc(act_s.sem, 1)
                    for c in range(2):
                        a = 128 if causal and c == 1 else 0
                        act.wait_ge(pe_s.sem, pe_s.at(i, f"s{p}_{c}"))
                        if c == 0:
                            if p >= 2:
                                act.wait_ge(pe_s.sem, pe_s.at(i, f"pv{p - 2}"))
                            else:
                                act.wait_ge(pe_s.sem, pe_s.before(i, f"pv{HEADS // 2 - 2 + p}"))
                        act.activation(prob[p % 2][:, c, :, a:SEQ], sbank[c][:, :, a:SEQ], ACT.Exp, scale=scale)\
                            .then_inc(act_s.sem, 1)
                act.wait_ge(pe_s.sem, pe_s.at(i, f"s{last_pair}_1"))
                act.copy(kf, kk[:, bass.ds(i * SEQ + SEQ, SEQ)]).then_inc(act_s.sem, 1)
                act.wait_ge(pe_s.sem, pe_s.at(i, "ot"))
                act.activation(out[:, tok(i, SEQ)], tbank[:, SEQ:2 * SEQ], ACT.Identity,
                               bias=bv if bv is not None else 0.0).then_inc(act_s.sem, 1)

        @block.vector
        def _(dve):
            dve_s.prime(dve)

            def mask_keys(i, p):
                if p >= 2:
                    dve.wait_ge(pe_s.sem, pe_s.at(i, f"max{p - 2}"))
                for h in range(2):
                    head = 2 * p + h
                    last = dve.tensor_scalar(km[p % 2][:, h, :], kk[:, bass.ds(i * SEQ + SEQ, SEQ)],
                                             k.c["head_mask"][:, head:head + 1], None, ALU.mult)
                last.then_inc(dve_s.sem, 1)

            def row_maxima(i, p):
                dve.wait_ge(pe_s.sem, pe_s.at(i, f"max{p}"))
                if p == 0:
                    dve.wait_ge(pe_s.sem, pe_s.before(i, "mt"))
                if causal:
                    dve.tensor_reduce(mx[:, 0, 2 * p:2 * p + 2], mbank[p % 2][:, 0, :, 0:128], AX_X, ALU.max)
                    dve.tensor_reduce(mx[:, 1, 2 * p:2 * p + 2], mbank[p % 2][:, 1, :, :], AX_X, ALU.max)\
                        .then_inc(dve_s.sem, 1)
                else:
                    dve.tensor_reduce(mx[:, :, 2 * p:2 * p + 2], mbank[p % 2], AX_X, ALU.max).then_inc(dve_s.sem, 1)

            with dve.Fori(0, trips) as i:
                dve.wait_ge(pe_s.sem, pe_s.before(i, f"max{last_pair}"))
                dve.tensor_copy(qb, q[:, bass.ds(i * SEQ + SEQ, SEQ)]).then_inc(dve_s.sem, 1)
                mask_keys(i, 0)
                mask_keys(i, 1)
                for p in pairs:
                    row_maxima(i, p)
                    if p + 2 < HEADS // 2:
                        mask_keys(i, p + 2)
                dve.wait_ge(pe_s.sem, pe_s.at(i, f"pv{last_pair}"))
                dve.reciprocal(recip, obank[:, :, :, HEAD_DIM]).then_inc(dve_s.sem, 1)
                dve.wait_ge(dve_s.sem, dve_s.at(i, "recip"))
                dve.wait_ge(pe_s.sem, pe_s.before(i, "ot"))
                for c in range(2):
                    last = dve.tensor_tensor(ob[:, c, :].rearrange("p (h d) -> p h d", d=HEAD_DIM),
                                             obank[:, c, :, 0:HEAD_DIM],
                                             recip[:, c, :].unsqueeze(2).to_broadcast([128, HEADS, HEAD_DIM]),
                                             ALU.mult)
                last.then_inc(dve_s.sem, 1)
                dve.wait_ge(pe_s.sem, pe_s.at(i, "mt"))
                dve.tensor_scalar(shift[0:HEADS, :], mtbank[0:HEADS, :], -1.0, None, ALU.mult)\
                    .then_inc(dve_s.sem, 1)

        @block.gpsimd
        def _(pool):
            pool_s.prime(pool)
            with pool.Fori(0, trips) as i:
                for p in [*range(1, HEADS // 2), 0]:
                    if p == 0:
                        pool.wait_ge(pe_s.sem, pe_s.at(i, f"s{last_pair - 1}_1"))
                        pool.wait_ge(act_s.sem, act_s.at(i, "qcopy"))
                    elif p == 1:
                        pool.wait_ge(pe_s.sem, pe_s.before(i, f"s{last_pair}_1"))
                    else:
                        pool.wait_ge(pe_s.sem, pe_s.at(i, f"s{p - 2}_1"))
                    pool.tensor_tensor(qm[p % 2], qf.unsqueeze(1).to_broadcast([128, 2, SEQ]),
                                       k.c["head_mask"][:, 2 * p:2 * p + 2].unsqueeze(2).to_broadcast([128, 2, SEQ]),
                                       ALU.mult).then_inc(pool_s.sem, 1)


def output_stage(k, name, parts, add_to, dst, factor=None, bias=None):
    nc = k.nc
    pe_s = Steps(k, "products", ["m0", "m1"], TILES // 2)
    dve_s = Steps(k, "added", ["a0", "a1"], TILES // 2)
    with nc.Block() as block:
        @block.tensor
        def _(pe):
            pe_s.prime(pe)
            with pe.Fori(0, TILES // 2) as i:
                for u in range(2):
                    pe.wait_ge(dve_s.sem, dve_s.before(i, f"a{u}"))
                    for n, (w, src, off) in enumerate(parts):
                        last = pe.matmul(k.psum[:, u, :], w, src[:, bass.ds(i * (2 * TILE) + (u * TILE + off), TILE)],
                                         start=(n == 0), stop=(n == len(parts) - 1))
                    last.then_inc(pe_s.sem, 1)

        @block.vector
        def _(dve):
            dve_s.prime(dve)
            with dve.Fori(0, TILES // 2) as i:
                for u in range(2):
                    cols = bass.ds(i * (2 * TILE) + u * TILE, TILE)
                    dve.wait_ge(pe_s.sem, pe_s.at(i, f"m{u}"))
                    dve.scalar_tensor_tensor(out=dst[:, cols], in0=k.psum[:, u, :],
                                             scalar=bias if bias is not None else float(factor or 1.0),
                                             in1=add_to[:, cols], op0=ALU.add if bias is not None else ALU.mult,
                                             op1=ALU.add).then_inc(dve_s.sem, 1)
def gated_mlp_stage(k, name, src, widths, w_lin, w_act, b_lin, b_act, w_out, func, table, add_to, dst, b_out):
    nc = k.nc
    tiles = range(len(widths))
    pe_steps, act_steps, dve_steps = [], [], []
    for n in tiles:
        pe_steps += [f"act{n}", f"lin{n}"]
        act_steps += [f"f{n}"]
        dve_steps += [f"h{n}"]
    pe_s = Steps(k, "products", pe_steps + ["out"], TILES)
    act_s = Steps(k, "gates", act_steps, TILES)
    dve_s = Steps(k, "hidden", dve_steps + ["sum"], TILES)
    k.arena.reset()
    gate = [k.arena.take(TILE) for _ in range(2)]
    hid = [k.arena.take(TILE) for _ in tiles]
    abank = [k.psum[:, n, :] for n in range(3)]
    lbank = [k.psum[:, 3 + n, :] for n in range(3)]
    obank = k.psum[:, 6, :]
    N = len(widths)

    def earlier(steps, i, prefix, n, back):
        return steps.at(i, f"{prefix}{n - back}") if n >= back else steps.before(i, f"{prefix}{n - back + N}")

    with nc.Block() as block:
        @block.tensor
        def _(pe):
            pe_s.prime(pe)
            with pe.Fori(0, TILES) as i:
                for n, w in enumerate(widths):
                    at = sum(widths[:n])
                    back = 3 if n >= 3 else None
                    last_user = max(m for m in tiles if m % 3 == n % 3)
                    pe.wait_ge(dve_s.sem, dve_s.at(i, f"h{n - 3}") if back else dve_s.before(i, f"h{last_user}"))
                    pe.matmul(abank[n % 3][0:w, :], w_act[:, at:at + w], src[:, tok(i, TILE)],
                              start=True, stop=True).then_inc(pe_s.sem, 1)
                    pe.matmul(lbank[n % 3][0:w, :], w_lin[:, at:at + w], src[:, tok(i, TILE)],
                              start=True, stop=True).then_inc(pe_s.sem, 1)
                pe.wait_ge(dve_s.sem, dve_s.before(i, "sum"))
                for n, w in enumerate(widths):
                    pe.wait_ge(dve_s.sem, dve_s.at(i, f"h{n}"))
                    last = pe.matmul(obank, w_out[0:w, n * 128:(n + 1) * 128], hid[n][0:w, :],
                                     start=(n == 0), stop=(n == N - 1))
                last.then_inc(pe_s.sem, 1)

        @block.scalar
        def _(act):
            act_s.prime(act)
            act.preload_act_table_set(table)
            with act.Fori(0, TILES) as i:
                for n, w in enumerate(widths):
                    act.wait_ge(pe_s.sem, pe_s.at(i, f"act{n}"))
                    if n >= 2:
                        act.wait_ge(dve_s.sem, dve_s.at(i, f"h{n - 2}"))
                    else:
                        act.wait_ge(dve_s.sem, dve_s.before(i, f"h{max(m for m in tiles if m % 2 == n % 2)}"))
                    b = b_act[0:w, n:n + 1] if b_act is not None else 0.0
                    act.activation(gate[n % 2][0:w, :], abank[n % 3][0:w, :], func, bias=b).then_inc(act_s.sem, 1)

        @block.vector
        def _(dve):
            dve_s.prime(dve)
            with dve.Fori(0, TILES) as i:
                for n, w in enumerate(widths):
                    dve.wait_ge(pe_s.sem, pe_s.at(i, f"lin{n}"))
                    dve.wait_ge(pe_s.sem, pe_s.before(i, "out"))
                    dve.wait_ge(act_s.sem, act_s.at(i, f"f{n}"))
                    b = b_lin[0:w, n:n + 1] if b_lin is not None else 1.0
                    dve.scalar_tensor_tensor(out=hid[n][0:w, :], in0=lbank[n % 3][0:w, :], scalar=b,
                                             in1=gate[n % 2][0:w, :],
                                             op0=ALU.add if b_lin is not None else ALU.mult,
                                             op1=ALU.mult).then_inc(dve_s.sem, 1)
                dve.wait_ge(pe_s.sem, pe_s.at(i, "out"))
                dve.scalar_tensor_tensor(out=dst[:, tok(i, TILE)], in0=obank,
                                         scalar=b_out if b_out is not None else 1.0, in1=add_to[:, tok(i, TILE)],
                                         op0=ALU.add if b_out is not None else ALU.mult, op1=ALU.add)\
                    .then_inc(dve_s.sem, 1)


def add_stage(k, name, src, dst):
    half = TOKENS * 5 // 8
    with k.nc.Block() as block:
        @block.vector
        def _(dve):
            dve.tensor_tensor(dst[:, 0:half], dst[:, 0:half], src[:, 0:half], ALU.add)

        @block.gpsimd
        def _(pool):
            pool.tensor_tensor(dst[:, half:TOKENS], dst[:, half:TOKENS], src[:, half:TOKENS], ALU.add)


EXPERTS, HIDDEN = 8, 512


def router_stage(k, name, z, w, R, RT):
    nc = k.nc
    pe_s = Steps(k, "logits", ["logits"], TILES)
    act_s = Steps(k, "tokens", ["copy"], TILES)
    dve_s = Steps(k, "kept", ["lg"], TILES)
    lg = k.arena.take(32 * EXPERTS).rearrange("p (t e) -> p t e", e=EXPERTS)
    zt = k.arena.take(TILE)
    lbank = k.psum[:, 0, 0:32].rearrange("p (t e) -> p t e", e=EXPERTS)
    with nc.Block() as block:
        @block.tensor
        def _(pe):
            pe_s.prime(pe)
            with pe.Fori(0, TILES) as i:
                pe.wait_ge(act_s.sem, act_s.at(i, "copy"))
                pe.wait_ge(dve_s.sem, dve_s.before(i, "lg"))
                for j in range(4):
                    pe.matmul(lbank[:, j, :], zt[:, j * 128:(j + 1) * 128], w["wr"], start=True, stop=False)
                    last = pe.matmul(lbank[:, j, :], k.c["ones"][0:1, :], w["br"][0:1, :], start=False, stop=True)
                last.then_inc(pe_s.sem, 1)

        @block.scalar
        def _(act):
            act_s.prime(act)
            with act.Fori(0, TILES) as i:
                act.wait_ge(pe_s.sem, pe_s.before(i, "logits"))
                act.copy(zt, z[:, tok(i, TILE)]).then_inc(act_s.sem, 1)

        @block.vector
        def _(dve):
            dve_s.prime(dve)
            with dve.Fori(0, TILES) as i:
                dve.wait_ge(pe_s.sem, pe_s.at(i, "logits"))
                dve.tensor_copy(lg[:, bass.ds(i * 4, 4), :], lbank).then_inc(dve_s.sem, 1)

    chain = Count(k, "router_chain", 18)
    weighed = Count(k, "router_exp", 1)
    turned = Count(k, "router_turned", 8)
    shape = [128, 32, EXPERTS]

    def wide(ap):
        return ap.unsqueeze(2).to_broadcast(shape)

    def small():
        return k.arena.take(32)

    top, first, second = [small(), small()], k.arena.take(256), k.arena.take(256)
    first, second = (a.rearrange("p (t e) -> p t e", e=EXPERTS) for a in (first, second))
    rank, diff, ex, den, w1, w2 = small(), small(), small(), small(), small(), small()
    even = k.arena.take(256).rearrange("p (t e) -> p t e", e=EXPERTS)
    rest = k.arena.take(256).rearrange("p (t e) -> p t e", e=EXPERTS)
    rev = k.c["reverse"].unsqueeze(1).to_broadcast(shape)
    with nc.Block() as block:
        @block.vector
        def _(dve):
            def pick(at, values, best, onehot):
                dve.tensor_reduce(best, values, AX_X, ALU.max).then_inc(chain.sem, 1)
                dve.wait_ge(chain.sem, chain.at(at + 1))
                dve.tensor_tensor(even, values, wide(best), ALU.is_equal).then_inc(chain.sem, 1)
                dve.wait_ge(chain.sem, chain.at(at + 2))
                dve.tensor_tensor(even, even, rev, ALU.mult).then_inc(chain.sem, 1)
                dve.wait_ge(chain.sem, chain.at(at + 3))
                dve.tensor_reduce(rank, even, AX_X, ALU.max).then_inc(chain.sem, 1)
                dve.wait_ge(chain.sem, chain.at(at + 4))
                dve.tensor_tensor(onehot, rev, wide(rank), ALU.is_equal).then_inc(chain.sem, 1)
                dve.wait_ge(chain.sem, chain.at(at + 5))

            pick(0, lg, top[0], first)
            dve.scalar_tensor_tensor(out=rest, in0=first, scalar=NEG, in1=lg, op0=ALU.mult, op1=ALU.add)\
                .then_inc(chain.sem, 1)
            dve.wait_ge(chain.sem, chain.at(6))
            pick(6, rest, top[1], second)
            dve.tensor_tensor(diff, top[1], top[0], ALU.subtract).then_inc(chain.sem, 1)
            dve.wait_ge(weighed.sem, weighed.at(1))
            dve.tensor_scalar(den, ex, 1.0, None, ALU.add).then_inc(chain.sem, 1)
            dve.wait_ge(chain.sem, chain.at(13))
            dve.reciprocal(w1, den).then_inc(chain.sem, 1)
            dve.wait_ge(chain.sem, chain.at(14))
            dve.tensor_tensor(w2, ex, w1, ALU.mult).then_inc(chain.sem, 1)
            dve.tensor_tensor(first, first, wide(w1), ALU.mult).then_inc(chain.sem, 1)
            dve.wait_ge(chain.sem, chain.at(15))
            dve.tensor_tensor(second, second, wide(w2), ALU.mult).then_inc(chain.sem, 1)
            dve.wait_ge(chain.sem, chain.at(17))
            dve.tensor_tensor(R, first, second, ALU.add).then_inc(chain.sem, 1)
            for b in range(8):
                dve.wait_ge(turned.sem, turned.at(b + 1))
                dve.tensor_copy(RT[0:EXPERTS, b * 512:(b + 1) * 512], k.psum[0:EXPERTS, b, :])

        @block.scalar
        def _(act):
            act.preload_act_table_set(EXP_LN)
            act.wait_ge(chain.sem, chain.at(12))
            act.activation(ex, diff, ACT.Exp).then_inc(weighed.sem, 1)

        @block.tensor
        def _(pe):
            pe.wait_ge(chain.sem, chain.at(18))
            for b in range(8):
                for j in range(4):
                    last = pe.transpose(k.psum[0:EXPERTS, b, j * 128:(j + 1) * 128], R[:, 4 * b + j, :], k.c["ident"])
                last.then_inc(turned.sem, 1)


def experts_stage(k, name, z, w, R, RT, out):
    nc = k.nc
    ex, quads = range(EXPERTS), range(4)
    pe_steps, act_steps, dve_steps = ["base"], ["zcopy", "rcopy", "rtcopy"], []
    for e in ex:
        pe_steps += [f"h{e}_{f}" for f in quads] + ([f"o{e - 1}"] if e else [])
        act_steps += ([] if e else ["base"]) + [f"r{e}_{f}" for f in quads]
        dve_steps += [f"a{e}"]
    pe_s = Steps(k, "products", pe_steps + [f"o{EXPERTS - 1}", "turn"], TILES)
    act_s = Steps(k, "relus", act_steps + ["out"], TILES)
    dve_s = Steps(k, "weighed", dve_steps, TILES)
    zt = k.arena.take(TILE)
    r4 = k.arena.take(4 * EXPERTS).rearrange("p (t e) -> p t e", e=EXPERTS)
    rt4 = k.arena.take(TILE)
    hid = [k.arena.take(4 * TILE).rearrange("p (f t) -> p f t", f=4) for _ in range(2)]
    acc = k.arena.take(TILE)
    w1 = w["w1"].rearrange("p (e f) -> p e f", e=EXPERTS)
    w2 = w["w2"].rearrange("p (e f d) -> p e f d", e=EXPERTS, f=4)
    b1 = w["b1"].rearrange("p (e f) -> p e f", e=EXPERTS)
    hbank = [k.psum[:, f, :] for f in quads]
    obank = [k.psum[:, 4 + u, :] for u in range(2)]
    base, turn = k.psum[:, 6, :], k.psum[:, 7, :]

    def part(ap, j):
        return ap[:, j * 128:(j + 1) * 128]

    with nc.Block() as block:
        @block.tensor
        def _(pe):
            pe_s.prime(pe)

            def expert_out(i, e):
                pe.wait_ge(act_s.sem, act_s.at(i, f"r{e}_3"))
                if e >= 2:
                    pe.wait_ge(dve_s.sem, dve_s.at(i, f"a{e - 2}"))
                else:
                    pe.wait_ge(dve_s.sem, dve_s.before(i, f"a{EXPERTS - 2 + e}"))
                for j in quads:
                    for f in quads:
                        last = pe.matmul(part(obank[e % 2], j), part(hid[e % 2][:, f, :], j), w2[:, e, f, :],
                                         start=(f == 0), stop=(f == 3))
                last.then_inc(pe_s.sem, 1)

            with pe.Fori(0, TILES) as i:
                pe.wait_ge(act_s.sem, act_s.at(i, "rtcopy"))
                pe.wait_ge(act_s.sem, act_s.before(i, "base"))
                for j in quads:
                    pe.matmul(part(base, j), part(zt, j), k.c["ident"], start=True, stop=False)
                    last = pe.matmul(part(base, j), part(rt4, j)[0:EXPERTS, :], w["b2"][0:EXPERTS, :],
                                     start=False, stop=True)
                last.then_inc(pe_s.sem, 1)
                for e in ex:
                    for f in quads:
                        if e:
                            pe.wait_ge(act_s.sem, act_s.at(i, f"r{e - 1}_{f}"))
                        else:
                            pe.wait_ge(act_s.sem, act_s.before(i, f"r{EXPERTS - 1}_{f}"))
                        pe.matmul(hbank[f], w1[:, e, f * 128:(f + 1) * 128], zt, start=True, stop=True)\
                            .then_inc(pe_s.sem, 1)
                    if e:
                        expert_out(i, e - 1)
                expert_out(i, EXPERTS - 1)
                pe.wait_ge(dve_s.sem, dve_s.at(i, f"a{EXPERTS - 1}"))
                pe.wait_ge(act_s.sem, act_s.before(i, "out"))
                for j in quads:
                    last = pe.transpose(part(turn, j), part(acc, j), k.c["ident"])
                last.then_inc(pe_s.sem, 1)

        @block.scalar
        def _(act):
            act_s.prime(act)
            with act.Fori(0, TILES) as i:
                act.wait_ge(pe_s.sem, pe_s.before(i, f"h{EXPERTS - 1}_3"))
                act.copy(zt, z[:, tok(i, TILE)]).then_inc(act_s.sem, 1)
                act.wait_ge(dve_s.sem, dve_s.before(i, f"a{EXPERTS - 1}"))
                act.copy(r4, R[:, bass.ds(i * 4, 4), :]).then_inc(act_s.sem, 1)
                act.copy(rt4[0:EXPERTS, :], RT[0:EXPERTS, tok(i, TILE)]).then_inc(act_s.sem, 1)
                act.wait_ge(pe_s.sem, pe_s.at(i, "base"))
                act.wait_ge(pe_s.sem, pe_s.before(i, "turn"))
                act.copy(acc, base).then_inc(act_s.sem, 1)
                for e in ex:
                    for f in quads:
                        act.wait_ge(pe_s.sem, pe_s.at(i, f"h{e}_{f}"))
                        if f == 0:
                            if e >= 2:
                                act.wait_ge(pe_s.sem, pe_s.at(i, f"o{e - 2}"))
                            else:
                                act.wait_ge(pe_s.sem, pe_s.before(i, f"o{EXPERTS - 2 + e}"))
                        act.activation(hid[e % 2][:, f, :], hbank[f], ACT.Relu, bias=b1[:, e, f:f + 1])\
                            .then_inc(act_s.sem, 1)
                act.wait_ge(pe_s.sem, pe_s.at(i, "turn"))
                act.copy(out[:, tok(i, TILE)], turn).then_inc(act_s.sem, 1)

        @block.vector
        def _(dve):
            dve_s.prime(dve)
            with dve.Fori(0, TILES) as i:
                for e in ex:
                    dve.wait_ge(pe_s.sem, pe_s.at(i, f"o{e}"))
                    if e == 0:
                        dve.wait_ge(act_s.sem, act_s.at(i, "base"))
                    else:
                        dve.wait_ge(dve_s.sem, dve_s.at(i, f"a{e - 1}"))
                    for j in quads:
                        last = dve.scalar_tensor_tensor(out=part(acc, j), in0=part(obank[e % 2], j),
                                                        scalar=r4[:, j, e:e + 1], in1=part(acc, j),
                                                        op0=ALU.mult, op1=ALU.add)
                    last.then_inc(dve_s.sem, 1)


def l1_ffn(k, name, w):
    norm_stage(k, f"{name}_ln", k.X, [(k.Z, None, None)], True, "eps5")
    k.arena.reset()
    R = k.arena.take(32 * EXPERTS).rearrange("p (t e) -> p t e", e=EXPERTS)
    RT = k.Y
    router_stage(k, f"{name}_router", k.Z, w, R, RT)
    k.arena.used = 32 * EXPERTS
    experts_stage(k, f"{name}_experts", k.Z, w, R, RT, k.H)
    norm_stage(k, f"{name}_last", k.H, [(k.Z, w["gamma"], w["beta"])], True, "eps5")
    add_stage(k, f"{name}_add", k.Z, k.X)


def more_groups(groups, i):
    A = "L1_ffn_"
    w1, w2 = i[A + "W1"], i[A + "W2"]
    groups["l1_ffn"] = {
        "w1": w1.transpose(2, 0, 1), "w2": w2.transpose(2, 0, 1).reshape(4, 128, EXPERTS, 128).transpose(1, 2, 0, 3),
        "b1": i[A + "b1"].reshape(EXPERTS, 4, 128).transpose(2, 0, 1), "b2": i[A + "b2"], "wr": i[A + "Wr"].T,
        "br": i[A + "br"].reshape(1, -1), "gamma": column(i[A + "gamma"]), "beta": column(i[A + "beta"])}
    groups["l0_ffn"] = l0_ffn_group(i)
    groups["l1_attn_b"] = l1_attn_b_group(i)
    groups["l0_attn_a"], groups["ssm_scan"] = l0_attn_a_groups(i)


WHEADS, WDIM = 8, 64
TINY = 1e-24
TINY_SCALE = 2.0 ** 20


def shift_stage(k, name, src, dst):

    def per_batch(ap):
        return ap.rearrange("p (b t) -> p b t", t=SEQ)

    with k.nc.Block() as block:
        @block.vector
        def _(dve):
            dve.memset(per_batch(dst[64:128, 0:TOKENS])[:, :, 0:1], 0.0)
            dve.tensor_copy(per_batch(dst[64:128, 0:TOKENS])[:, :, 1:SEQ],
                            per_batch(src[64:128, 0:TOKENS])[:, :, 0:SEQ - 1])

        @block.scalar
        def _(act):
            act.copy(dst[0:64, 0:TOKENS // 2], src[0:64, 0:TOKENS // 2])

        @block.gpsimd
        def _(pool):
            pool.tensor_copy(dst[0:64, TOKENS // 2:TOKENS], src[0:64, TOKENS // 2:TOKENS])


def window_attention_stage(k, name, src, y_padded, w, tables):
    nc = k.nc
    groups, heads = range(4), range(WHEADS)
    pe_steps = ["proj0", "proj1", "s0", "s1"]
    for n, first in enumerate((["ss0"], ["ss1"], ["rot0", "proj2"], ["rot1", "proj3"], ["ss2"], ["ss3"], ["rot2"],
                               ["rot3"])):
        pe_steps += ([f"pv{n}"] + first if n in (2, 3) else first + [f"pv{n}"]) + \
            ([f"s{n + 2}"] if n < 6 else [])
    pe_steps += ["max0", "v0", "v1", "turn0", "turn1", "max1", "max2", "max3", "wo", "mt"]
    act_steps = ["hcopy", "sq0", "sq1", "e0", "e1", "ln0", "exp0", "e2", "ln1", "exp1", "e3", "sq2", "e4", "sq3",
                 "e5", "ln2", "exp2", "e6", "ln3", "exp3", "e7", "v0", "v1", "turn0", "turn1"]
    dve_steps = ["clip0", "clip1", "nrm0", "nrm1", "sin0", "add0", "sin1", "add1"]
    dve_steps += ["clip2", "clip3", "nrm2", "nrm3", "sin2", "sin3", "recip", "norm", "max0", "add2", "add3", "max1", "max2", "max3", "sum", "shift"]
    pool_steps = ["cos0", "cos1", "low0", "low1", "cos2", "cos3", "low2", "low3"]
    trips = BATCH + 1
    pe_s = Steps(k, "products", pe_steps, trips)
    act_s = Steps(k, "lookups", act_steps, trips)
    dve_s = Steps(k, "vectors", dve_steps, trips)
    pool_s = Steps(k, "sides", pool_steps, trips)
    k.arena.reset()
    take = k.arena.take
    hb = take(SEQ)
    sq = [take(TILE) for _ in groups]
    rs = [take(TILE) for _ in range(2)]
    flat = [take(TILE) for _ in range(2)]
    cosd = [take(TILE) for _ in range(2)]
    qk = take(8 * SEQ).rearrange("p (f t) -> p f t", f=8)
    qkb = k.arena.take_bf16(8 * SEQ).rearrange("p (f t) -> p f t", f=8)
    v = take(2 * WHEADS * (WDIM + 1)).rearrange("p (c h d) -> p c h d", c=2, h=WHEADS)
    prob = [take(320) for _ in range(2)]
    mx = take(2 * WHEADS).rearrange("p (c h) -> p c h", c=2)
    recip = take(16)
    ob = take(2 * 512).rearrange("p (c h d) -> p c h d", c=2, h=WHEADS)
    oT = take(4 * SEQ).rearrange("p (f t) -> p f t", f=4)
    shift = k.shift
    bank = [k.psum[:, n, :] for n in range(8)]
    mbanks = [k.psum[:, 3:5, :], k.psum[:, 0:2, :]] * 2

    def flat8(g):
        return qk[:, 2 * g:2 * g + 2, :].rearrange("p f t -> p (f t)")

    def unit(h, c):
        n = 2 * h + c
        return bank[5 + n // 6][:, 65 * (n % 6):65 * (n % 6) + 65]

    filled = Count(k, "filled", 4)
    with nc.Block() as block:
        @block.vector
        def _(dve):
            dve.memset(v.rearrange("p c h d -> p (c h d)"), 1.0).then_inc(filled.sem, 1)
            dve.memset(qk.rearrange("p f t -> p (f t)"), 0.0).then_inc(filled.sem, 1)
            dve.memset(shift[:, :], 0.0).then_inc(filled.sem, 1)
            dve.memset(src[:, TOKENS:TOKENS + SEQ], 0.0).then_inc(filled.sem, 1)
            dve.wait_ge(filled.sem, filled.at(4))

    with nc.Block() as block:
        @block.tensor
        def _(pe):
            pe_s.prime(pe)

            def project(i, g):
                if g >= 2:
                    pe.wait_ge(dve_s.sem, dve_s.at(i, f"nrm{g - 2}"))
                for m in range(2):
                    at = m * 512 + g * 128
                    last = pe.matmul(bank[g % 2][:, m * SEQ:(m + 1) * SEQ], w["wqkv"][:, at:at + 128], hb,
                                     start=True, stop=True)
                last.then_inc(pe_s.sem, 1)

            def sum_squares(i, g):
                pe.wait_ge(act_s.sem, act_s.at(i, f"sq{g}"))
                if g == 0:
                    pe.wait_ge(dve_s.sem, dve_s.before(i, "sum"))
                else:
                    pe.wait_ge(dve_s.sem, dve_s.at(i, {1: "clip0", 2: "sin1", 3: "clip2"}[g]))
                pe.matmul(bank[2], k.c64["head_sum"], sq[g], start=True, stop=True).then_inc(pe_s.sem, 1)

            def rotate(i, g):
                pe.wait_ge(dve_s.sem, dve_s.at(i, f"nrm{g}"))
                if g % 2:
                    pe.wait_ge(dve_s.sem, dve_s.at(i, f"sin{g - 1}"))
                pe.matmul(bank[2], k.c64["rot"], flat[g % 2], start=True, stop=True).then_inc(pe_s.sem, 1)

            def scores(i, h):
                f, rows = h // 2, slice(64 * (h % 2), 64 * (h % 2) + 64)
                if h >= 2:
                    pe.wait_ge(act_s.sem, act_s.at(i, f"e{h - 2}"))
                else:
                    pe.wait_ge(dve_s.sem, dve_s.before(i, "shift"))
                to = bank[3 + h % 2]
                pe.matmul(to[:, 0:192], qk[rows, 2 * f + 1, 0:128], qk[rows, 2 * f, 0:192], start=True, stop=True)
                pe.matmul(to[:, 192:320], qk[rows, 2 * f + 1, 128:256], qk[rows, 2 * f, 128:256], start=False,
                          stop=True, skip_group_check=True)
                pe.matmul(to[:, 0:320], k.cb["ident"], k.cb64["band_kq"], start=False, stop=True,
                          skip_group_check=True)
                pe.matmul(to[:, 0:192], k.cb["pick_head"][:, h, :], shift[:, 0:192], start=False, stop=True,
                          skip_group_check=True)
                pe.matmul(to[:, 192:320], k.cb["pick_head"][:, h, :], shift[:, 128:256], start=False, stop=True,
                          skip_group_check=True).then_inc(pe_s.sem, 1)

            def values(i, h):
                pe.wait_ge(act_s.sem, act_s.at(i, f"e{h}"))
                pb = prob[h % 2]
                pe.matmul(unit(h, 0), pb[:, 0:128], v[:, 0, h, :], start=True, stop=True)
                pe.matmul(unit(h, 1), pb[:, 192:320], v[:, 1, h, :], start=True, stop=True)
                pe.matmul(unit(h, 1)[0:64, :], pb[:, 128:192], v[:, 0, h, :], start=False, stop=True,
                          skip_group_check=True).then_inc(pe_s.sem, 1)

            def maxima(i, f):
                pe.wait_ge(pool_s.sem, pool_s.at(i, f"low{f}"))
                for r in range(2):
                    to, rows = mbanks[f][:, r, :], slice(64 * r, 64 * r + 64)
                    pe.matmul(to[:, 0:128], qkb[rows, 2 * f, 0:128], qkb[rows, 2 * f + 1, 0:128],
                              start=True, stop=True)
                    pe.matmul(to[:, 128:320], qkb[rows, 2 * f, 128:256], qkb[rows, 2 * f + 1, 64:256],
                              start=False, stop=True, skip_group_check=True)
                    last = pe.matmul(to[:, 0:320], k.cb["ident"], k.cb64["band_qk"], start=False, stop=True,
                                     skip_group_check=True)
                last.then_inc(pe_s.sem, 1)

            def turn(i, half):
                for m in range(2):
                    f = 2 * half + m
                    for c in range(2):
                        last = pe.transpose(bank[3 + half][:, m * SEQ + c * 128:m * SEQ + (c + 1) * 128],
                                            ob[:, c, 2 * f:2 * f + 2, :].rearrange("p h d -> p (h d)"),
                                            k.c["ident"])
                last.then_inc(pe_s.sem, 1)

            with pe.Fori(0, trips) as i:
                pe.wait_ge(act_s.sem, act_s.at(i, "hcopy"))
                pe.wait_ge(dve_s.sem, dve_s.before(i, "max3"))
                project(i, 0)
                project(i, 1)
                scores(i, 0)
                scores(i, 1)
                for n in heads:
                    if n in (0, 1):
                        sum_squares(i, n)
                    elif n in (4, 5):
                        sum_squares(i, n - 2)
                    elif n in (6, 7):
                        rotate(i, n - 4)
                    values(i, n)
                    if n in (2, 3):
                        rotate(i, n - 2)
                        project(i, n)
                    if n < 6:
                        scores(i, n + 2)
                maxima(i, 0)
                for c in range(2):
                    pe.matmul(bank[c], hb[:, c * 128:(c + 1) * 128], w["wqkv"][:, 1024:1536],
                              start=True, stop=True).then_inc(pe_s.sem, 1)
                pe.wait_ge(dve_s.sem, dve_s.at(i, "max0"))
                turn(i, 0)
                turn(i, 1)
                pe.wait_ge(act_s.sem, act_s.at(i, "v1"))
                maxima(i, 1)
                pe.wait_ge(act_s.sem, act_s.at(i, "turn1"))
                maxima(i, 2)
                pe.wait_ge(dve_s.sem, dve_s.at(i, "max1"))
                maxima(i, 3)
                for f in groups:
                    last = pe.matmul(bank[2][:, 0:SEQ], w["wo"][:, f * 128:(f + 1) * 128], oT[:, f, :],
                                     start=(f == 0), stop=(f == 3))
                last.then_inc(pe_s.sem, 1)
                pe.wait_ge(dve_s.sem, dve_s.at(i, "max3"))
                for c in range(2):
                    last = pe.transpose(bank[5][0:WHEADS, c * 128:(c + 1) * 128], mx[:, c, :], k.c["ident"])
                last.then_inc(pe_s.sem, 1)

        @block.scalar
        def _(act):
            act_s.prime(act)
            act.preload_act_table_set(EXP_LN)

            def square(i, g):
                act.wait_ge(pe_s.sem, pe_s.at(i, f"proj{g}"))
                act.wait_ge(pe_s.sem, pe_s.before(i, f"ss{g}"))
                act.activation(sq[g], bank[g % 2], ACT.Square).then_inc(act_s.sem, 1)

            def root(i, g):
                act.wait_ge(dve_s.sem, dve_s.at(i, f"clip{g}"))
                act.activation(rs[g % 2], rs[g % 2], ACT.Ln, scale=TINY_SCALE).then_inc(act_s.sem, 1)
                act.wait_ge(act_s.sem, act_s.at(i, f"ln{g}"))
                act.activation(rs[g % 2], rs[g % 2], ACT.Exp, scale=-0.5, bias=k.c64["half_ln"])\
                    .then_inc(act_s.sem, 1)

            def probabilities(i, h):
                act.wait_ge(pe_s.sem, pe_s.at(i, f"s{h}"))
                if h >= 2:
                    act.wait_ge(pe_s.sem, pe_s.at(i, f"pv{h - 2}"))
                act.activation(prob[h % 2], bank[3 + h % 2][:, 0:320], ACT.Exp, scale=8.0).then_inc(act_s.sem, 1)

            with act.Fori(0, trips) as i:
                act.wait_ge(pe_s.sem, pe_s.before(i, "v1"))
                act.copy(hb, src[:, tok(i, SEQ)]).then_inc(act_s.sem, 1)
                square(i, 0)
                square(i, 1)
                probabilities(i, 0)
                probabilities(i, 1)
                root(i, 0)
                probabilities(i, 2)
                root(i, 1)
                probabilities(i, 3)
                square(i, 2)
                probabilities(i, 4)
                square(i, 3)
                probabilities(i, 5)
                root(i, 2)
                probabilities(i, 6)
                root(i, 3)
                probabilities(i, 7)
                for c in range(2):
                    act.wait_ge(pe_s.sem, pe_s.at(i, f"v{c}"))
                    act.copy(v[:, c, :, 0:WDIM], bank[c].rearrange("p (h d) -> p h d", d=WDIM))\
                        .then_inc(act_s.sem, 1)
                for half in range(2):
                    act.wait_ge(pe_s.sem, pe_s.at(i, f"turn{half}"))
                    if half == 0:
                        act.wait_ge(pe_s.sem, pe_s.before(i, "wo"))
                    act.copy(oT[:, 2 * half:2 * half + 2, :].rearrange("p f t -> p (f t)"), bank[3 + half])\
                        .then_inc(act_s.sem, 1)

        @block.vector
        def _(dve):
            dve_s.prime(dve)

            def clip(i, g):
                dve.wait_ge(pe_s.sem, pe_s.at(i, f"ss{g}"))
                if g >= 2:
                    dve.wait_ge(dve_s.sem, dve_s.at(i, f"add{g - 2}"))
                    dve.wait_ge(pool_s.sem, pool_s.at(i, f"low{g - 2}"))
                else:
                    dve.wait_ge(pool_s.sem, pool_s.before(i, f"low{g + 2}"))
                dve.tensor_scalar(rs[g % 2], bank[2], TINY, None, ALU.max).then_inc(dve_s.sem, 1)

            def unit_vectors(i, g):
                dve.wait_ge(act_s.sem, act_s.at(i, f"exp{g}"))
                if g >= 2:
                    dve.wait_ge(pe_s.sem, pe_s.at(i, f"rot{g - 2}"))
                    dve.wait_ge(pool_s.sem, pool_s.at(i, f"cos{g - 2}"))
                for m, scale in ((0, w["qs"]), (1, w["ks"])):
                    cols = slice(m * SEQ, (m + 1) * SEQ)
                    last = dve.scalar_tensor_tensor(out=flat[g % 2][:, cols], in0=bank[g % 2][:, cols], scalar=scale,
                                                    in1=rs[g % 2][:, cols], op0=ALU.mult, op1=ALU.mult)
                last.then_inc(dve_s.sem, 1)

            def rotary(i, g):
                dve.wait_ge(pe_s.sem, pe_s.at(i, f"rot{g}"))
                dve.wait_ge(dve_s.sem, dve_s.at(i, f"nrm{g}"))
                dve.tensor_tensor(rs[g % 2], bank[2], tables["sin"], ALU.mult).then_inc(dve_s.sem, 1)

            def turned(i, g):
                dve.wait_ge(dve_s.sem, dve_s.at(i, f"sin{g}"))
                dve.wait_ge(pool_s.sem, pool_s.at(i, f"cos{g}"))
                dve.wait_ge(pe_s.sem, pe_s.at(i, f"s{2 * g + 1}"))
                dve.tensor_tensor(flat8(g), cosd[g % 2], rs[g % 2], ALU.add).then_inc(dve_s.sem, 1)

            with dve.Fori(0, trips) as i:
                for a in (0, 2):
                    clip(i, a)
                    clip(i, a + 1)
                    unit_vectors(i, a)
                    unit_vectors(i, a + 1)
                    rotary(i, a)
                    if a == 0:
                        turned(i, 0)
                    rotary(i, a + 1)
                    if a == 0:
                        turned(i, 1)
                dve.wait_ge(pe_s.sem, pe_s.at(i, f"pv{WHEADS - 1}"))
                for b, n in ((5, 6), (6, 6), (7, 4)):
                    o = bank[b][:, 0:65 * n].rearrange("p (n d) -> p n d", d=65)
                    last = dve.reciprocal(recip[:, 6 * (b - 5):6 * (b - 5) + n], o[:, :, WDIM])
                last.then_inc(dve_s.sem, 1)
                dve.wait_ge(dve_s.sem, dve_s.at(i, "recip"))
                dve.wait_ge(pe_s.sem, pe_s.before(i, "turn1"))
                for b, n in ((5, 6), (6, 6), (7, 4)):
                    for c in range(2):
                        o = bank[b][:, 0:65 * n].rearrange("p (h c d) -> p h c d", c=2, d=65)[:, :, c, 0:WDIM]
                        r = recip[:, 6 * (b - 5):6 * (b - 5) + n].rearrange("p (h c) -> p h c", c=2)[:, :, c]
                        last = dve.tensor_tensor(ob[:, c, 3 * (b - 5):3 * (b - 5) + n // 2, :], o,
                                                 r.unsqueeze(2).to_broadcast([128, n // 2, WDIM]), ALU.mult)
                last.then_inc(dve_s.sem, 1)
                for f in groups:
                    if f == 0:
                        dve.wait_ge(pe_s.sem, pe_s.before(i, "mt"))
                    if f == 1:
                        turned(i, 2)
                        turned(i, 3)
                    dve.wait_ge(pe_s.sem, pe_s.at(i, f"max{f}"))
                    two = mbanks[f]
                    dve.tensor_reduce(mx[:, 0, 2 * f:2 * f + 2], two[:, :, 0:128], AX_X, ALU.max)
                    dve.tensor_reduce(mx[:, 1, 2 * f:2 * f + 2], two[:, :, 128:320], AX_X, ALU.max)\
                        .then_inc(dve_s.sem, 1)
                dve.wait_ge(pe_s.sem, pe_s.at(i, "wo"))
                dve.tensor_tensor(y_padded[:, tok(i, SEQ)], bank[2][:, 0:SEQ], y_padded[:, tok(i, SEQ)], ALU.add)\
                    .then_inc(dve_s.sem, 1)
                dve.wait_ge(pe_s.sem, pe_s.at(i, "mt"))
                dve.tensor_scalar(shift[0:WHEADS, :], bank[5][0:WHEADS, 0:SEQ], -1.0, None, ALU.mult)\
                    .then_inc(dve_s.sem, 1)

        @block.gpsimd
        def _(pool):
            pool_s.prime(pool)

            def cosine(i, g):
                pool.wait_ge(dve_s.sem, dve_s.at(i, f"nrm{g}"))
                if g >= 2:
                    pool.wait_ge(dve_s.sem, dve_s.at(i, f"add{g - 2}"))
                pool.tensor_tensor(cosd[g % 2], flat[g % 2], tables["cos"], ALU.mult).then_inc(pool_s.sem, 1)

            def low(i, g):
                pool.wait_ge(pool_s.sem, pool_s.at(i, f"cos{g}"))
                pool.wait_ge(dve_s.sem, dve_s.at(i, f"sin{g}"))
                if g == 0:
                    pool.wait_ge(pe_s.sem, pe_s.before(i, "max3"))
                pool.tensor_tensor(qkb[:, 2 * g:2 * g + 2, :].rearrange("p f t -> p (f t)"), cosd[g % 2],
                                   rs[g % 2], ALU.add).then_inc(pool_s.sem, 1)

            with pool.Fori(0, trips) as i:
                for g in (0, 2):
                    cosine(i, g)
                    cosine(i, g + 1)
                    low(i, g)
                    low(i, g + 1)


def l0_ffn(k, name, w):
    norm_stage(k, f"{name}_ln", k.X, [(k.Y, None, None)], True, "eps5")
    zero_stage(k, f"{name}_pad", [(k.Y_padded[:, 0:SEQ], 0.0)])
    k.c64 = {n: w[n] for n in ("head_sum", "rot", "half_ln")}
    k.cb64 = {n: w[n].bitcast(BF16) for n in ("band_qk", "band_kq")}
    tables = {n: w[n] for n in ("sin", "cos")}
    for layer in range(2):
        s = f"{name}_{layer}"
        lw = {n[:-1]: a for n, a in w.items() if n.endswith(str(layer))}
        shift_stage(k, f"{s}_shift1", k.Y, k.H)
        window_attention_stage(k, f"{s}_attn", k.H, k.Y_padded, lw, tables)
        shift_stage(k, f"{s}_shift2", k.Y, k.H)
        norm_stage(k, f"{s}_norm", k.H, [(k.Z, lw["lg"], lw["lb"])], True, "eps5")
        gated_mlp_stage(k, f"{s}_mlp", k.Z, [128, 128, 85], lw["w_lin"], lw["w_act"], lw["b_lin"], lw["b_act"],
                        lw["w_out"], ACT.Gelu, GELU_SET, k.Y, k.Y, lw["b_out"])
    add_stage(k, f"{name}_add", k.Y, k.X)


def l0_ffn_group(i):
    A = "L0_ffn_"
    f = np.float32
    g = {}
    for layer in range(2):
        w1, b1, w2 = i[A + "w1"][layer], i[A + "b1"][layer], i[A + "w2"][layer]
        hid = w2.shape[0]

        def rows(a):
            out = np.zeros((128, 3, a.shape[1]), a.dtype)
            for n in range(3):
                part = a[n * 128:(n + 1) * 128]
                out[0:part.shape[0], n] = part
            return out

        g[f"wqkv{layer}"] = i[A + "wqkv"][layer]
        g[f"wo{layer}"] = i[A + "wo"][layer].reshape(4, 128, 128).transpose(1, 0, 2)
        g[f"w_lin{layer}"], g[f"w_act{layer}"] = w1[:, 0:hid], w1[:, hid:]
        g[f"w_out{layer}"] = rows(w2)
        g[f"b_lin{layer}"], g[f"b_act{layer}"] = rows(column(b1[0:hid])), rows(column(b1[hid:]))
        g[f"b_out{layer}"] = column(i[A + "b2"][layer])
        g[f"qs{layer}"] = column(np.tile(i[A + "q_scale"][layer], 2))
        g[f"ks{layer}"] = column(np.tile(i[A + "k_scale"][layer], 2))
        g[f"lg{layer}"], g[f"lb{layer}"] = column(i[A + "ln_g"][layer]), column(i[A + "ln_b"][layer])
    feature = np.arange(128)
    g["head_sum"] = (feature[:, None] // 64 == feature[None, :] // 64).astype(f)
    g["rot"] = rotation(64, False)
    g["half_ln"] = np.full((128, 1), 0.5 * np.log(TINY_SCALE), f)
    half_idx = np.arange(0, 64, 2, dtype=f)
    inv = (1.0 / 10000.0 ** (half_idx / f(64))).astype(f)
    t = np.arange(SEQ, dtype=f)
    freqs = (t[:, None] * inv[None, :]).astype(f)
    base = ((half_idx + f(0.4 * 64)) / f(1.4 * 64)).astype(f)
    power = ((t - SEQ // 2) / f(32.0)).astype(f)
    scale = (base[None, :] ** power[:, None]).astype(f)

    def table(a):
        return np.tile(np.concatenate([a, a], 1).T, (2, 1)).astype(f)

    g["cos"] = np.concatenate([table(np.cos(freqs) * scale), table(np.cos(freqs) / scale)], 1)
    g["sin"] = np.concatenate([table(np.sin(freqs) * scale), table(np.sin(freqs) / scale)], 1)
    p, c = np.arange(128)[:, None], np.arange(320)[None, :]
    d = np.where(c < 128, p - c, 64 + p - (c - 128))
    band_qk = np.where((d >= 0) & (d <= 64), 0, NEG)
    d = np.where(c < 192, c - p, c - 192 - p)
    band_kq = np.where((d >= 0) & (d <= 64), 0, NEG)
    for n, m in (("band_qk", band_qk), ("band_kq", band_kq)):
        g[n] = bf16_pairs(m)
    return g


FEATURES = 64
RF_EPS = 1e-6


def random_feature_stage(k, name, z, w, out):
    nc = k.nc
    wide = HEADS * FEATURES
    trips = BATCH + 1
    pe_s = Steps(k, "products", ["q", "k", "t0", "v", "t1", "h2", "lk0", "lk1", "n", "mt", "z", "mb", "lq0", "o", "lq1",
                                 "turn"], trips)
    act_s = Steps(k, "lookups", ["eq0", "copy", "q", "k", "k2", "eq1", "t0", "t1", "v", "ek0", "ek1", "out"], trips)
    dve_s = Steps(k, "vectors", ["h2", "mk0", "mk1", "mks", "mk", "nn", "m1", "diag", "eps", "m", "sk0", "sk1", "mq0",
                                 "sq0", "recip", "ctx", "mq1", "sq1"], trips)
    k.arena.reset()
    take = k.arena.take
    zt, qf, kf, k2 = take(SEQ), take(SEQ), take(SEQ), take(SEQ)
    v = take(2 * HEADS * VCOLS).rearrange("p (c h d) -> p c h d", c=2, h=HEADS)
    ak = [take(wide) for _ in range(2)]
    pq = [take(wide) for _ in range(2)]
    pT = [take(wide) for _ in range(2)]
    mk = take(2 * HEADS).rearrange("p (c h) -> p c h", c=2)
    mq = take(2 * HEADS).rearrange("p (c h) -> p c h", c=2)
    h2 = take(2 * HEADS).rearrange("p (c h) -> p c h", c=2)
    m = take(2 * HEADS).rearrange("p (c h) -> p c h", c=2)
    mkb, m1, diag = take(HEADS), take(1), take(HEADS)
    nn = take(8 * 18).rearrange("p (a c) -> p a c", a=8)
    recip = take(2 * HEADS).rearrange("p (c h) -> p c h", c=2)
    ctx = take(SEQ).rearrange("p (c f) -> p c f", c=2)
    bank = [k.psum[:, n, :] for n in range(8)]
    nbank = bank[6][:, 0:144].rearrange("p (a c) -> p a c", a=8)
    zbank = bank[6][:, 144:160]
    hbank = bank[7][:, 288:320].rearrange("p (c h) -> p c h", c=2)
    obank = bank[7][:, 0:288].rearrange("p (c h d) -> p c h d", c=2, h=HEADS)
    sums = nn.rearrange("p a (b c) -> p (a b) c", b=2)[:, :, HEAD_DIM]

    def logits(c):
        return k.psum[:, 2 + 2 * c:4 + 2 * c, :]

    def by_head(ap):
        return ap.rearrange("p (h f) -> p h f", f=FEATURES)

    def logits_by_head(c):
        return logits(c).rearrange("p a (h f) -> p (a h) f", f=FEATURES)

    def spread(ap):
        return ap.unsqueeze(2).to_broadcast([128, HEADS, FEATURES])

    fills = [(v.rearrange("p c h d -> p (c h d)"), 1.0)] + [(buf, 1.0) for buf in ak + pq]
    filled = Count(k, "filled", len(fills))
    with nc.Block() as block:
        @block.vector
        def _(dve):
            for buf, value in fills:
                dve.memset(buf, value).then_inc(filled.sem, 1)
            dve.wait_ge(filled.sem, filled.at(len(fills)))

    with nc.Block() as block:
        @block.tensor
        def _(pe):
            pe_s.prime(pe)

            def feature_logits(x, c):
                for a in range(2):
                    cols = slice(512 * a, 512 * a + 512)
                    last = pe.matmul(logits(c)[:, a, :], x[:, c * 128:(c + 1) * 128], w["wrf"][:, cols],
                                     start=True, stop=True)
                last.then_inc(pe_s.sem, 1)

            def turn_features(c):
                for p in range(8):
                    last = pe.transpose(logits(c)[:, p // 4, (p % 4) * 128:(p % 4 + 1) * 128],
                                        pq[c][:, p * 128:(p + 1) * 128], k.c["ident"])
                last.then_inc(pe_s.sem, 1)

            with pe.Fori(0, trips) as i:
                pe.wait_ge(act_s.sem, act_s.before(i, "k2"))
                pe.wait_ge(dve_s.sem, dve_s.before(i, "m"))
                pe.matmul(bank[0][:, 0:SEQ], w["wq"], z[:, tok(i, SEQ)], start=True, stop=True).then_inc(pe_s.sem, 1)
                pe.matmul(bank[0][:, SEQ:2 * SEQ], w["wk"], z[:, tok(i, SEQ)], start=True, stop=True)\
                    .then_inc(pe_s.sem, 1)
                pe.wait_ge(act_s.sem, act_s.at(i, "eq0"))
                turn_features(0)
                pe.wait_ge(act_s.sem, act_s.at(i, "copy"))
                for c in range(2):
                    to = bank[1][:, c * 128:(c + 1) * 128]
                    pe.matmul(to, zt[:, c * 128:(c + 1) * 128], w["wv"], start=True, stop=False)
                    last = pe.matmul(to, k.c["ones"][0:1, :], w["bv"][0:1, :], start=False, stop=True)
                last.then_inc(pe_s.sem, 1)
                pe.wait_ge(act_s.sem, act_s.at(i, "eq1"))
                turn_features(1)
                for c in range(2):
                    last = pe.matmul(hbank[:, c, :], k2[:, c * 128:(c + 1) * 128], w["half_square"],
                                     start=True, stop=True)
                last.then_inc(pe_s.sem, 1)
                for c in range(2):
                    pe.wait_ge(act_s.sem, act_s.at(i, f"t{c}"))
                    feature_logits(kf, c)
                    pe.wait_ge(act_s.sem, act_s.before(i, "ek1"))
                    for p in range(4 * c, 4 * c + 4):
                        for c2 in range(2):
                            last = pe.matmul(nbank[:, p, :], ak[c2][:, p * 128:(p + 1) * 128],
                                             v[:, c2, 2 * p:2 * p + 2, :].rearrange("p h d -> p (h d)"),
                                             start=(c2 == 0), stop=(c2 == 1))
                last.then_inc(pe_s.sem, 1)
                pe.wait_ge(dve_s.sem, dve_s.at(i, "mk"))
                pe.transpose(bank[0][0:HEADS, 0:128], mkb, k.c["ident"]).then_inc(pe_s.sem, 1)
                pe.wait_ge(dve_s.sem, dve_s.at(i, "nn"))
                pe.matmul(zbank, w["eps_sum"], sums, start=True, stop=True).then_inc(pe_s.sem, 1)
                pe.wait_ge(dve_s.sem, dve_s.at(i, "diag"))
                pe.matmul(bank[0][:, 128:144], k.c["ones"][0:HEADS, :], diag[0:HEADS, :], start=True, stop=True)\
                    .then_inc(pe_s.sem, 1)
                pe.wait_ge(dve_s.sem, dve_s.at(i, "eps"))
                for c in range(2):
                    for p in range(8):
                        last = pe.matmul(obank[:, c, 2 * p:2 * p + 2, :].rearrange("p h d -> p (h d)"),
                                         pT[c][:, p * 128:(p + 1) * 128], nn[:, p, :], start=True, stop=True)
                    if c == 1:
                        last.then_inc(pe_s.sem, 1)
                    pe.wait_ge(dve_s.sem, dve_s.at(i, f"sk{c}"))
                    feature_logits(qf, c)
                pe.wait_ge(dve_s.sem, dve_s.at(i, "ctx"))
                pe.wait_ge(act_s.sem, act_s.at(i, "v"))
                for c in range(2):
                    last = pe.transpose(bank[1][:, SEQ + c * 128:SEQ + (c + 1) * 128], ctx[:, c, :], k.c["ident"])
                last.then_inc(pe_s.sem, 1)

        @block.scalar
        def _(act):
            act_s.prime(act)
            act.preload_act_table_set(EXP_LN)

            def query_features(i, c):
                act.wait_ge(dve_s.sem, dve_s.before(i, f"sq{c}"))
                act.activation(pq[c], pq[c], ACT.Exp).then_inc(act_s.sem, 1)

            with act.Fori(0, trips) as i:
                query_features(i, 0)
                act.wait_ge(pe_s.sem, pe_s.before(i, "v"))
                act.copy(zt, z[:, tok(i, SEQ)]).then_inc(act_s.sem, 1)
                act.wait_ge(pe_s.sem, pe_s.at(i, "k"))
                act.wait_ge(pe_s.sem, pe_s.before(i, "lq1"))
                act.activation(qf, bank[0][:, 0:SEQ], ACT.Identity, bias=w["bq"]).then_inc(act_s.sem, 1)
                act.activation(kf, bank[0][:, SEQ:2 * SEQ], ACT.Identity, bias=w["bk"]).then_inc(act_s.sem, 1)
                act.activation(k2, bank[0][:, SEQ:2 * SEQ], ACT.Square, bias=w["bk"]).then_inc(act_s.sem, 1)
                query_features(i, 1)
                for c in range(2):
                    act.wait_ge(pe_s.sem, pe_s.at(i, f"t{c}"))
                    act.wait_ge(pe_s.sem, pe_s.before(i, "o"))
                    act.copy(pT[c].rearrange("p (a t) -> p a t", a=2), logits(c)).then_inc(act_s.sem, 1)
                act.wait_ge(pe_s.sem, pe_s.at(i, "v"))
                act.wait_ge(pe_s.sem, pe_s.at(i, "n"))
                act.copy(v[:, :, :, 0:HEAD_DIM],
                         bank[1][:, 0:SEQ].rearrange("p (c h d) -> p c h d", c=2, d=HEAD_DIM)).then_inc(act_s.sem, 1)
                for c in range(2):
                    act.wait_ge(dve_s.sem, dve_s.at(i, f"sk{c}"))
                    act.activation(ak[c], ak[c], ACT.Exp).then_inc(act_s.sem, 1)
                act.wait_ge(pe_s.sem, pe_s.at(i, "turn"))
                act.copy(out[:, tok(i, SEQ)], bank[1][:, SEQ:2 * SEQ]).then_inc(act_s.sem, 1)

        @block.vector
        def _(dve):
            dve_s.prime(dve)

            def shift_queries(i, c):
                dve.wait_ge(pe_s.sem, pe_s.at(i, f"lq{c}"))
                dve.tensor_reduce(mq[:, c, :], logits_by_head(c), AX_X, ALU.max).then_inc(dve_s.sem, 1)
                dve.wait_ge(dve_s.sem, dve_s.at(i, f"mq{c}"))
                dve.tensor_tensor(by_head(pq[c]), logits_by_head(c), spread(mq[:, c, :]), ALU.subtract)\
                    .then_inc(dve_s.sem, 1)

            with dve.Fori(0, trips) as i:
                dve.wait_ge(pe_s.sem, pe_s.at(i, "h2"))
                dve.tensor_copy(h2, hbank).then_inc(dve_s.sem, 1)
                for c in range(2):
                    dve.wait_ge(pe_s.sem, pe_s.at(i, f"lk{c}"))
                    dve.tensor_reduce(mk[:, c, :], logits_by_head(c), AX_X, ALU.max).then_inc(dve_s.sem, 1)
                dve.wait_ge(dve_s.sem, dve_s.at(i, "mk1"))
                dve.tensor_tensor(mk, mk, h2, ALU.add).then_inc(dve_s.sem, 1)
                dve.wait_ge(dve_s.sem, dve_s.at(i, "mks"))
                dve.tensor_tensor(mkb, mk[:, 0, :], mk[:, 1, :], ALU.max).then_inc(dve_s.sem, 1)
                dve.wait_ge(pe_s.sem, pe_s.at(i, "n"))
                dve.tensor_tensor(nn, nbank, w["own_head"].unsqueeze(1).to_broadcast([128, 8, 18]), ALU.mult)\
                    .then_inc(dve_s.sem, 1)
                dve.wait_ge(pe_s.sem, pe_s.at(i, "mt"))
                dve.tensor_reduce(m1[0:HEADS, :], bank[0][0:HEADS, 0:128], AX_X, ALU.max).then_inc(dve_s.sem, 1)
                dve.wait_ge(dve_s.sem, dve_s.at(i, "m1"))
                dve.tensor_scalar(diag[0:HEADS, :], k.c["ident"][0:HEADS, 0:HEADS], m1[0:HEADS, :], None, ALU.mult)\
                    .then_inc(dve_s.sem, 1)
                dve.wait_ge(pe_s.sem, pe_s.at(i, "z"))
                dve.tensor_tensor(sums, zbank, sums, ALU.add).then_inc(dve_s.sem, 1)
                dve.wait_ge(pe_s.sem, pe_s.at(i, "mb"))
                dve.tensor_tensor(m, bank[0][:, 128:144].unsqueeze(1).to_broadcast([128, 2, HEADS]), h2,
                                  ALU.subtract).then_inc(dve_s.sem, 1)
                dve.wait_ge(dve_s.sem, dve_s.at(i, "m"))
                for c in range(2):
                    dve.tensor_tensor(by_head(ak[c]), logits_by_head(c), spread(m[:, c, :]), ALU.subtract)\
                        .then_inc(dve_s.sem, 1)
                shift_queries(i, 0)
                dve.wait_ge(pe_s.sem, pe_s.at(i, "o"))
                dve.reciprocal(recip, obank[:, :, :, HEAD_DIM]).then_inc(dve_s.sem, 1)
                dve.wait_ge(dve_s.sem, dve_s.at(i, "recip"))
                dve.wait_ge(pe_s.sem, pe_s.before(i, "turn"))
                for c in range(2):
                    last = dve.tensor_tensor(ctx[:, c, :].rearrange("p (h d) -> p h d", d=HEAD_DIM),
                                             obank[:, c, :, 0:HEAD_DIM],
                                             recip[:, c, :].unsqueeze(2).to_broadcast([128, HEADS, HEAD_DIM]),
                                             ALU.mult)
                last.then_inc(dve_s.sem, 1)
                shift_queries(i, 1)


def l1_attn_b(k, name, w):
    norm_stage(k, f"{name}_ln", k.X, [(k.H, None, None)], True, "eps5")
    zero_stage(k, f"{name}_pad", [(k.H[:, TOKENS:TOKENS + SEQ], 0.0)])
    random_feature_stage(k, name, k.H, w, k.Y_padded)
    output_stage(k, f"{name}_out", [(w["wo"], k.Y, 0)], k.X, k.X, bias=w["bo"])


def l1_attn_b_group(i):
    A, f = "L1_attn_b_", np.float32
    wrf = np.zeros((HEADS, HEAD_DIM, HEADS, FEATURES), f)
    for h in range(HEADS):
        wrf[h, :, h] = i[A + "Wrf"][0, h]
    feature, head = np.arange(128)[:, None], np.arange(HEADS)[None, :]
    half = np.arange(128) // 64
    return {"wq": i[A + "Wq"].T, "wk": i[A + "Wk"].T, "wv": i[A + "Wv"].T, "wo": i[A + "Wo"].T,
            "bq": column(i[A + "bq"]), "bk": column(i[A + "bk"]), "bv": i[A + "bv"].reshape(1, -1),
            "bo": column(i[A + "bo"]), "wrf": wrf.reshape(128, -1),
            "half_square": np.where(feature // HEAD_DIM == head, -0.5, 0).astype(f),
            "eps_sum": np.where(half[:, None] == half[None, :], RF_EPS, 0).astype(f),
            "own_head": (half[:, None] == np.arange(18)[None, :] // VCOLS).astype(f)}


QUARTER = 4 * SEQ
QUARTERS = TOKENS // QUARTER
STATE = 128


def ssm_gates_stage(k, name, xn, w, B, C, U):
    nc = k.nc
    pe_s = Steps(k, "products", ["sel", "b", "c", "imp", "gate"], TILES)
    act_s = Steps(k, "sigmoids", ["sel", "imp", "gate"], TILES)
    dve_s = Steps(k, "gated", ["x2", "b", "c", "u"], TILES)
    take = k.arena.take
    sel, x2, imp, gate = take(TILE), take(TILE), take(TILE), take(TILE)
    sel_bias = take(1)
    ready = Count(k, "filled", 1)
    bank = [k.psum[:, n, :] for n in range(5)]
    with nc.Block() as block:
        @block.vector
        def _(dve):
            dve.tensor_tensor(sel_bias, w["bsel"], w["sel_gate"], ALU.mult).then_inc(ready.sem, 1)
            dve.wait_ge(ready.sem, ready.at(1))

    with nc.Block() as block:
        @block.tensor
        def _(pe):
            pe_s.prime(pe)
            with pe.Fori(0, TILES) as i:
                x = xn[:, tok(i, TILE)]
                pe.wait_ge(act_s.sem, act_s.before(i, "sel"))
                pe.matmul(bank[0], w["wsel"], x, start=True, stop=True).then_inc(pe_s.sem, 1)
                pe.wait_ge(dve_s.sem, dve_s.before(i, "c"))
                pe.matmul(bank[1], w["wx"][:, 64:192], x, start=True, stop=True).then_inc(pe_s.sem, 1)
                pe.matmul(bank[2], w["wx"][:, 192:320], x, start=True, stop=True).then_inc(pe_s.sem, 1)
                pe.wait_ge(dve_s.sem, dve_s.at(i, "x2"))
                pe.wait_ge(act_s.sem, act_s.before(i, "gate"))
                pe.matmul(bank[3], w["wimp"], x2, start=True, stop=True).then_inc(pe_s.sem, 1)
                pe.matmul(bank[4], w["wg"], x2, start=True, stop=True).then_inc(pe_s.sem, 1)

        @block.scalar
        def _(act):
            act_s.prime(act)
            act.preload_act_table_set(SIGMOID_SET)
            with act.Fori(0, TILES) as i:
                act.wait_ge(pe_s.sem, pe_s.at(i, "sel"))
                act.wait_ge(dve_s.sem, dve_s.before(i, "x2"))
                act.activation(sel, bank[0], ACT.Sigmoid, scale=w["sel_gate"], bias=sel_bias).then_inc(act_s.sem, 1)
                act.wait_ge(pe_s.sem, pe_s.at(i, "imp"))
                act.wait_ge(dve_s.sem, dve_s.before(i, "c"))
                act.activation(imp, bank[3], ACT.Sigmoid, bias=w["bimp"]).then_inc(act_s.sem, 1)
                act.wait_ge(pe_s.sem, pe_s.at(i, "gate"))
                act.wait_ge(dve_s.sem, dve_s.before(i, "u"))
                act.activation(gate, bank[4], ACT.Sigmoid, bias=w["bg"]).then_inc(act_s.sem, 1)

        @block.vector
        def _(dve):
            dve_s.prime(dve)
            with dve.Fori(0, TILES) as i:
                dve.wait_ge(act_s.sem, act_s.at(i, "sel"))
                dve.wait_ge(pe_s.sem, pe_s.before(i, "gate"))
                dve.wait_ge(dve_s.sem, dve_s.before(i, "u"))
                dve.tensor_tensor(x2, xn[:, tok(i, TILE)], sel, ALU.mult).then_inc(dve_s.sem, 1)
                dve.wait_ge(act_s.sem, act_s.at(i, "imp"))
                dve.wait_ge(pe_s.sem, pe_s.at(i, "c"))
                dve.tensor_tensor(B[:, tok(i, TILE)], bank[1], imp, ALU.mult).then_inc(dve_s.sem, 1)
                dve.tensor_tensor(C[:, tok(i, TILE)], bank[2], imp, ALU.mult).then_inc(dve_s.sem, 1)
                dve.wait_ge(act_s.sem, act_s.at(i, "gate"))
                dve.wait_ge(dve_s.sem, dve_s.at(i, "x2"))
                dve.tensor_tensor(U[:, tok(i, TILE)], x2, gate, ALU.mult).then_inc(dve_s.sem, 1)


def ssm_delta_stage(k, name, xn, w, U):
    nc = k.nc
    pe_s = Steps(k, "products", ["dr", "dl"], TILES)
    act_s = Steps(k, "lookups", ["dr", "abs", "exp", "ln"], TILES)
    dve_s = Steps(k, "delta", ["max", "delta", "u"], TILES)
    at = k.arena.used
    take = k.arena.take
    dr, small, pos = take(TILE), take(TILE), take(TILE)
    with nc.Block() as block:
        @block.tensor
        def _(pe):
            pe_s.prime(pe)
            with pe.Fori(0, TILES) as i:
                pe.wait_ge(act_s.sem, act_s.before(i, "dr"))
                pe.matmul(k.psum[0:64, 0, :], w["wx"][:, 0:64], xn[:, tok(i, TILE)], start=True, stop=True)\
                    .then_inc(pe_s.sem, 1)
                pe.wait_ge(act_s.sem, act_s.at(i, "dr"))
                pe.wait_ge(dve_s.sem, dve_s.before(i, "max"))
                pe.matmul(k.psum[:, 1, :], w["wdt"][0:64, :], dr[0:64, :], start=True, stop=True)\
                    .then_inc(pe_s.sem, 1)

        @block.scalar
        def _(act):
            act_s.prime(act)
            act.preload_act_table_set(EXP_LN)
            with act.Fori(0, TILES) as i:
                act.wait_ge(pe_s.sem, pe_s.at(i, "dr"))
                act.copy(dr[0:64, :], k.psum[0:64, 0, :]).then_inc(act_s.sem, 1)
                act.wait_ge(pe_s.sem, pe_s.at(i, "dl"))
                act.wait_ge(dve_s.sem, dve_s.before(i, "delta"))
                act.activation(small, k.psum[:, 1, :], ACT.Abs, bias=w["bdt"]).then_inc(act_s.sem, 1)
                act.wait_ge(act_s.sem, act_s.at(i, "abs"))
                act.activation(small, small, ACT.Exp, scale=-1.0).then_inc(act_s.sem, 1)
                act.wait_ge(act_s.sem, act_s.at(i, "exp"))
                act.activation(small, small, ACT.Ln, bias=1.0).then_inc(act_s.sem, 1)

        @block.vector
        def _(dve):
            dve_s.prime(dve)
            with dve.Fori(0, TILES) as i:
                dve.wait_ge(act_s.sem, act_s.at(i, "abs"))
                dve.wait_ge(dve_s.sem, dve_s.before(i, "delta"))
                dve.tensor_scalar(pos, k.psum[:, 1, :], w["bdt"], 0.0, ALU.add, ALU.max).then_inc(dve_s.sem, 1)
                dve.wait_ge(act_s.sem, act_s.at(i, "ln"))
                dve.wait_ge(dve_s.sem, dve_s.at(i, "max"))
                dve.tensor_tensor(xn[:, tok(i, TILE)], pos, small, ALU.add).then_inc(dve_s.sem, 1)
                dve.wait_ge(dve_s.sem, dve_s.at(i, "delta"))
                dve.tensor_tensor(U[:, tok(i, TILE)], U[:, tok(i, TILE)], xn[:, tok(i, TILE)], ALU.mult)\
                    .then_inc(dve_s.sem, 1)
    k.arena.used = at


def scan_stage(k, name, xh, w, cst, delta, B, C, U, big):
    nc = k.nc
    pe_in = Steps(k, "spread", [f"{s}{u}" for u in (0, 1) for s in ("bd", "bu", "y")], 64 * QUARTERS)
    act_in = Steps(k, "decays", ["da0", "da1", "e0", "e1"], 64 * QUARTERS)
    dve_in = Steps(k, "scans", [f"{s}{u}" for u in (0, 1) for s in ("bx", "h")], 64 * QUARTERS)
    pool_in = Steps(k, "read_out", ["hc0", "hc1"], 64 * QUARTERS)
    splits = [f"{s}{n}" for s in ("d", "u") for n in ("t1", "r1", "t2", "r2", "t3", "s")]
    pe_q = Steps(k, "quarter_sums", ["init", "last"], QUARTERS)
    act_q = Steps(k, "quarter_taken", ["c", "y"], QUARTERS)
    dve_q = Steps(k, "quarter_split", splits, QUARTERS)
    pool_q = Steps(k, "quarter_zero", ["zero"], QUARTERS)
    take = k.arena.take
    DS = k.arena.take_bf16(4 * QUARTER)
    US = k.arena.take_bf16(4 * QUARTER)
    da = [take(QUARTER) for _ in range(2)]
    bx = [big.take(QUARTER) for _ in range(2)]
    hc = [big.take(QUARTER) for _ in range(2)]
    cq = big.take(QUARTER)
    onehot = [big.take(128) for _ in range(2)]
    diag, neg_a = big.take(128), big.take(128)
    zero_column = big.take(1)
    nothing = zero_column.to_broadcast([128, QUARTER])
    rest, low = bx[0], bx[1][:, 0:QUARTER // 2].bitcast(BF16)
    pick = cst["pick"].bitcast(BF16)
    delta_bank = [k.psum[:, 0:2, :], k.psum[:, 6:8, :]]
    u_bank, y_bank = k.psum[:, 2:4, :], k.psum[:, 4:6, :]
    prep = Count(k, "prepared", 2)
    with nc.Block() as block:
        @block.scalar
        def _(act):
            act.preload_act_table_set(EXP_LN)
            act.activation(neg_a, w["a_log"], ACT.Exp).then_inc(prep.sem, 1)

        @block.vector
        def _(dve):
            dve.tensor_scalar(diag, k.c["ident"], w["dp"], None, ALU.mult)
            dve.memset(zero_column, 0.0)
            for u in range(2):
                dve.memset(da[u], 0.0)
                dve.memset(onehot[u], 0.0)
            dve.wait_ge(prep.sem, prep.at(1))
            dve.tensor_scalar(neg_a, neg_a, -1.0, None, ALU.mult).then_inc(prep.sem, 1)
            dve.wait_ge(prep.sem, prep.at(2))

    with nc.Block() as block:
        @block.tensor
        def _(pe):
            for s in (pe_in, pe_q):
                s.prime(pe)
            with pe.Fori(0, QUARTERS) as q:
                pe.wait_ge(act_q.sem, act_q.before(q, "y"))
                pe.wait_ge(dve_q.sem, dve_q.at(q, "us"))
                pe.wait_ge(pool_q.sem, pool_q.at(q, "zero"))
                for h in range(2):
                    last = pe.matmul(y_bank[:, h, :], diag, xh[:, bass.ds(q * QUARTER + h * TILE, TILE)],
                                     start=True, stop=True)
                last.then_inc(pe_q.sem, 1)

                def spread(bank, src, u, g, j):
                    for h in range(2):
                        last = pe.matmul(bank[:, h, :], pick[0:96, bass.ds(j * 256 + u * 128, 128)],
                                         src[0:96, bass.ds(g * QUARTER + h * TILE, TILE)], start=True, stop=True)
                    last.then_inc(pe_in.sem, 1)

                def read_out(u):
                    for h in range(2):
                        last = pe.matmul(y_bank[:, h, :], onehot[u], hc[u][:, h * TILE:(h + 1) * TILE],
                                         start=False, stop=True, skip_group_check=True)
                    return last

                with pe.Fori(0, 4) as g:
                    with pe.Fori(0, 16) as j:
                        t = q * 64 + g * 16 + j
                        for u in range(2):
                            pe.wait_ge(act_in.sem, act_in.before(t, f"da{u}"))
                            spread(delta_bank[u], DS, u, g, j)
                            pe.wait_ge(dve_in.sem, dve_in.at(t, "bx0") if u else dve_in.before(t, "bx1"))
                            spread(u_bank, US, u, g, j)
                            pe.wait_ge(pool_in.sem, pool_in.before(t, f"hc{u}"))
                            pe.wait_ge(act_in.sem, act_in.before(t, f"e{u}"))
                            read_out(u).then_inc(pe_in.sem, 1)
                pe.wait_ge(pool_in.sem, pool_in.before(q * 64 + 64, "hc1"))
                pe.wait_ge(act_in.sem, act_in.before(q * 64 + 64, "e1"))
                read_out(0)
                read_out(1).then_inc(pe_q.sem, 1)

        @block.scalar
        def _(act):
            for s in (act_in, act_q):
                s.prime(act)
            act.preload_act_table_set(EXP_LN)
            with act.Fori(0, QUARTERS) as q:
                act.wait_ge(pool_in.sem, pool_in.before(q * 64, "hc1"))
                act.copy(cq, C[:, bass.ds(q * QUARTER, QUARTER)]).then_inc(act_q.sem, 1)
                with act.Fori(0, 4) as g:
                    with act.Fori(0, 16) as j:
                        t = q * 64 + g * 16 + j
                        for u in range(2):
                            act.wait_ge(pe_in.sem, pe_in.at(t, f"bd{u}"))
                            act.wait_ge(dve_in.sem, dve_in.before(t, f"h{u}"))
                            act.activation(da[u].rearrange("p (b t) -> p b t", t=SEQ)[:, :, 1:SEQ],
                                           delta_bank[u].rearrange("p h (b t) -> p (h b) t", t=SEQ)[:, :, 1:SEQ],
                                           ACT.Exp, scale=neg_a[:, bass.ds(g * 32 + j * 2 + u, 1)])\
                                .then_inc(act_in.sem, 1)
                        for u in range(2):
                            act.wait_ge(pe_in.sem, pe_in.at(t, f"y{u}"))
                            act.copy(onehot[u], cst["slide"][:, bass.ds(g * -32 + j * -2 + (127 - u), 128)])\
                                .then_inc(act_in.sem, 1)
                act.wait_ge(pe_q.sem, pe_q.at(q, "last"))
                act.copy(U[:, bass.ds(q * QUARTER, QUARTER)].rearrange("p (h t) -> p h t", h=2), y_bank)\
                    .then_inc(act_q.sem, 1)

        @block.vector
        def _(dve):
            for s in (dve_in, dve_q):
                s.prime(dve)
            with dve.Fori(0, QUARTERS) as q:
                dve.wait_ge(pool_in.sem, pool_in.before(q * 64, "hc1"))
                dve.wait_ge(pe_in.sem, pe_in.before(q * 64, "bu1"))
                for s, src, dst in (("d", delta, DS), ("u", U, US)):
                    value = src[:, bass.ds(q * QUARTER, QUARTER)]
                    for n in (1, 2, 3):
                        dve.tensor_copy(low, value).then_inc(dve_q.sem, 1)
                        dve.wait_ge(dve_q.sem, dve_q.at(q, f"{s}t{n}"))
                        for g in range(4):
                            last = dve.tensor_copy(dst[32 * (n - 1):32 * n, g * QUARTER:(g + 1) * QUARTER],
                                                   low[32 * g:32 * g + 32, :])
                        if n < 3:
                            dve.tensor_tensor(rest, value, low, ALU.subtract).then_inc(dve_q.sem, 1)
                            dve.wait_ge(dve_q.sem, dve_q.at(q, f"{s}r{n}"))
                            value = rest
                        else:
                            last.then_inc(dve_q.sem, 1)
                            if s == "d":
                                dve.wait_ge(dve_q.sem, dve_q.at(q, "ds"))
                with dve.Fori(0, 4) as g:
                    with dve.Fori(0, 16) as j:
                        t = q * 64 + g * 16 + j
                        for u in range(2):
                            dve.wait_ge(pe_in.sem, pe_in.at(t, f"bu{u}"))
                            dve.wait_ge(pool_in.sem, pool_in.before(t, f"hc{u}"))
                            dve.tensor_tensor(bx[u].rearrange("p (h t) -> p h t", h=2),
                                              u_bank, B[:, bass.ds(q * QUARTER, QUARTER)]
                                              .rearrange("p (h t) -> p h t", h=2), ALU.mult).then_inc(dve_in.sem, 1)
                            dve.wait_ge(dve_in.sem, dve_in.at(t, f"bx{u}"))
                            dve.wait_ge(act_in.sem, act_in.at(t, f"da{u}"))
                            dve.tensor_tensor_scan(bx[u], da[u], bx[u], 0.0, ALU.mult, ALU.add)\
                                .then_inc(dve_in.sem, 1)

        @block.gpsimd
        def _(pool):
            for s in (pool_in, pool_q):
                s.prime(pool)
            with pool.Fori(0, QUARTERS) as q:
                pool.wait_ge(pe_q.sem, pe_q.before(q, "last"))
                pool.wait_ge(act_q.sem, act_q.at(q, "c"))
                for u in range(2):
                    last = pool.tensor_tensor(hc[u], nothing, nothing, ALU.mult)
                last.then_inc(pool_q.sem, 1)
                with pool.Fori(0, 64) as j:
                    t = q * 64 + j
                    for u in range(2):
                        pool.wait_ge(pe_in.sem, pe_in.at(t, f"y{u}"))
                        pool.wait_ge(dve_in.sem, dve_in.at(t, f"h{u}"))
                        pool.tensor_tensor(hc[u], bx[u], cq, ALU.mult).then_inc(pool_in.sem, 1)


def l0_attn_a(k, name, w, big):
    norm_stage(k, f"{name}_ln", k.X, [(k.Z, None, None)], True, "eps5")
    norm_stage(k, f"{name}_rms1", k.Z, [(k.H, w["norm_attn"], None)], False, "eps6")
    softmax_attention(k, f"{name}_attn", k.H, w["wq"], w["wk"], w["wv"], False, qn=w["qn"], kn=w["kn"],
                      rope=(k.c["rot_halves"], k.c["cos_halves"], k.c["sin_halves"]), eps="eps6")
    output_stage(k, f"{name}_o", [(w["wo"], k.H, SEQ)], k.Z, k.Y, factor=0.5)
    norm_stage(k, f"{name}_rms2", k.Z, [(k.H, w["norm_ssm"], None)], False, "eps6")
    k.arena.reset()
    B, C, U = (k.arena.take(TOKENS) for _ in range(3))
    kept = k.arena.used
    ssm_gates_stage(k, f"{name}_gates", k.H, w, B, C, U)
    k.arena.used = kept
    ssm_delta_stage(k, f"{name}_delta", k.H, w, U)
    region = Region(k.wbig, WBIG)
    cst = big("ssm_scan")
    region.take(sum(n for _, n in k.layouts["ssm_scan"].values()))
    scan_stage(k, f"{name}_scan", k.Z, w, cst, k.H, B, C, U, region)
    output_stage(k, f"{name}_so", [(w["wout"], U, 0)], k.Y, k.Y, factor=0.5)
    norm_stage(k, f"{name}_rms3", k.Y, [(k.H, w["norm_ffn"], None)], False, "eps6")
    gated_mlp_stage(k, f"{name}_mlp", k.H, [128] * 4, w["w_lin"], w["w_act"], None, None, w["w_out"], ACT.Silu,
                    SILU_SET, k.Y, k.Y, None)
    add_stage(k, f"{name}_add", k.Y, k.X)


def l0_attn_a_groups(i):
    A, f = "L0_attn_a_", np.float32
    heads = np.repeat(np.arange(4), 4)

    def repeated(m):
        return m.reshape(128, 4, 8)[:, heads].reshape(128, 128)

    w1 = i[A + "W1"]
    g = {"wq": i[A + "Wq"], "wk": repeated(i[A + "Wk"]), "wv": repeated(i[A + "Wv"]), "wo": i[A + "Wo"],
         "wx": i[A + "Wx"], "wdt": i[A + "Wdt"], "a_log": i[A + "A_log"].T, "wsel": i[A + "Wsel"],
         "wimp": i[A + "Wimp"], "wg": i[A + "Wg"], "wout": i[A + "Wout"], "w_act": w1[:, 0:512],
         "w_lin": w1[:, 512:], "w_out": i[A + "W2"].reshape(4, 128, 128).transpose(1, 0, 2)}
    for n, name in (("norm_attn", "norm_attn_w"), ("norm_ssm", "ssm_norm_w"), ("norm_ffn", "norm_ffn_w"),
                    ("bdt", "bdt"), ("dp", "Dp"), ("bsel", "bsel"), ("sel_gate", "sel_gate"), ("bimp", "bimp"),
                    ("bg", "bg")):
        g[n] = column(i[A + name])
    g["qn"], g["kn"] = column(np.tile(i[A + "qn_w"], 16)), column(np.tile(i[A + "kn_w"], 16))
    pick = np.zeros((128, 32, 128), f)
    for d in range(32):
        for part in range(3):
            pick[32 * part + d, d] = 1
    slide = np.zeros((128, 255), f)
    slide[:, 127] = 1
    scan = {"pick": bf16_pairs(pick.reshape(128, -1)), "slide": slide}
    return g, scan
def zero_stage(k, name, fills):
    filled = Count(k, "filled", len(fills))
    with k.nc.Block() as block:
        @block.vector
        def _(dve):
            for ap, value in fills:
                dve.memset(ap, value).then_inc(filled.sem, 1)
            dve.wait_ge(filled.sem, filled.at(len(fills)))


def views(tensor, layout):
    return {name: tensor[:, at:at + n] for name, (at, n) in layout.items()}


def attention_buffers(k):
    k.arena.reset()
    q = k.arena.take((BATCH + 2) * SEQ)
    kk = k.arena.take((BATCH + 2) * SEQ)
    v = k.arena.take((2 * BATCH + 2) * HEADS * VCOLS).rearrange("p (t c) -> p t c", c=HEADS * VCOLS)
    k.arena_kept = k.arena.used
    last = (BATCH + 1) * SEQ
    fills = [(q[:, 0:SEQ], 0.0), (q[:, last:last + SEQ], 0.0), (kk[:, 0:SEQ], 0.0), (kk[:, last:last + SEQ], 0.0),
             (v.rearrange("p t c -> p (t c)"), 1.0)]
    return q, kk, v, fills


def softmax_attention(k, name, src, wq, wk, wv, causal, bv=None, **project):
    q, kk, v, fills = attention_buffers(k)
    zero_stage(k, f"{name}_pad", fills)
    project_stage(k, f"{name}_qkv", src, wq, wk, wv, q, kk, v, **project)
    attention_stage(k, name, q, kk, v, k.H, causal, HEAD_DIM ** -0.5, bv=bv)


def network(nc, stages, arrays, layouts, out):
    with ExitStack() as ctx:
        k = Core(nc, ctx)
        k.X = k.sb("X", [128, TOKENS])
        k.Z = k.sb("Z", [128, TOKENS])
        k.Y_padded = k.sb("Y", [128, SEQ + TOKENS])
        k.Y = k.Y_padded[:, SEQ:SEQ + TOKENS]
        k.H = k.sb("H", [128, TOKENS + SEQ])
        k.arena = Region(k.sb("arena", [128, ARENA]), ARENA)
        k.wbig = k.sb("wbig", [128, WBIG])
        k.wsmall = k.sb("wsmall", [128, WSMALL])
        cst = k.sb("cst", [128, arrays["constants"].shape[1]])
        cstb = k.sb("cstb", [128, arrays["constants_bf16"].shape[1]])
        k.shift = k.sb("shift", [128, SEQ], BF16)
        k.psum = ctx.enter_context(nc.psum_tensor("banks", [128, 8, 512], F32))
        k.c = views(cst, layouts["constants"])
        cb = {n: a.bitcast(BF16) for n, a in views(cstb, layouts["constants_bf16"]).items()}
        cb["pick_head"] = cb["pick_head"].rearrange("p (h m) -> p h m", h=HEADS)
        k.cb = cb

        def small(which):
            n = arrays[which].shape[1]
            copy_dram_stage(k, f"load_{which}", [(k.wsmall[:, 0:n], arrays[which])])
            return views(k.wsmall, layouts[which])

        def big(which):
            n = arrays[which].shape[1]
            copy_dram_stage(k, f"load_{which}", [(k.wbig[:, 0:n], arrays[which])])
            return views(k.wbig, layouts[which])

        copy_dram_stage(k, "load", [(k.X[:, :], arrays["x"]), (cst[:, :], arrays["constants"]),
                                    (cstb[:, :], arrays["constants_bf16"])])
        zero_stage(k, "shift", [(k.shift[:, :], 0.0)])
        k.big_holds = None
        k.layouts = layouts
        for n, stage in enumerate(stages):
            run_stage(k, n, stage, small, big)
        copy_dram_stage(k, "store", [(out, k.X[:, :])])


def run_stage(k, n, stage, small, big):
    if stage == "attn_b":
        w = small("attn_b")
        norm_stage(k, f"n{n}a", k.X, [(k.Z, None, None)], True, "eps5")
        norm_stage(k, f"n{n}b", k.Z, [(k.H, w["g"], None)], True, "eps5")
        softmax_attention(k, f"attn{n}", k.H, w["wq"], w["wk"], w["wv"], True)
        output_stage(k, f"o{n}", [(w["wo"], k.H, SEQ)], k.X, k.X)
    elif stage == "l1_attn_a":
        w = small("l1_attn_a")
        norm_stage(k, f"n{n}a", k.X, [(k.H, None, None)], True, "eps5")
        softmax_attention(k, f"attn{n}", k.H, w["wq"], w["wk"], w["wv"], True, bv=w["bv"], bq=w["bq"], bk=w["bk"],
                          rope=(k.c["rot_pairs"], k.c["cos_pairs"], k.c["sin_pairs"]))
        output_stage(k, f"o{n}", [(w["wo"], k.H, SEQ)], k.X, k.X, bias=w["bo"])
    elif stage == "l1_ffn":
        if k.big_holds != "l1_ffn":
            k.big_holds, k.big_w = "l1_ffn", big("l1_ffn")
        l1_ffn(k, f"moe{n}", k.big_w)
    elif stage == "l0_ffn":
        if k.big_holds != "l0_ffn":
            k.big_holds, k.big_w = "l0_ffn", big("l0_ffn")
        l0_ffn(k, f"ffn{n}", k.big_w)
    elif stage == "l1_attn_b":
        l1_attn_b(k, f"rf{n}", small("l1_attn_b"))
    elif stage == "l0_attn_a":
        l0_attn_a(k, f"a{n}", small("l0_attn_a"), big)
    else:
        raise ValueError(stage)


ARENA = 18944
WBIG = 8704
WSMALL = 3200


def constants():
    f = np.float32
    eye = np.eye(128, dtype=f)
    feature = np.arange(128)
    c = {
        "mean": np.full((128, 128), 1.0 / 128, f),
        "center": (eye - 1.0 / 128).astype(f),
        "ident": eye,
        "ones": np.ones((128, 128), f),
        "head_mean": (feature[:, None] // 8 == feature[None, :] // 8).astype(f) / 8,
        "head_mask": (feature[:, None] // 8 == np.arange(16)[None, :]).astype(f),
        "reverse": np.tile(np.arange(8, 0, -1, dtype=f), (128, 1)),
        "eps5": np.full((128, 1), 1e-5, f),
        "eps6": np.full((128, 1), 1e-6, f),
    }

    inv = (1.0 / 10000.0 ** (np.arange(0, 8, 2, dtype=f) / f(8))).astype(f)
    ang = (np.arange(SEQ, dtype=f)[None, :] * inv[:, None]).astype(f)
    halves = np.tile(np.concatenate([ang, ang], 0), (16, 1))
    pairs = np.tile(np.repeat(ang, 2, axis=0), (16, 1))
    c["rot_halves"], c["cos_halves"], c["sin_halves"] = rotation(8, False), np.cos(halves), np.sin(halves)
    c["rot_pairs"], c["cos_pairs"], c["sin_pairs"] = rotation(8, True), np.cos(pairs), np.sin(pairs)
    token = np.arange(128)
    later = token[None, :] > token[:, None]
    b = {"ident": eye, "causal_qk": np.where(later, NEG, 0), "causal_kq": np.where(later.T, NEG, 0)}
    pick = np.zeros((128, 16, 128), f)
    for h in range(16):
        pick[h, h] = 1
    b["pick_head"] = pick.reshape(128, -1)
    b = {name: bf16_pairs(a) for name, a in b.items()}
    return c, b


def rotation(width, pairs):
    f, feature = np.float32, np.arange(128)
    r = np.zeros((128, 128), f)
    for m in feature:
        base, j = m - m % width, m % width
        if pairs:
            r[m, m + 1 if j % 2 == 0 else m - 1] = -1 if j % 2 == 0 else 1
        else:
            half = width // 2
            r[m, m + half if j < half else m - half] = -1 if j < half else 1
    return np.ascontiguousarray(r.T)


def bf16_pairs(a):
    bits = (np.ascontiguousarray(a, np.float32).view(np.uint32) >> 16).astype(np.uint16)
    return bits.view(np.float32)


def packed(parts):
    layout, at, cols = {}, 0, []
    for name, a in parts.items():
        a = a.reshape(a.shape[0], -1)
        if a.shape[0] < 128:
            a = np.concatenate([a, np.zeros((128 - a.shape[0], a.shape[1]), a.dtype)], 0)
        layout[name] = (at, a.shape[1])
        at += a.shape[1]
        cols.append(a)
    return np.ascontiguousarray(np.concatenate(cols, 1)), layout


def column(a):
    return a.reshape(-1, 1)


STAGES = ['l0_attn_a', 'l0_ffn', 'attn_b', 'l0_ffn', 'l1_attn_a', 'l1_ffn', 'l1_attn_b', 'l1_ffn']


def kernel(**inputs):
    import concourse.bacc as _bacc
    from concourse.bass_utils import run_bass_kernel_spmd as _run

    i = {n: np.asarray(a) for n, a in inputs.items()}
    c, b = constants()
    groups = {"constants": c, "constants_bf16": b}
    A = "L0_attn_b_"
    groups["attn_b"] = {"wq": i[A + "Wq"], "wk": i[A + "Wkv"][:, 0:128], "wv": i[A + "Wkv"][:, 128:256],
                        "wo": i[A + "Wo"], "g": column(i[A + "g_ln"])}
    A = "L1_attn_a_"
    w, bb = i[A + "qkv_w"], i[A + "qkv_b"]
    groups["l1_attn_a"] = {"wq": w[0:128].T, "wk": w[128:256].T, "wv": w[256:384].T, "wo": i[A + "proj_w"].T,
                           "bq": column(bb[0:128]), "bk": column(bb[128:256]), "bv": column(bb[256:384]),
                           "bo": column(i[A + "proj_b"])}
    more_groups(groups, i)
    nc = _bacc.Bacc("TRN2", target_bir_lowering=False, num_devices=1)
    sent = {"x": np.ascontiguousarray(i["L0_attn_a_x"].reshape(TOKENS, DIM).T)}
    layouts = {}
    for name, parts in groups.items():
        sent[name], layouts[name] = packed(parts)
    dram = {n: nc.dram_tensor(f"in_{n}", a.shape, mybir.dt.from_np(a.dtype), kind="ExternalInput").ap()
            for n, a in sent.items()}
    out = nc.dram_tensor("out_x", (DIM, TOKENS), F32, kind="ExternalOutput").ap()
    network(nc, STAGES, dram, layouts, out)
    r = _run(nc, [{f"in_{n}": a for n, a in sent.items()}], core_ids=[0])
    return np.ascontiguousarray(r.results[0]["out_x"].T).reshape(BATCH, SEQ, DIM)
```

```python
from contextlib import ExitStack

import numpy as np

import concourse.bass as bass
from concourse import mybir

F32 = mybir.dt.float32
BF16 = mybir.dt.bfloat16
U32 = mybir.dt.uint32
ACT = mybir.ActivationFunctionType
ALU = mybir.AluOpType
AX_X = mybir.AxisListType.X

BATCH, SEQ, DIM = 16, 256, 128
TOKENS = BATCH * SEQ
TILE = 512
TILES = TOKENS // TILE
HEADS, HEAD_DIM = 16, 8
VCOLS = HEAD_DIM + 1
NEG = -1.0e30

EXP_LN = "natural_log_exp_and_others"
GELU_SET = "gelu_and_others"
SILU_SET = "silu_and_others"
SIGMOID_SET = "sigmoid_and_others"


class Steps:

    def __init__(self, k, role, steps, trips):
        self.sem, self.base = k.shared(role, len(steps) * (trips + 1))
        self.place = {s: n for n, s in enumerate(steps)}
        self.count = len(steps)
        assert len(self.place) == self.count

    def at(self, trip, step):
        return trip * self.count + (self.base + self.count + self.place[step] + 1)

    def before(self, trip, step):
        return trip * self.count + (self.base + self.place[step] + 1)

    def skip(self, eng, trip, *steps):
        eng.wait_ge(self.sem, self.at(trip, steps[0]) - 1)
        eng.sem_inc(self.sem, len(steps))

    def prime(self, eng):
        eng.sem_inc(self.sem, self.count)


class Count:

    def __init__(self, k, role, total):
        self.sem, self.base = k.shared(role, total)

    def at(self, n):
        return self.base + n


class Region:

    def __init__(self, tensor, columns):
        self.tensor, self.columns, self.used = tensor, columns, 0

    def reset(self):
        self.used = 0

    def take(self, columns):
        at = self.used
        self.used += columns
        assert self.used <= self.columns, (self.used, self.columns)
        return self.tensor[:, at:at + columns]

    def take_bf16(self, columns):
        return self.take((columns + 1) // 2).bitcast(BF16)


class Core:

    def __init__(self, nc, ctx):
        self.nc, self.ctx = nc, ctx
        self.roles = {}
        self.table = None

    def sb(self, name, shape, dt=F32):
        return self.ctx.enter_context(self.nc.sbuf_tensor(name, shape, dt))

    def sem(self, name):
        return self.ctx.enter_context(self.nc.semaphore(name))

    def load_table(self, act, table):
        if self.table != table:
            act.preload_act_table_set(table)
            self.table = table

    def shared(self, role, total):
        if role not in self.roles:
            self.roles[role] = [self.sem(role), 0]
        sem, base = self.roles[role]
        self.roles[role][1] = base + total
        return sem, base


def tok(i, width, extra=0):
    return bass.ds(i * width + extra, width)


def copy_dram_stage(k, name, pairs):
    landed = [Count(k, f"landed{n}", 16) for n in range(len(pairs))]
    with k.nc.Block() as block:
        @block.sync
        def _(sp):
            for n, (dst, src) in enumerate(pairs):
                sp.dma_start(dst, src).then_inc(landed[n].sem, 16)
            for n in range(len(pairs)):
                sp.wait_ge(landed[n].sem, landed[n].at(16))


def norm_stage(k, name, src, outs, center, eps):
    nc = k.nc
    tiles, ahead, bufs = range(TILES), 3, 4
    pe_order = [("center", t) for t in range(ahead)] if center else []
    act_order = [("sq", t) for t in range(ahead)]
    for t in tiles:
        pe_order += [("var", t)] + ([("center", t + ahead)] if center and t + ahead < TILES else [])
        act_order += [("ln", t), ("exp", t)] + ([("sq", t + ahead)] if t + ahead < TILES else [])
    biased = any(b is not None for _, _, b in outs)
    pe_s = Steps(k, "sums", [f"{s}{t}" for s, t in pe_order], 1)
    act_s = Steps(k, "roots", [f"{s}{t}" for s, t in act_order], 1)
    dve_s = Steps(k, "scaled", [f"{s}{t}" for t in tiles for s in (("z", "b") if biased else ("z",))], 1)
    k.arena.reset()
    sq = [k.arena.take(TILE) for _ in range(bufs)]
    rs = [k.arena.take(TILE) for _ in range(bufs)]
    pre = [k.arena.take(TILE) for _ in range(bufs)]
    cbank = [k.psum[:, u, :] for u in range(bufs)]
    vbank = [k.psum[:, bufs + u, :] for u in range(bufs)]

    def columns(ap, t):
        return ap[:, t * TILE:(t + 1) * TILE]

    with nc.Block() as block:
        @block.tensor
        def _(pe):
            pe_s.prime(pe)
            for what, t in pe_order:
                if what == "center":
                    if t >= bufs:
                        pe.wait_ge(dve_s.sem, dve_s.at(0, f"z{t - bufs}"))
                    pe.matmul(cbank[t % bufs], k.c["center"], columns(src, t), start=True, stop=True)\
                        .then_inc(pe_s.sem, 1)
                else:
                    pe.wait_ge(act_s.sem, act_s.at(0, f"sq{t}"))
                    if t >= bufs:
                        pe.wait_ge(act_s.sem, act_s.at(0, f"ln{t - bufs}"))
                    pe.matmul(vbank[t % bufs], k.c["mean"], sq[t % bufs], start=True, stop=True)\
                        .then_inc(pe_s.sem, 1)

        @block.scalar
        def _(act):
            act_s.prime(act)
            k.load_table(act, EXP_LN)
            for what, t in act_order:
                if what == "sq":
                    if center:
                        act.wait_ge(pe_s.sem, pe_s.at(0, f"center{t}"))
                    if t >= bufs:
                        act.wait_ge(pe_s.sem, pe_s.at(0, f"var{t - bufs}"))
                    act.activation(sq[t % bufs], cbank[t % bufs] if center else columns(src, t), ACT.Square)\
                        .then_inc(act_s.sem, 1)
                elif what == "ln":
                    act.wait_ge(pe_s.sem, pe_s.at(0, f"var{t}"))
                    if t >= bufs:
                        act.wait_ge(dve_s.sem, dve_s.at(0, f"z{t - bufs}"))
                    act.activation(rs[t % bufs], vbank[t % bufs], ACT.Ln, bias=k.c[eps]).then_inc(act_s.sem, 1)
                else:
                    act.wait_ge(act_s.sem, act_s.at(0, f"ln{t}"))
                    act.activation(rs[t % bufs], rs[t % bufs], ACT.Exp, scale=-0.5).then_inc(act_s.sem, 1)

        @block.vector
        def _(dve):
            dve_s.prime(dve)
            for t in tiles:
                dve.wait_ge(act_s.sem, act_s.at(0, f"exp{t}"))
                if biased and t >= bufs:
                    dve.wait_ge(dve_s.sem, dve_s.at(0, f"b{t - bufs}"))
                for dst, w, b in outs:
                    to = pre[t % bufs] if b is not None else columns(dst, t)
                    c = cbank[t % bufs] if center else columns(src, t)
                    if w is None:
                        last = dve.tensor_tensor(to, c, rs[t % bufs], ALU.mult)
                    else:
                        last = dve.scalar_tensor_tensor(out=to, in0=c, scalar=w, in1=rs[t % bufs],
                                                        op0=ALU.mult, op1=ALU.mult)
                last.then_inc(dve_s.sem, 1)
                if biased:
                    dve.wait_ge(dve_s.sem, dve_s.at(0, f"z{t}"))
                    dve.tensor_scalar(columns(outs[0][0], t), pre[t % bufs], outs[0][2], None, ALU.add)\
                        .then_inc(dve_s.sem, 1)


def project_stage(k, name, src, wq, wk, wv, q, kk, v, bq=None, bk=None, qn=None, kn=None, rope=None, eps=None,
                  bv_row=None):
    nc = k.nc
    normed, rotary = qn is not None, rope is not None
    sides = ["q", "k"]
    pe_steps = ["q", "k", "v"]
    act_steps = ["copy"]
    dve_steps = ["vcopy"]
    pool_steps = []
    for s in sides:
        if normed:
            act_steps += [f"sq_{s}"]
        else:
            act_steps += [f"id_{s}"]
    for s in sides:
        if normed:
            pe_steps += [f"mean_{s}"]
            act_steps += [f"ln_{s}", f"exp_{s}"]
            dve_steps += [f"nrm_{s}"]
    for s in sides:
        if rotary:
            pe_steps += [f"rot_{s}"]
            dve_steps += [f"sin_{s}", f"add_{s}"]
            pool_steps += [f"cos_{s}"]
    pe_s = Steps(k, "products", pe_steps, TILES)
    act_s = Steps(k, "lookups", act_steps, TILES)
    dve_s = Steps(k, "vectors", dve_steps, TILES)
    pool_s = Steps(k, "cosines", pool_steps, TILES) if rotary else None
    k.arena.used = k.arena_kept
    zt = k.arena.take(TILE)
    sq = {s: k.arena.take(TILE) for s in sides}
    rs = {s: k.arena.take(TILE) for s in sides}
    flat = {s: k.arena.take(TILE) for s in sides}
    cosd = {s: k.arena.take(TILE) for s in sides}
    bank = {"q": k.psum[:, 0, :], "k": k.psum[:, 1, :], "v": k.psum[:, 2, :], "mean_q": k.psum[:, 3, :],
            "mean_k": k.psum[:, 4, :], "rot_q": k.psum[:, 5, :], "rot_k": k.psum[:, 6, :]}
    weight = {"q": wq, "k": wk}
    bias = {"q": bq, "k": bk}
    norm_w = {"q": qn, "k": kn}
    dst = {"q": q, "k": kk}

    def two(ap):
        return ap.rearrange("p (b t) -> p b t", b=2)

    def both(table):
        return table.unsqueeze(1).to_broadcast([128, 2, SEQ])

    def bank_read(s):
        return (dve_s, f"nrm_{s}") if normed else (act_s, f"id_{s}")

    with nc.Block() as block:
        @block.tensor
        def _(pe):
            pe_s.prime(pe)
            with pe.Fori(0, TILES) as i:
                for s in sides:
                    r, step = bank_read(s)
                    pe.wait_ge(r.sem, r.before(i, step))
                    pe.matmul(bank[s], weight[s], src[:, tok(i, TILE)], start=True, stop=True).then_inc(pe_s.sem, 1)
                pe.wait_ge(act_s.sem, act_s.at(i, "copy"))
                pe.wait_ge(dve_s.sem, dve_s.before(i, "vcopy"))
                for j in range(4):
                    last = pe.matmul(bank["v"][:, j * 128:(j + 1) * 128], zt[:, j * 128:(j + 1) * 128], wv,
                                     start=True, stop=bv_row is None)
                    if bv_row is not None:
                        last = pe.matmul(bank["v"][:, j * 128:(j + 1) * 128], k.c["ones"][0:1, :], bv_row,
                                         start=False, stop=True)
                last.then_inc(pe_s.sem, 1)
                if normed:
                    for s in sides:
                        pe.wait_ge(act_s.sem, act_s.at(i, f"sq_{s}"))
                        pe.wait_ge(act_s.sem, act_s.before(i, f"ln_{s}"))
                        pe.matmul(bank[f"mean_{s}"], k.c["head_mean"], sq[s], start=True, stop=True)\
                            .then_inc(pe_s.sem, 1)
                if rotary:
                    for s in sides:
                        r, step = (dve_s, f"nrm_{s}") if normed else (act_s, f"id_{s}")
                        pe.wait_ge(r.sem, r.at(i, step))
                        pe.wait_ge(dve_s.sem, dve_s.before(i, f"sin_{s}"))
                        pe.matmul(bank[f"rot_{s}"], rope[0], flat[s], start=True, stop=True).then_inc(pe_s.sem, 1)

        @block.scalar
        def _(act):
            act_s.prime(act)
            k.load_table(act, EXP_LN)
            with act.Fori(0, TILES) as i:
                act.wait_ge(pe_s.sem, pe_s.before(i, "v"))
                act.copy(zt, src[:, tok(i, TILE)]).then_inc(act_s.sem, 1)
                for s in sides:
                    act.wait_ge(pe_s.sem, pe_s.at(i, s))
                    if normed:
                        act.wait_ge(pe_s.sem, pe_s.before(i, f"mean_{s}"))
                        act.activation(sq[s], bank[s], ACT.Square).then_inc(act_s.sem, 1)
                        continue
                    if rotary:
                        act.wait_ge(pe_s.sem, pe_s.before(i, f"rot_{s}"))
                        act.wait_ge(pool_s.sem, pool_s.before(i, f"cos_{s}"))
                    to = flat[s] if rotary else dst[s][:, bass.ds(i * TILE + SEQ, TILE)]
                    act.activation(to, bank[s], ACT.Identity, bias=bias[s] if bias[s] is not None else 0.0)\
                        .then_inc(act_s.sem, 1)
                if normed:
                    for s in sides:
                        act.wait_ge(pe_s.sem, pe_s.at(i, f"mean_{s}"))
                        act.wait_ge(dve_s.sem, dve_s.before(i, f"{'add' if rotary else 'nrm'}_{s}"))
                        act.activation(rs[s], bank[f"mean_{s}"], ACT.Ln, bias=k.c[eps]).then_inc(act_s.sem, 1)
                        act.wait_ge(act_s.sem, act_s.at(i, f"ln_{s}"))
                        act.activation(rs[s], rs[s], ACT.Exp, scale=-0.5).then_inc(act_s.sem, 1)

        @block.vector
        def _(dve):
            dve_s.prime(dve)
            with dve.Fori(0, TILES) as i:
                dve.wait_ge(pe_s.sem, pe_s.at(i, "v"))
                vt = v[:, bass.ds(i * 4 + 2, 4), :].rearrange("p t (h c) -> p t h c", c=VCOLS)[:, :, :, 0:HEAD_DIM]
                bv4 = bank["v"].rearrange("p (t h c) -> p t h c", t=4, c=HEAD_DIM)
                dve.tensor_copy(vt, bv4).then_inc(dve_s.sem, 1)
                if normed:
                    for s in sides:
                        dve.wait_ge(act_s.sem, act_s.at(i, f"exp_{s}"))
                        if rotary:
                            dve.wait_ge(pe_s.sem, pe_s.before(i, f"rot_{s}"))
                            dve.wait_ge(pool_s.sem, pool_s.before(i, f"cos_{s}"))
                        dve.scalar_tensor_tensor(out=flat[s], in0=bank[s], scalar=norm_w[s], in1=rs[s],
                                                 op0=ALU.mult, op1=ALU.mult).then_inc(dve_s.sem, 1)
                if rotary:
                    for s in sides:
                        dve.wait_ge(pe_s.sem, pe_s.at(i, f"rot_{s}"))
                        dve.wait_ge(dve_s.sem, dve_s.before(i, f"add_{s}"))
                        if normed:
                            dve.wait_ge(pe_s.sem, pe_s.at(i, f"mean_{s}"))
                        dve.tensor_tensor(two(rs[s]) if not normed else two(rs[s]), two(bank[f"rot_{s}"]),
                                          both(rope[2]), ALU.mult).then_inc(dve_s.sem, 1)
                        dve.wait_ge(dve_s.sem, dve_s.at(i, f"sin_{s}"))
                        dve.wait_ge(pool_s.sem, pool_s.at(i, f"cos_{s}"))
                        dve.tensor_tensor(dst[s][:, bass.ds(i * TILE + SEQ, TILE)], cosd[s], rs[s], ALU.add)\
                            .then_inc(dve_s.sem, 1)

        if rotary:
            @block.gpsimd
            def _(pool):
                pool_s.prime(pool)
                with pool.Fori(0, TILES) as i:
                    for s in sides:
                        r, step = (dve_s, f"nrm_{s}") if normed else (act_s, f"id_{s}")
                        pool.wait_ge(r.sem, r.at(i, step))
                        pool.wait_ge(dve_s.sem, dve_s.before(i, f"add_{s}"))
                        pool.tensor_tensor(two(cosd[s]), two(flat[s]), both(rope[1]), ALU.mult)\
                            .then_inc(pool_s.sem, 1)


def attention_stage(k, name, q, kk, v, out, causal, scale, bv=None):
    nc = k.nc
    pairs = range(HEADS // 2)
    last_pair = HEADS // 2 - 1
    order = [("shift", 0)]
    for p in range(1, HEADS // 2):
        order += [("s", p), ("max", p - 1), ("pv", p - 1)]
    order += [("max", last_pair), ("pv", last_pair), ("mt", 0), ("raw", 0), ("ot", 0)]
    pe_steps = []
    for what, p in order:
        if what != "raw":
            pe_steps += [f"s{p}_0", f"s{p}_1"] if what in ("s", "shift") else \
                [what] if what in ("ot", "mt") else [f"{what}{p}"]
    act_steps = [f"e{p}_{c}" for p in range(last_pair) for c in range(2)] + \
        ["qcopy", f"e{last_pair}_0", f"e{last_pair}_1", "kcopy", "ot"]
    dve_steps = ["qcopy", "km0", "km1"]
    for p in range(HEADS // 2 - 2):
        dve_steps += [f"max{p}", f"km{p + 2}"]
    dve_steps += [f"max{last_pair - 1}", f"max{last_pair}", "recip", "norm", "shift"]
    pool_steps = [f"qm{p}" for p in range(1, HEADS // 2)] + ["qm0"]
    pe_s = Steps(k, "products", pe_steps, BATCH + 1)
    act_s = Steps(k, "exponentials", act_steps, BATCH + 1)
    dve_s = Steps(k, "vectors", dve_steps, BATCH + 1)
    pool_s = Steps(k, "queries", pool_steps, BATCH + 1)
    k.arena.used = k.arena_kept
    kf = k.arena.take(SEQ)
    qf = k.arena.take(SEQ)
    qb = k.arena.take_bf16(SEQ)
    km = [k.arena.take_bf16(2 * SEQ).rearrange("p (h t) -> p h t", h=2) for _ in range(2)]
    qm = [k.arena.take(2 * SEQ).rearrange("p (h t) -> p h t", h=2) for _ in range(2)]
    prob = [k.arena.take(4 * SEQ).rearrange("p (c h t) -> p c h t", c=2, h=2) for _ in range(2)]
    mx = k.arena.take(2 * HEADS).rearrange("p (c h) -> p c h", c=2)
    shift = k.shift
    recip = k.arena.take(2 * HEADS).rearrange("p (c h) -> p c h", c=2)
    ob = k.arena.take(SEQ).rearrange("p (c f) -> p c f", c=2)
    mbank = [k.psum[:, 2 * u:2 * u + 2, :].rearrange("p c (h t) -> p c h t", h=2) for u in range(2)]
    sbank = [k.psum[:, 4 + u, :].rearrange("p (h t) -> p h t", h=2) for u in range(2)]
    obank = k.psum[:, 6, 0:2 * HEADS * VCOLS].rearrange("p (c h d) -> p c h d", c=2, h=HEADS)
    tbank, mtbank = k.psum[:, 7, :], k.psum[:, 0, 0:SEQ]
    ident, identb = k.c["ident"], k.cb["ident"]
    with nc.Block() as block:
        @block.tensor
        def _(pe):
            pe_s.prime(pe)

            def maxima(i, p):
                pe.wait_ge(dve_s.sem, dve_s.at(i, f"km{p}"))
                if p >= 2:
                    pe.wait_ge(dve_s.sem, dve_s.at(i, f"max{p - 2}"))
                for c in range(2):
                    n = 128 if causal and c == 0 else SEQ
                    last = pe.matmul(mbank[p % 2][:, c, :, 0:n], qb[:, c * 128:(c + 1) * 128],
                                     km[p % 2][:, :, 0:n], start=True, stop=True)
                    if causal:
                        for h in range(2):
                            last = pe.matmul(mbank[p % 2][:, c, h, c * 128:(c + 1) * 128], identb,
                                             k.cb["causal_qk"], start=False, stop=True, skip_group_check=True)
                last.then_inc(pe_s.sem, 1)

            first = [0, 128 if causal else 0]

            def raw(p, c):
                pe.matmul(sbank[c][:, :, first[c]:SEQ], kf[:, c * 128:(c + 1) * 128],
                          qm[p % 2][:, :, first[c]:SEQ], start=True, stop=True)
                if causal:
                    for h in range(2):
                        pe.matmul(sbank[c][:, h, c * 128:(c + 1) * 128], identb, k.cb["causal_kq"],
                                  start=False, stop=True, skip_group_check=True)

            def shifts(p):
                for c in range(2):
                    for h in range(2):
                        last = pe.matmul(sbank[c][:, h, first[c]:SEQ], k.cb["pick_head"][:, 2 * p + h, :],
                                         shift[:, first[c]:SEQ], start=False, stop=True, skip_group_check=True)
                    last.then_inc(pe_s.sem, 1)

            def scores(i, p):
                pe.wait_ge(pool_s.sem, pool_s.at(i, f"qm{p}"))
                for c in range(2):
                    pe.wait_ge(act_s.sem, act_s.at(i, f"e{p - 1}_{c}"))
                    raw(p, c)
                shifts(p)

            def first_raw(i):
                pe.wait_ge(pool_s.sem, pool_s.at(i, "qm0"))
                pe.wait_ge(act_s.sem, act_s.at(i, "kcopy"))
                raw(0, 0)
                raw(0, 1)

            def first_shifts(i):
                pe.wait_ge(dve_s.sem, dve_s.before(i, "shift"))
                shifts(0)

            def values(i, p):
                pe.wait_ge(act_s.sem, act_s.at(i, f"e{p}_1"))
                for h in range(2):
                    head = 2 * p + h
                    for c in range(2):
                        kts = [0] if causal and c == 0 else [0, 1]
                        for kt in kts:
                            vt = v[:, bass.ds(i * 2 + kt, 1), head * VCOLS:(head + 1) * VCOLS]
                            last = pe.matmul(obank[:, c, head, :], prob[p % 2][:, kt, h, c * 128:(c + 1) * 128],
                                             vt.rearrange("p a c -> p (a c)"),
                                             start=(kt == kts[0]), stop=(kt == kts[-1]))
                last.then_inc(pe_s.sem, 1)

            def turn_out(i):
                pe.wait_ge(dve_s.sem, dve_s.at(i, "norm"))
                pe.wait_ge(act_s.sem, act_s.before(i, "ot"))
                for c in range(2):
                    last = pe.transpose(tbank[:, SEQ + c * 128:SEQ + (c + 1) * 128], ob[:, c, :], ident)
                last.then_inc(pe_s.sem, 1)

            def turn_maxima(i):
                pe.wait_ge(dve_s.sem, dve_s.at(i, f"max{last_pair}"))
                for c in range(2):
                    last = pe.transpose(mtbank[0:HEADS, c * 128:(c + 1) * 128], mx[:, c, :], ident)
                last.then_inc(pe_s.sem, 1)

            def trip(i, new, old):
                for what, p in order:
                    if what in ("max", "mt", "raw"):
                        if new:
                            if what == "max":
                                maxima(i, p)
                            elif what == "mt":
                                turn_maxima(i)
                            else:
                                first_raw(i)
                        elif what != "raw":
                            pe_s.skip(pe, i, f"max{p}" if what == "max" else what)
                    elif old:
                        if what == "shift":
                            first_shifts(i)
                        elif what == "s":
                            scores(i, p)
                        elif what == "pv":
                            values(i, p)
                        else:
                            turn_out(i)
                    elif what in ("shift", "s"):
                        pe_s.skip(pe, i, f"s{p}_0", f"s{p}_1")
                    else:
                        pe_s.skip(pe, i, f"pv{p}" if what == "pv" else what)

            trip(0, True, False)
            with pe.Fori(1, BATCH) as i:
                trip(i, True, True)
            trip(BATCH, False, True)

        @block.scalar
        def _(act):
            act_s.prime(act)
            k.load_table(act, EXP_LN)
            def trip(i, new, old):
                for p in pairs:
                    if p == last_pair:
                        if new:
                            act.wait_ge(pool_s.sem, pool_s.at(i, f"qm{last_pair}"))
                            act.copy(qf, q[:, bass.ds(i * SEQ + SEQ, SEQ)]).then_inc(act_s.sem, 1)
                        else:
                            act_s.skip(act, i, "qcopy")
                    if not old:
                        act_s.skip(act, i, f"e{p}_0", f"e{p}_1")
                        continue
                    for c in range(2):
                        a = 128 if causal and c == 1 else 0
                        act.wait_ge(pe_s.sem, pe_s.at(i, f"s{p}_{c}"))
                        if c == 0:
                            if p >= 2:
                                act.wait_ge(pe_s.sem, pe_s.at(i, f"pv{p - 2}"))
                            else:
                                act.wait_ge(pe_s.sem, pe_s.before(i, f"pv{HEADS // 2 - 2 + p}"))
                        act.activation(prob[p % 2][:, c, :, a:SEQ], sbank[c][:, :, a:SEQ], ACT.Exp, scale=scale)\
                            .then_inc(act_s.sem, 1)
                if new:
                    act.wait_ge(pe_s.sem, pe_s.at(i, f"s{last_pair}_1"))
                    act.copy(kf, kk[:, bass.ds(i * SEQ + SEQ, SEQ)]).then_inc(act_s.sem, 1)
                else:
                    act_s.skip(act, i, "kcopy")
                if old:
                    act.wait_ge(pe_s.sem, pe_s.at(i, "ot"))
                    act.activation(out[:, tok(i, SEQ)], tbank[:, SEQ:2 * SEQ], ACT.Identity,
                                   bias=bv if bv is not None else 0.0).then_inc(act_s.sem, 1)
                else:
                    act_s.skip(act, i, "ot")

            trip(0, True, False)
            with act.Fori(1, BATCH) as i:
                trip(i, True, True)
            trip(BATCH, False, True)

        @block.vector
        def _(dve):
            dve_s.prime(dve)

            def mask_keys(i, p):
                if p >= 2:
                    dve.wait_ge(pe_s.sem, pe_s.at(i, f"max{p - 2}"))
                for h in range(2):
                    head = 2 * p + h
                    last = dve.tensor_scalar(km[p % 2][:, h, :], kk[:, bass.ds(i * SEQ + SEQ, SEQ)],
                                             k.c["head_mask"][:, head:head + 1], None, ALU.mult)
                last.then_inc(dve_s.sem, 1)

            def row_maxima(i, p):
                dve.wait_ge(pe_s.sem, pe_s.at(i, f"max{p}"))
                if p == 0:
                    dve.wait_ge(pe_s.sem, pe_s.before(i, "mt"))
                if causal:
                    dve.tensor_reduce(mx[:, 0, 2 * p:2 * p + 2], mbank[p % 2][:, 0, :, 0:128], AX_X, ALU.max)
                    dve.tensor_reduce(mx[:, 1, 2 * p:2 * p + 2], mbank[p % 2][:, 1, :, :], AX_X, ALU.max)\
                        .then_inc(dve_s.sem, 1)
                else:
                    dve.tensor_reduce(mx[:, :, 2 * p:2 * p + 2], mbank[p % 2], AX_X, ALU.max).then_inc(dve_s.sem, 1)

            def trip(i, new, old):
                if new:
                    dve.wait_ge(pe_s.sem, pe_s.before(i, f"max{last_pair}"))
                    dve.tensor_copy(qb, q[:, bass.ds(i * SEQ + SEQ, SEQ)]).then_inc(dve_s.sem, 1)
                    mask_keys(i, 0)
                    mask_keys(i, 1)
                    for p in pairs:
                        row_maxima(i, p)
                        if p + 2 < HEADS // 2:
                            mask_keys(i, p + 2)
                else:
                    dve_s.skip(dve, i, *dve_steps[0:dve_steps.index("recip")])
                if old:
                    dve.wait_ge(pe_s.sem, pe_s.at(i, f"pv{last_pair}"))
                    dve.reciprocal(recip, obank[:, :, :, HEAD_DIM]).then_inc(dve_s.sem, 1)
                    dve.wait_ge(dve_s.sem, dve_s.at(i, "recip"))
                    dve.wait_ge(pe_s.sem, pe_s.before(i, "ot"))
                    for c in range(2):
                        last = dve.tensor_tensor(ob[:, c, :].rearrange("p (h d) -> p h d", d=HEAD_DIM),
                                                 obank[:, c, :, 0:HEAD_DIM],
                                                 recip[:, c, :].unsqueeze(2).to_broadcast([128, HEADS, HEAD_DIM]),
                                                 ALU.mult)
                    last.then_inc(dve_s.sem, 1)
                else:
                    dve_s.skip(dve, i, "recip", "norm")
                if new:
                    dve.wait_ge(pe_s.sem, pe_s.at(i, "mt"))
                    dve.tensor_scalar(shift[0:HEADS, :], mtbank[0:HEADS, :], -1.0, None, ALU.mult)\
                        .then_inc(dve_s.sem, 1)
                else:
                    dve_s.skip(dve, i, "shift")

            trip(0, True, False)
            with dve.Fori(1, BATCH) as i:
                trip(i, True, True)
            trip(BATCH, False, True)

        @block.gpsimd
        def _(pool):
            pool_s.prime(pool)
            def trip(i, new, old):
                for p in [*range(1, HEADS // 2), 0]:
                    if not (old if p else new):
                        pool_s.skip(pool, i, f"qm{p}")
                        continue
                    if p == 0:
                        pool.wait_ge(pe_s.sem, pe_s.at(i, f"s{last_pair - 1}_1"))
                        pool.wait_ge(act_s.sem, act_s.at(i, "qcopy"))
                    elif p == 1:
                        pool.wait_ge(pe_s.sem, pe_s.before(i, f"s{last_pair}_1"))
                    else:
                        pool.wait_ge(pe_s.sem, pe_s.at(i, f"s{p - 2}_1"))
                    pool.tensor_tensor(qm[p % 2], qf.unsqueeze(1).to_broadcast([128, 2, SEQ]),
                                       k.c["head_mask"][:, 2 * p:2 * p + 2].unsqueeze(2).to_broadcast([128, 2, SEQ]),
                                       ALU.mult).then_inc(pool_s.sem, 1)

            trip(0, True, False)
            with pool.Fori(1, BATCH) as i:
                trip(i, True, True)
            trip(BATCH, False, True)


def output_stage(k, name, parts, add_to, dst, factor=None, bias=None):
    nc = k.nc
    pe_s = Steps(k, "products", ["m0", "m1"], TILES // 2)
    dve_s = Steps(k, "added", ["a0", "a1"], TILES // 2)
    with nc.Block() as block:
        @block.tensor
        def _(pe):
            pe_s.prime(pe)
            with pe.Fori(0, TILES // 2) as i:
                for u in range(2):
                    pe.wait_ge(dve_s.sem, dve_s.before(i, f"a{u}"))
                    for n, (w, src, off) in enumerate(parts):
                        last = pe.matmul(k.psum[:, u, :], w, src[:, bass.ds(i * (2 * TILE) + (u * TILE + off), TILE)],
                                         start=(n == 0), stop=(n == len(parts) - 1))
                    last.then_inc(pe_s.sem, 1)

        @block.vector
        def _(dve):
            dve_s.prime(dve)
            with dve.Fori(0, TILES // 2) as i:
                for u in range(2):
                    cols = bass.ds(i * (2 * TILE) + u * TILE, TILE)
                    dve.wait_ge(pe_s.sem, pe_s.at(i, f"m{u}"))
                    dve.scalar_tensor_tensor(out=dst[:, cols], in0=k.psum[:, u, :],
                                             scalar=bias if bias is not None else float(factor or 1.0),
                                             in1=add_to[:, cols], op0=ALU.add if bias is not None else ALU.mult,
                                             op1=ALU.add).then_inc(dve_s.sem, 1)
def gated_mlp_stage(k, name, src, widths, w_lin, w_act, b_lin, b_act, w_out, func, table, add_to, dst, b_out):
    nc = k.nc
    tiles = range(len(widths))
    pe_steps, act_steps, dve_steps = [], [], []
    for n in tiles:
        pe_steps += [f"act{n}", f"lin{n}"]
        act_steps += [f"f{n}"]
        dve_steps += [f"h{n}"]
    pe_s = Steps(k, "products", pe_steps + ["out"], TILES)
    act_s = Steps(k, "gates", act_steps, TILES)
    dve_s = Steps(k, "hidden", dve_steps + ["sum"], TILES)
    k.arena.reset()
    gate = [k.arena.take(TILE) for _ in range(2)]
    hid = [k.arena.take(TILE) for _ in tiles]
    abank = [k.psum[:, n, :] for n in range(3)]
    lbank = [k.psum[:, 3 + n, :] for n in range(3)]
    obank = k.psum[:, 6, :]
    N = len(widths)

    def earlier(steps, i, prefix, n, back):
        return steps.at(i, f"{prefix}{n - back}") if n >= back else steps.before(i, f"{prefix}{n - back + N}")

    with nc.Block() as block:
        @block.tensor
        def _(pe):
            pe_s.prime(pe)
            with pe.Fori(0, TILES) as i:
                for n, w in enumerate(widths):
                    at = sum(widths[:n])
                    back = 3 if n >= 3 else None
                    last_user = max(m for m in tiles if m % 3 == n % 3)
                    pe.wait_ge(dve_s.sem, dve_s.at(i, f"h{n - 3}") if back else dve_s.before(i, f"h{last_user}"))
                    pe.matmul(abank[n % 3][0:w, :], w_act[:, at:at + w], src[:, tok(i, TILE)],
                              start=True, stop=True).then_inc(pe_s.sem, 1)
                    pe.matmul(lbank[n % 3][0:w, :], w_lin[:, at:at + w], src[:, tok(i, TILE)],
                              start=True, stop=True).then_inc(pe_s.sem, 1)
                pe.wait_ge(dve_s.sem, dve_s.before(i, "sum"))
                for n, w in enumerate(widths):
                    pe.wait_ge(dve_s.sem, dve_s.at(i, f"h{n}"))
                    last = pe.matmul(obank, w_out[0:w, n * 128:(n + 1) * 128], hid[n][0:w, :],
                                     start=(n == 0), stop=(n == N - 1))
                last.then_inc(pe_s.sem, 1)

        @block.scalar
        def _(act):
            act_s.prime(act)
            k.load_table(act, table)
            with act.Fori(0, TILES) as i:
                for n, w in enumerate(widths):
                    act.wait_ge(pe_s.sem, pe_s.at(i, f"act{n}"))
                    if n >= 2:
                        act.wait_ge(dve_s.sem, dve_s.at(i, f"h{n - 2}"))
                    else:
                        act.wait_ge(dve_s.sem, dve_s.before(i, f"h{max(m for m in tiles if m % 2 == n % 2)}"))
                    b = b_act[0:w, n:n + 1] if b_act is not None else 0.0
                    act.activation(gate[n % 2][0:w, :], abank[n % 3][0:w, :], func, bias=b).then_inc(act_s.sem, 1)

        @block.vector
        def _(dve):
            dve_s.prime(dve)
            with dve.Fori(0, TILES) as i:
                for n, w in enumerate(widths):
                    dve.wait_ge(pe_s.sem, pe_s.at(i, f"lin{n}"))
                    dve.wait_ge(pe_s.sem, pe_s.before(i, "out"))
                    dve.wait_ge(act_s.sem, act_s.at(i, f"f{n}"))
                    b = b_lin[0:w, n:n + 1] if b_lin is not None else 1.0
                    dve.scalar_tensor_tensor(out=hid[n][0:w, :], in0=lbank[n % 3][0:w, :], scalar=b,
                                             in1=gate[n % 2][0:w, :],
                                             op0=ALU.add if b_lin is not None else ALU.mult,
                                             op1=ALU.mult).then_inc(dve_s.sem, 1)
                dve.wait_ge(pe_s.sem, pe_s.at(i, "out"))
                dve.scalar_tensor_tensor(out=dst[:, tok(i, TILE)], in0=obank,
                                         scalar=b_out if b_out is not None else 1.0, in1=add_to[:, tok(i, TILE)],
                                         op0=ALU.add if b_out is not None else ALU.mult, op1=ALU.add)\
                    .then_inc(dve_s.sem, 1)


def add_stage(k, name, src, dst):
    half = TOKENS * 5 // 8
    with k.nc.Block() as block:
        @block.vector
        def _(dve):
            dve.tensor_tensor(dst[:, 0:half], dst[:, 0:half], src[:, 0:half], ALU.add)

        @block.gpsimd
        def _(pool):
            pool.tensor_tensor(dst[:, half:TOKENS], dst[:, half:TOKENS], src[:, half:TOKENS], ALU.add)


EXPERTS, HIDDEN = 8, 512


def router_stage(k, name, z, w, R, RT):
    nc = k.nc
    us, trips = range(4), TILES // 4
    pe_s = Steps(k, "logits", [f"logits{u}" for u in us], trips)
    act_s = Steps(k, "tokens", [f"copy{u}" for u in us], trips)
    dve_s = Steps(k, "kept", [f"lg{u}" for u in us], trips)
    lg = k.arena.take(32 * EXPERTS).rearrange("p (t e) -> p t e", e=EXPERTS)
    zt = [k.arena.take(TILE) for _ in us]
    lbank = [k.psum[:, u, 0:32].rearrange("p (t e) -> p t e", e=EXPERTS) for u in us]
    with nc.Block() as block:
        @block.tensor
        def _(pe):
            pe_s.prime(pe)
            with pe.Fori(0, trips) as i:
                for u in us:
                    pe.wait_ge(act_s.sem, act_s.at(i, f"copy{u}"))
                    pe.wait_ge(dve_s.sem, dve_s.before(i, f"lg{u}"))
                    for j in range(4):
                        pe.matmul(lbank[u][:, j, :], zt[u][:, j * 128:(j + 1) * 128], w["wr"], start=True, stop=False)
                        last = pe.matmul(lbank[u][:, j, :], k.c["ones"][0:1, :], w["br"][0:1, :], start=False,
                                         stop=True)
                    last.then_inc(pe_s.sem, 1)

        @block.scalar
        def _(act):
            act_s.prime(act)
            with act.Fori(0, trips) as i:
                for u in us:
                    act.wait_ge(pe_s.sem, pe_s.before(i, f"logits{u}"))
                    act.copy(zt[u], z[:, bass.ds(i * (4 * TILE) + u * TILE, TILE)]).then_inc(act_s.sem, 1)

        @block.vector
        def _(dve):
            dve_s.prime(dve)
            with dve.Fori(0, trips) as i:
                for u in us:
                    dve.wait_ge(pe_s.sem, pe_s.at(i, f"logits{u}"))
                    dve.tensor_copy(lg[:, bass.ds(i * 16 + u * 4, 4), :], lbank[u]).then_inc(dve_s.sem, 1)

    chain = Count(k, "router_chain", 18)
    weighed = Count(k, "router_exp", 1)
    turned = Count(k, "router_turned", 8)
    shape = [128, 32, EXPERTS]

    def wide(ap):
        return ap.unsqueeze(2).to_broadcast(shape)

    def small():
        return k.arena.take(32)

    top, first, second = [small(), small()], k.arena.take(256), k.arena.take(256)
    first, second = (a.rearrange("p (t e) -> p t e", e=EXPERTS) for a in (first, second))
    rank, diff, ex, den, w1, w2 = small(), small(), small(), small(), small(), small()
    even = k.arena.take(256).rearrange("p (t e) -> p t e", e=EXPERTS)
    rest = k.arena.take(256).rearrange("p (t e) -> p t e", e=EXPERTS)
    rev = k.c["reverse"].unsqueeze(1).to_broadcast(shape)
    with nc.Block() as block:
        @block.vector
        def _(dve):
            def pick(at, values, best, onehot):
                dve.tensor_reduce(best, values, AX_X, ALU.max).then_inc(chain.sem, 1)
                dve.wait_ge(chain.sem, chain.at(at + 1))
                dve.tensor_tensor(even, values, wide(best), ALU.is_equal).then_inc(chain.sem, 1)
                dve.wait_ge(chain.sem, chain.at(at + 2))
                dve.tensor_tensor(even, even, rev, ALU.mult).then_inc(chain.sem, 1)
                dve.wait_ge(chain.sem, chain.at(at + 3))
                dve.tensor_reduce(rank, even, AX_X, ALU.max).then_inc(chain.sem, 1)
                dve.wait_ge(chain.sem, chain.at(at + 4))
                dve.tensor_tensor(onehot, rev, wide(rank), ALU.is_equal).then_inc(chain.sem, 1)
                dve.wait_ge(chain.sem, chain.at(at + 5))

            pick(0, lg, top[0], first)
            dve.scalar_tensor_tensor(out=rest, in0=first, scalar=NEG, in1=lg, op0=ALU.mult, op1=ALU.add)\
                .then_inc(chain.sem, 1)
            dve.wait_ge(chain.sem, chain.at(6))
            pick(6, rest, top[1], second)
            dve.tensor_tensor(diff, top[1], top[0], ALU.subtract).then_inc(chain.sem, 1)
            dve.wait_ge(weighed.sem, weighed.at(1))
            dve.tensor_scalar(den, ex, 1.0, None, ALU.add).then_inc(chain.sem, 1)
            dve.wait_ge(chain.sem, chain.at(13))
            dve.reciprocal(w1, den).then_inc(chain.sem, 1)
            dve.wait_ge(chain.sem, chain.at(14))
            dve.tensor_tensor(w2, ex, w1, ALU.mult).then_inc(chain.sem, 1)
            dve.tensor_tensor(first, first, wide(w1), ALU.mult).then_inc(chain.sem, 1)
            dve.wait_ge(chain.sem, chain.at(15))
            dve.tensor_tensor(second, second, wide(w2), ALU.mult).then_inc(chain.sem, 1)
            dve.wait_ge(chain.sem, chain.at(17))
            dve.tensor_tensor(R, first, second, ALU.add).then_inc(chain.sem, 1)
            for b in range(8):
                dve.wait_ge(turned.sem, turned.at(b + 1))
                dve.tensor_copy(RT[0:EXPERTS, b * 512:(b + 1) * 512], k.psum[0:EXPERTS, b, :])

        @block.scalar
        def _(act):
            k.load_table(act, EXP_LN)
            act.wait_ge(chain.sem, chain.at(12))
            act.activation(ex, diff, ACT.Exp).then_inc(weighed.sem, 1)

        @block.tensor
        def _(pe):
            pe.wait_ge(chain.sem, chain.at(18))
            for b in range(8):
                for j in range(4):
                    last = pe.transpose(k.psum[0:EXPERTS, b, j * 128:(j + 1) * 128], R[:, 4 * b + j, :], k.c["ident"])
                last.then_inc(turned.sem, 1)


def experts_stage(k, name, z, w, R, RT, out):
    nc = k.nc
    ex, quads = range(EXPERTS), range(4)
    pe_steps, act_steps, dve_steps = [], ["zcopy", "rtcopy"], []
    for e in ex:
        pe_steps += [f"h{e}_{f}" for f in quads] + ([f"o{e - 1}"] if e else ["base", "turn"])
        act_steps += [f"r{e}_{f}" for f in quads] + ([] if e else ["out", "rcopy", "base"])
        dve_steps += [f"a{e}"]
    pe_s = Steps(k, "products", pe_steps + [f"o{EXPERTS - 1}"], TILES)
    act_s = Steps(k, "relus", act_steps, TILES)
    turned = Count(k, "last_turned", 1)
    dve_s = Steps(k, "weighed", dve_steps, TILES)
    zt = k.arena.take(TILE)
    r4 = k.arena.take(4 * EXPERTS).rearrange("p (t e) -> p t e", e=EXPERTS)
    rt4 = k.arena.take(TILE)
    hid = [k.arena.take(4 * TILE).rearrange("p (f t) -> p f t", f=4) for _ in range(2)]
    acc = k.arena.take(TILE)
    w1 = w["w1"].rearrange("p (e f) -> p e f", e=EXPERTS)
    w2 = w["w2"].rearrange("p (e f d) -> p e f d", e=EXPERTS, f=4)
    b1 = w["b1"].rearrange("p (e f) -> p e f", e=EXPERTS)
    hbank = [k.psum[:, f, :] for f in quads]
    obank = [k.psum[:, 4 + u, :] for u in range(2)]
    base, turn = k.psum[:, 6, :], k.psum[:, 7, :]

    def part(ap, j):
        return ap[:, j * 128:(j + 1) * 128]

    with nc.Block() as block:
        @block.tensor
        def _(pe):
            pe_s.prime(pe)

            def expert_out(i, e):
                pe.wait_ge(act_s.sem, act_s.at(i, f"r{e}_3"))
                if e >= 2:
                    pe.wait_ge(dve_s.sem, dve_s.at(i, f"a{e - 2}"))
                else:
                    pe.wait_ge(dve_s.sem, dve_s.before(i, f"a{EXPERTS - 2 + e}"))
                for j in quads:
                    for f in quads:
                        last = pe.matmul(part(obank[e % 2], j), part(hid[e % 2][:, f, :], j), w2[:, e, f, :],
                                         start=(f == 0), stop=(f == 3))
                last.then_inc(pe_s.sem, 1)

            def turn_sum():
                for j in quads:
                    last = pe.transpose(part(turn, j), part(acc, j), k.c["ident"])
                return last

            def trip(i, first):
                for e in ex:
                    for f in quads:
                        if e:
                            pe.wait_ge(act_s.sem, act_s.at(i, f"r{e - 1}_{f}"))
                        else:
                            pe.wait_ge(act_s.sem, act_s.at(i, "zcopy"))
                        pe.matmul(hbank[f], w1[:, e, f * 128:(f + 1) * 128], zt, start=True, stop=True)\
                            .then_inc(pe_s.sem, 1)
                    if e:
                        expert_out(i, e - 1)
                        continue
                    pe.wait_ge(act_s.sem, act_s.at(i, "rtcopy"))
                    pe.wait_ge(act_s.sem, act_s.before(i, "base"))
                    for j in quads:
                        pe.matmul(part(base, j), part(zt, j), k.c["ident"], start=True, stop=False)
                        last = pe.matmul(part(base, j), part(rt4, j)[0:EXPERTS, :], w["b2"][0:EXPERTS, :],
                                         start=False, stop=True)
                    last.then_inc(pe_s.sem, 1)
                    if first:
                        pe_s.skip(pe, i, "turn")
                    else:
                        pe.wait_ge(dve_s.sem, dve_s.before(i, f"a{EXPERTS - 1}"))
                        pe.wait_ge(act_s.sem, act_s.before(i, "out"))
                        turn_sum().then_inc(pe_s.sem, 1)
                expert_out(i, EXPERTS - 1)

            trip(0, True)
            with pe.Fori(1, TILES) as i:
                trip(i, False)
            pe.wait_ge(dve_s.sem, dve_s.at(TILES - 1, f"a{EXPERTS - 1}"))
            pe.wait_ge(act_s.sem, act_s.at(TILES - 1, "out"))
            turn_sum().then_inc(turned.sem, 1)

        @block.scalar
        def _(act):
            act_s.prime(act)

            def trip(i, first):
                act.wait_ge(pe_s.sem, pe_s.before(i, f"h{EXPERTS - 1}_3"))
                act.copy(zt, z[:, tok(i, TILE)]).then_inc(act_s.sem, 1)
                act.copy(rt4[0:EXPERTS, :], RT[0:EXPERTS, tok(i, TILE)]).then_inc(act_s.sem, 1)
                for e in ex:
                    for f in quads:
                        act.wait_ge(pe_s.sem, pe_s.at(i, f"h{e}_{f}"))
                        if f == 0:
                            if e >= 2:
                                act.wait_ge(pe_s.sem, pe_s.at(i, f"o{e - 2}"))
                            else:
                                act.wait_ge(pe_s.sem, pe_s.before(i, f"o{EXPERTS - 2 + e}"))
                        act.activation(hid[e % 2][:, f, :], hbank[f], ACT.Relu, bias=b1[:, e, f:f + 1])\
                            .then_inc(act_s.sem, 1)
                    if e:
                        continue
                    if first:
                        act_s.skip(act, i, "out")
                    else:
                        act.wait_ge(pe_s.sem, pe_s.at(i, "turn"))
                        act.copy(out[:, bass.ds(i * TILE - TILE, TILE)], turn).then_inc(act_s.sem, 1)
                    act.wait_ge(dve_s.sem, dve_s.before(i, f"a{EXPERTS - 1}"))
                    act.copy(r4, R[:, bass.ds(i * 4, 4), :]).then_inc(act_s.sem, 1)
                    act.wait_ge(pe_s.sem, pe_s.at(i, "base"))
                    act.wait_ge(pe_s.sem, pe_s.at(i, "turn"))
                    act.copy(acc, base).then_inc(act_s.sem, 1)

            trip(0, True)
            with act.Fori(1, TILES) as i:
                trip(i, False)
            act.wait_ge(turned.sem, turned.at(1))
            act.copy(out[:, TOKENS - TILE:TOKENS], turn)

        @block.vector
        def _(dve):
            dve_s.prime(dve)
            with dve.Fori(0, TILES) as i:
                for e in ex:
                    dve.wait_ge(pe_s.sem, pe_s.at(i, f"o{e}"))
                    if e == 0:
                        dve.wait_ge(act_s.sem, act_s.at(i, "base"))
                    else:
                        dve.wait_ge(dve_s.sem, dve_s.at(i, f"a{e - 1}"))
                    for j in quads:
                        last = dve.scalar_tensor_tensor(out=part(acc, j), in0=part(obank[e % 2], j),
                                                        scalar=r4[:, j, e:e + 1], in1=part(acc, j),
                                                        op0=ALU.mult, op1=ALU.add)
                    last.then_inc(dve_s.sem, 1)


def l1_ffn(k, name, w):
    norm_stage(k, f"{name}_ln", k.X, [(k.Z, None, None)], True, "eps5")
    k.arena.reset()
    R = k.arena.take(32 * EXPERTS).rearrange("p (t e) -> p t e", e=EXPERTS)
    RT = k.Y
    router_stage(k, f"{name}_router", k.Z, w, R, RT)
    k.arena.used = 32 * EXPERTS
    experts_stage(k, f"{name}_experts", k.Z, w, R, RT, k.H)
    norm_stage(k, f"{name}_last", k.H, [(k.Z, w["gamma"], w["beta"])], True, "eps5")
    add_stage(k, f"{name}_add", k.Z, k.X)


def more_groups(groups, i):
    A = "L1_ffn_"
    w1, w2 = i[A + "W1"], i[A + "W2"]
    groups["l1_ffn"] = {
        "w1": w1.transpose(2, 0, 1), "w2": w2.transpose(2, 0, 1).reshape(4, 128, EXPERTS, 128).transpose(1, 2, 0, 3),
        "b1": i[A + "b1"].reshape(EXPERTS, 4, 128).transpose(2, 0, 1), "b2": i[A + "b2"], "wr": i[A + "Wr"].T,
        "br": i[A + "br"].reshape(1, -1), "gamma": column(i[A + "gamma"]), "beta": column(i[A + "beta"])}
    groups["l0_ffn"] = l0_ffn_group(i)
    groups["l1_attn_b"] = l1_attn_b_group(i)
    groups["l0_attn_a"], groups["ssm_scan"] = l0_attn_a_groups(i)


WHEADS, WDIM = 8, 64
TINY = 1e-24
TINY_SCALE = 2.0 ** 20


def shift_stage(k, name, src, dst):

    def per_batch(ap):
        return ap.rearrange("p (b t) -> p b t", t=SEQ)

    with k.nc.Block() as block:
        @block.vector
        def _(dve):
            dve.memset(per_batch(dst[64:128, 0:TOKENS])[:, :, 0:1], 0.0)
            dve.tensor_copy(per_batch(dst[64:128, 0:TOKENS])[:, :, 1:SEQ],
                            per_batch(src[64:128, 0:TOKENS])[:, :, 0:SEQ - 1])

        @block.scalar
        def _(act):
            act.copy(dst[0:64, 0:TOKENS // 2], src[0:64, 0:TOKENS // 2])

        @block.gpsimd
        def _(pool):
            pool.tensor_copy(dst[0:64, TOKENS // 2:TOKENS], src[0:64, TOKENS // 2:TOKENS])


def window_attention_stage(k, name, src, y_padded, w, tables):
    nc = k.nc
    groups, heads = range(4), range(WHEADS)
    pe_steps = ["proj0", "proj1", "s0", "s1"]
    new_steps = [["ss0"], ["ss1"], ["rot0", "proj2"], ["rot1", "proj3"], ["ss2"], ["ss3"], ["rot2"], ["rot3"]]
    for n, first in enumerate(new_steps):
        pe_steps += ([f"pv{n}"] + first if n in (2, 3) else first + [f"pv{n}"]) + \
            ([f"s{n + 2}"] if n < 6 else [])
    pe_steps += ["max0", "v0", "v1", "turn0", "turn1", "max1", "max2", "max3", "wo", "mt"]
    act_steps = ["hcopy", "sq0", "sq1", "e0", "e1", "ln0", "exp0", "e2", "ln1", "exp1", "e3", "sq2", "e4", "sq3",
                 "e5", "ln2", "exp2", "e6", "ln3", "exp3", "e7", "v0", "v1", "turn0", "turn1"]
    dve_steps = ["clip0", "clip1", "nrm0", "nrm1", "sin0", "add0", "sin1", "add1"]
    dve_steps += ["clip2", "clip3", "nrm2", "nrm3", "sin2", "sin3", "recip", "norm", "max0", "add2", "add3", "max1", "max2", "max3", "sum", "shift"]
    pool_steps = ["cos0", "cos1", "low0", "low1", "cos2", "cos3", "low2", "low3"]
    trips = BATCH + 1
    pe_s = Steps(k, "products", pe_steps, trips)
    act_s = Steps(k, "lookups", act_steps, trips)
    dve_s = Steps(k, "vectors", dve_steps, trips)
    pool_s = Steps(k, "sides", pool_steps, trips)
    k.arena.reset()
    take = k.arena.take
    hb = take(SEQ)
    sq = [take(TILE) for _ in groups]
    rs = [take(TILE) for _ in range(2)]
    flat = [take(TILE) for _ in range(2)]
    cosd = [take(TILE) for _ in range(2)]
    qk = take(8 * SEQ).rearrange("p (f t) -> p f t", f=8)
    qkb = k.arena.take_bf16(8 * SEQ).rearrange("p (f t) -> p f t", f=8)
    v = take(2 * WHEADS * (WDIM + 1)).rearrange("p (c h d) -> p c h d", c=2, h=WHEADS)
    prob = [take(320) for _ in range(2)]
    mx = take(2 * WHEADS).rearrange("p (c h) -> p c h", c=2)
    recip = take(16)
    ob = take(2 * 512).rearrange("p (c h d) -> p c h d", c=2, h=WHEADS)
    oT = take(4 * SEQ).rearrange("p (f t) -> p f t", f=4)
    shift = k.shift
    bank = [k.psum[:, n, :] for n in range(8)]
    mbanks = [k.psum[:, 3:5, :], k.psum[:, 0:2, :]] * 2

    def flat8(g):
        return qk[:, 2 * g:2 * g + 2, :].rearrange("p f t -> p (f t)")

    def unit(h, c):
        n = 2 * h + c
        return bank[5 + n // 6][:, 65 * (n % 6):65 * (n % 6) + 65]

    filled = Count(k, "filled", 4)
    with nc.Block() as block:
        @block.vector
        def _(dve):
            dve.memset(v.rearrange("p c h d -> p (c h d)"), 1.0).then_inc(filled.sem, 1)
            dve.memset(qk.rearrange("p f t -> p (f t)"), 0.0).then_inc(filled.sem, 1)
            dve.memset(shift[:, :], 0.0).then_inc(filled.sem, 1)
            dve.memset(src[:, TOKENS:TOKENS + SEQ], 0.0).then_inc(filled.sem, 1)
            dve.wait_ge(filled.sem, filled.at(4))

    with nc.Block() as block:
        @block.tensor
        def _(pe):
            pe_s.prime(pe)

            def project(i, g):
                if g >= 2:
                    pe.wait_ge(dve_s.sem, dve_s.at(i, f"nrm{g - 2}"))
                for m in range(2):
                    at = m * 512 + g * 128
                    last = pe.matmul(bank[g % 2][:, m * SEQ:(m + 1) * SEQ], w["wqkv"][:, at:at + 128], hb,
                                     start=True, stop=True)
                last.then_inc(pe_s.sem, 1)

            def sum_squares(i, g):
                pe.wait_ge(act_s.sem, act_s.at(i, f"sq{g}"))
                if g == 0:
                    pe.wait_ge(dve_s.sem, dve_s.before(i, "sum"))
                else:
                    pe.wait_ge(dve_s.sem, dve_s.at(i, {1: "clip0", 2: "sin1", 3: "clip2"}[g]))
                pe.matmul(bank[2], k.c64["head_sum"], sq[g], start=True, stop=True).then_inc(pe_s.sem, 1)

            def rotate(i, g):
                pe.wait_ge(dve_s.sem, dve_s.at(i, f"nrm{g}"))
                if g % 2:
                    pe.wait_ge(dve_s.sem, dve_s.at(i, f"sin{g - 1}"))
                pe.matmul(bank[2], k.c64["rot"], flat[g % 2], start=True, stop=True).then_inc(pe_s.sem, 1)

            def scores(i, h):
                f, rows = h // 2, slice(64 * (h % 2), 64 * (h % 2) + 64)
                if h >= 2:
                    pe.wait_ge(act_s.sem, act_s.at(i, f"e{h - 2}"))
                else:
                    pe.wait_ge(dve_s.sem, dve_s.before(i, "shift"))
                to = bank[3 + h % 2]
                pe.matmul(to[:, 0:192], qk[rows, 2 * f + 1, 0:128], qk[rows, 2 * f, 0:192], start=True, stop=True)
                pe.matmul(to[:, 192:320], qk[rows, 2 * f + 1, 128:256], qk[rows, 2 * f, 128:256], start=False,
                          stop=True, skip_group_check=True)
                pe.matmul(to[:, 0:320], k.cb["ident"], k.cb64["band_kq"], start=False, stop=True,
                          skip_group_check=True)
                pe.matmul(to[:, 0:192], k.cb["pick_head"][:, h, :], shift[:, 0:192], start=False, stop=True,
                          skip_group_check=True)
                pe.matmul(to[:, 192:320], k.cb["pick_head"][:, h, :], shift[:, 128:256], start=False, stop=True,
                          skip_group_check=True).then_inc(pe_s.sem, 1)

            def values(i, h):
                pe.wait_ge(act_s.sem, act_s.at(i, f"e{h}"))
                pb = prob[h % 2]
                pe.matmul(unit(h, 0), pb[:, 0:128], v[:, 0, h, :], start=True, stop=True)
                pe.matmul(unit(h, 1), pb[:, 192:320], v[:, 1, h, :], start=True, stop=True)
                pe.matmul(unit(h, 1)[0:64, :], pb[:, 128:192], v[:, 0, h, :], start=False, stop=True,
                          skip_group_check=True).then_inc(pe_s.sem, 1)

            def maxima(i, f):
                pe.wait_ge(pool_s.sem, pool_s.at(i, f"low{f}"))
                for r in range(2):
                    to, rows = mbanks[f][:, r, :], slice(64 * r, 64 * r + 64)
                    pe.matmul(to[:, 0:128], qkb[rows, 2 * f, 0:128], qkb[rows, 2 * f + 1, 0:128],
                              start=True, stop=True)
                    pe.matmul(to[:, 128:320], qkb[rows, 2 * f, 128:256], qkb[rows, 2 * f + 1, 64:256],
                              start=False, stop=True, skip_group_check=True)
                    last = pe.matmul(to[:, 0:320], k.cb["ident"], k.cb64["band_qk"], start=False, stop=True,
                                     skip_group_check=True)
                last.then_inc(pe_s.sem, 1)

            def turn(i, half):
                for m in range(2):
                    f = 2 * half + m
                    for c in range(2):
                        last = pe.transpose(bank[3 + half][:, m * SEQ + c * 128:m * SEQ + (c + 1) * 128],
                                            ob[:, c, 2 * f:2 * f + 2, :].rearrange("p h d -> p (h d)"),
                                            k.c["ident"])
                last.then_inc(pe_s.sem, 1)

            def trip(i, new, old):
                if new:
                    pe.wait_ge(act_s.sem, act_s.at(i, "hcopy"))
                    pe.wait_ge(dve_s.sem, dve_s.before(i, "max3"))
                    project(i, 0)
                    project(i, 1)
                else:
                    pe_s.skip(pe, i, "proj0", "proj1")
                if old:
                    scores(i, 0)
                    scores(i, 1)
                else:
                    pe_s.skip(pe, i, "s0", "s1")

                def of_new(n):
                    if n in (0, 1, 4, 5):
                        sum_squares(i, n % 4 + (2 if n >= 4 else 0))
                    elif n in (2, 3):
                        rotate(i, n - 2)
                        project(i, n)
                    else:
                        rotate(i, n - 4)

                for n in heads:
                    late = n in (2, 3)
                    if new and not late:
                        of_new(n)
                    elif not late:
                        pe_s.skip(pe, i, *new_steps[n])
                    if old:
                        values(i, n)
                    else:
                        pe_s.skip(pe, i, f"pv{n}")
                    if new and late:
                        of_new(n)
                    elif late:
                        pe_s.skip(pe, i, *new_steps[n])
                    if n < 6:
                        if old:
                            scores(i, n + 2)
                        else:
                            pe_s.skip(pe, i, f"s{n + 2}")
                if new:
                    maxima(i, 0)
                    for c in range(2):
                        pe.matmul(bank[c], hb[:, c * 128:(c + 1) * 128], w["wqkv"][:, 1024:1536],
                                  start=True, stop=True).then_inc(pe_s.sem, 1)
                else:
                    pe_s.skip(pe, i, "max0", "v0", "v1")
                pe.wait_ge(dve_s.sem, dve_s.at(i, "max0"))
                if old:
                    turn(i, 0)
                    turn(i, 1)
                else:
                    pe_s.skip(pe, i, "turn0", "turn1")
                if new:
                    pe.wait_ge(act_s.sem, act_s.at(i, "v1"))
                    maxima(i, 1)
                pe.wait_ge(act_s.sem, act_s.at(i, "turn1"))
                if new:
                    maxima(i, 2)
                    pe.wait_ge(dve_s.sem, dve_s.at(i, "max1"))
                    maxima(i, 3)
                else:
                    pe_s.skip(pe, i, "max1", "max2", "max3")
                if old:
                    for f in groups:
                        last = pe.matmul(bank[2][:, 0:SEQ], w["wo"][:, f * 128:(f + 1) * 128], oT[:, f, :],
                                         start=(f == 0), stop=(f == 3))
                    last.then_inc(pe_s.sem, 1)
                else:
                    pe_s.skip(pe, i, "wo")
                if new:
                    pe.wait_ge(dve_s.sem, dve_s.at(i, "max3"))
                    for c in range(2):
                        last = pe.transpose(bank[5][0:WHEADS, c * 128:(c + 1) * 128], mx[:, c, :], k.c["ident"])
                    last.then_inc(pe_s.sem, 1)
                else:
                    pe_s.skip(pe, i, "mt")

            trip(0, True, False)
            with pe.Fori(1, BATCH) as i:
                trip(i, True, True)
            trip(BATCH, False, True)

        @block.scalar
        def _(act):
            act_s.prime(act)
            k.load_table(act, EXP_LN)

            def square(i, g):
                act.wait_ge(pe_s.sem, pe_s.at(i, f"proj{g}"))
                act.wait_ge(pe_s.sem, pe_s.before(i, f"ss{g}"))
                act.activation(sq[g], bank[g % 2], ACT.Square).then_inc(act_s.sem, 1)

            def root(i, g):
                act.wait_ge(dve_s.sem, dve_s.at(i, f"clip{g}"))
                act.activation(rs[g % 2], rs[g % 2], ACT.Ln, scale=TINY_SCALE).then_inc(act_s.sem, 1)
                act.wait_ge(act_s.sem, act_s.at(i, f"ln{g}"))
                act.activation(rs[g % 2], rs[g % 2], ACT.Exp, scale=-0.5, bias=k.c64["half_ln"])\
                    .then_inc(act_s.sem, 1)

            def probabilities(i, h):
                act.wait_ge(pe_s.sem, pe_s.at(i, f"s{h}"))
                if h >= 2:
                    act.wait_ge(pe_s.sem, pe_s.at(i, f"pv{h - 2}"))
                act.activation(prob[h % 2], bank[3 + h % 2][:, 0:320], ACT.Exp, scale=8.0).then_inc(act_s.sem, 1)

            def trip(i, new, old):
                if new:
                    act.wait_ge(pe_s.sem, pe_s.before(i, "v1"))
                    act.copy(hb, src[:, tok(i, SEQ)]).then_inc(act_s.sem, 1)
                else:
                    act_s.skip(act, i, "hcopy")
                for what, n in (("sq", 0), ("sq", 1), ("e", 0), ("e", 1), ("root", 0), ("e", 2), ("root", 1), ("e", 3),
                                ("sq", 2), ("e", 4), ("sq", 3), ("e", 5), ("root", 2), ("e", 6), ("root", 3),
                                ("e", 7)):
                    if what == "e":
                        if old:
                            probabilities(i, n)
                        else:
                            act_s.skip(act, i, f"e{n}")
                    elif new:
                        (square if what == "sq" else root)(i, n)
                    elif what == "sq":
                        act_s.skip(act, i, f"sq{n}")
                    else:
                        act_s.skip(act, i, f"ln{n}", f"exp{n}")
                for c in range(2):
                    if new:
                        act.wait_ge(pe_s.sem, pe_s.at(i, f"v{c}"))
                        act.copy(v[:, c, :, 0:WDIM], bank[c].rearrange("p (h d) -> p h d", d=WDIM))\
                            .then_inc(act_s.sem, 1)
                    else:
                        act_s.skip(act, i, f"v{c}")
                for half in range(2):
                    if not old:
                        act_s.skip(act, i, f"turn{half}")
                        continue
                    act.wait_ge(pe_s.sem, pe_s.at(i, f"turn{half}"))
                    if half == 0:
                        act.wait_ge(pe_s.sem, pe_s.before(i, "wo"))
                    act.copy(oT[:, 2 * half:2 * half + 2, :].rearrange("p f t -> p (f t)"), bank[3 + half])\
                        .then_inc(act_s.sem, 1)

            trip(0, True, False)
            with act.Fori(1, BATCH) as i:
                trip(i, True, True)
            trip(BATCH, False, True)

        @block.vector
        def _(dve):
            dve_s.prime(dve)

            def clip(i, g):
                dve.wait_ge(pe_s.sem, pe_s.at(i, f"ss{g}"))
                if g >= 2:
                    dve.wait_ge(dve_s.sem, dve_s.at(i, f"add{g - 2}"))
                    dve.wait_ge(pool_s.sem, pool_s.at(i, f"low{g - 2}"))
                else:
                    dve.wait_ge(pool_s.sem, pool_s.before(i, f"low{g + 2}"))
                dve.tensor_scalar(rs[g % 2], bank[2], TINY, None, ALU.max).then_inc(dve_s.sem, 1)

            def unit_vectors(i, g):
                dve.wait_ge(act_s.sem, act_s.at(i, f"exp{g}"))
                if g >= 2:
                    dve.wait_ge(pe_s.sem, pe_s.at(i, f"rot{g - 2}"))
                    dve.wait_ge(pool_s.sem, pool_s.at(i, f"cos{g - 2}"))
                for m, scale in ((0, w["qs"]), (1, w["ks"])):
                    cols = slice(m * SEQ, (m + 1) * SEQ)
                    last = dve.scalar_tensor_tensor(out=flat[g % 2][:, cols], in0=bank[g % 2][:, cols], scalar=scale,
                                                    in1=rs[g % 2][:, cols], op0=ALU.mult, op1=ALU.mult)
                last.then_inc(dve_s.sem, 1)

            def rotary(i, g):
                dve.wait_ge(pe_s.sem, pe_s.at(i, f"rot{g}"))
                dve.wait_ge(dve_s.sem, dve_s.at(i, f"nrm{g}"))
                dve.tensor_tensor(rs[g % 2], bank[2], tables["sin"], ALU.mult).then_inc(dve_s.sem, 1)

            def turned(i, g):
                dve.wait_ge(dve_s.sem, dve_s.at(i, f"sin{g}"))
                dve.wait_ge(pool_s.sem, pool_s.at(i, f"cos{g}"))
                dve.wait_ge(pe_s.sem, pe_s.at(i, f"s{2 * g + 1}"))
                dve.tensor_tensor(flat8(g), cosd[g % 2], rs[g % 2], ALU.add).then_inc(dve_s.sem, 1)

            def trip(i, new, old):
                if new:
                    for a in (0, 2):
                        clip(i, a)
                        clip(i, a + 1)
                        unit_vectors(i, a)
                        unit_vectors(i, a + 1)
                        rotary(i, a)
                        if a == 0:
                            turned(i, 0)
                        rotary(i, a + 1)
                        if a == 0:
                            turned(i, 1)
                else:
                    dve_s.skip(dve, i, *dve_steps[0:dve_steps.index("recip")])
                if old:
                    dve.wait_ge(pe_s.sem, pe_s.at(i, f"pv{WHEADS - 1}"))
                    for b, n in ((5, 6), (6, 6), (7, 4)):
                        o = bank[b][:, 0:65 * n].rearrange("p (n d) -> p n d", d=65)
                        last = dve.reciprocal(recip[:, 6 * (b - 5):6 * (b - 5) + n], o[:, :, WDIM])
                    last.then_inc(dve_s.sem, 1)
                    dve.wait_ge(dve_s.sem, dve_s.at(i, "recip"))
                    dve.wait_ge(pe_s.sem, pe_s.before(i, "turn1"))
                    for b, n in ((5, 6), (6, 6), (7, 4)):
                        for c in range(2):
                            o = bank[b][:, 0:65 * n].rearrange("p (h c d) -> p h c d", c=2, d=65)[:, :, c, 0:WDIM]
                            r = recip[:, 6 * (b - 5):6 * (b - 5) + n].rearrange("p (h c) -> p h c", c=2)[:, :, c]
                            last = dve.tensor_tensor(ob[:, c, 3 * (b - 5):3 * (b - 5) + n // 2, :], o,
                                                     r.unsqueeze(2).to_broadcast([128, n // 2, WDIM]), ALU.mult)
                    last.then_inc(dve_s.sem, 1)
                else:
                    dve_s.skip(dve, i, "recip", "norm")
                if new:
                    for f in groups:
                        if f == 0:
                            dve.wait_ge(pe_s.sem, pe_s.before(i, "mt"))
                        if f == 1:
                            turned(i, 2)
                            turned(i, 3)
                        dve.wait_ge(pe_s.sem, pe_s.at(i, f"max{f}"))
                        two = mbanks[f]
                        dve.tensor_reduce(mx[:, 0, 2 * f:2 * f + 2], two[:, :, 0:128], AX_X, ALU.max)
                        dve.tensor_reduce(mx[:, 1, 2 * f:2 * f + 2], two[:, :, 128:320], AX_X, ALU.max)\
                            .then_inc(dve_s.sem, 1)
                else:
                    dve_s.skip(dve, i, *dve_steps[dve_steps.index("max0"):dve_steps.index("sum")])
                if old:
                    dve.wait_ge(pe_s.sem, pe_s.at(i, "wo"))
                    dve.tensor_tensor(y_padded[:, tok(i, SEQ)], bank[2][:, 0:SEQ], y_padded[:, tok(i, SEQ)], ALU.add)\
                        .then_inc(dve_s.sem, 1)
                else:
                    dve_s.skip(dve, i, "sum")
                if new:
                    dve.wait_ge(pe_s.sem, pe_s.at(i, "mt"))
                    dve.tensor_scalar(shift[0:WHEADS, :], bank[5][0:WHEADS, 0:SEQ], -1.0, None, ALU.mult)\
                        .then_inc(dve_s.sem, 1)
                else:
                    dve_s.skip(dve, i, "shift")

            trip(0, True, False)
            with dve.Fori(1, BATCH) as i:
                trip(i, True, True)
            trip(BATCH, False, True)

        @block.gpsimd
        def _(pool):
            pool_s.prime(pool)

            def cosine(i, g):
                pool.wait_ge(dve_s.sem, dve_s.at(i, f"nrm{g}"))
                if g >= 2:
                    pool.wait_ge(dve_s.sem, dve_s.at(i, f"add{g - 2}"))
                pool.tensor_tensor(cosd[g % 2], flat[g % 2], tables["cos"], ALU.mult).then_inc(pool_s.sem, 1)

            def low(i, g):
                pool.wait_ge(pool_s.sem, pool_s.at(i, f"cos{g}"))
                pool.wait_ge(dve_s.sem, dve_s.at(i, f"sin{g}"))
                if g == 0:
                    pool.wait_ge(pe_s.sem, pe_s.before(i, "max3"))
                pool.tensor_tensor(qkb[:, 2 * g:2 * g + 2, :].rearrange("p f t -> p (f t)"), cosd[g % 2],
                                   rs[g % 2], ALU.add).then_inc(pool_s.sem, 1)

            def trip(i):
                for g in (0, 2):
                    cosine(i, g)
                    cosine(i, g + 1)
                    low(i, g)
                    low(i, g + 1)

            trip(0)
            with pool.Fori(1, BATCH) as i:
                trip(i)
            pool_s.skip(pool, BATCH, *pool_steps)


def l0_ffn(k, name, w):
    norm_stage(k, f"{name}_ln", k.X, [(k.Y, None, None)], True, "eps5")
    zero_stage(k, f"{name}_pad", [(k.Y_padded[:, 0:SEQ], 0.0)])
    k.c64 = {n: w[n] for n in ("head_sum", "rot", "half_ln")}
    k.cb64 = {n: w[n].bitcast(BF16) for n in ("band_qk", "band_kq")}
    tables = {n: w[n] for n in ("sin", "cos")}
    for layer in range(2):
        s = f"{name}_{layer}"
        lw = {n[:-1]: a for n, a in w.items() if n.endswith(str(layer))}
        shift_stage(k, f"{s}_shift1", k.Y, k.H)
        window_attention_stage(k, f"{s}_attn", k.H, k.Y_padded, lw, tables)
        shift_stage(k, f"{s}_shift2", k.Y, k.H)
        norm_stage(k, f"{s}_norm", k.H, [(k.Z, lw["lg"], lw["lb"])], True, "eps5")
        gated_mlp_stage(k, f"{s}_mlp", k.Z, [128, 128, 85], lw["w_lin"], lw["w_act"], lw["b_lin"], lw["b_act"],
                        lw["w_out"], ACT.Gelu, GELU_SET, k.Y, k.Y, lw["b_out"])
    add_stage(k, f"{name}_add", k.Y, k.X)


def l0_ffn_group(i):
    A = "L0_ffn_"
    f = np.float32
    g = {}
    for layer in range(2):
        w1, b1, w2 = i[A + "w1"][layer], i[A + "b1"][layer], i[A + "w2"][layer]
        hid = w2.shape[0]

        def rows(a):
            out = np.zeros((128, 3, a.shape[1]), a.dtype)
            for n in range(3):
                part = a[n * 128:(n + 1) * 128]
                out[0:part.shape[0], n] = part
            return out

        g[f"wqkv{layer}"] = i[A + "wqkv"][layer]
        g[f"wo{layer}"] = i[A + "wo"][layer].reshape(4, 128, 128).transpose(1, 0, 2)
        g[f"w_lin{layer}"], g[f"w_act{layer}"] = w1[:, 0:hid], w1[:, hid:]
        g[f"w_out{layer}"] = rows(w2)
        g[f"b_lin{layer}"], g[f"b_act{layer}"] = rows(column(b1[0:hid])), rows(column(b1[hid:]))
        g[f"b_out{layer}"] = column(i[A + "b2"][layer])
        g[f"qs{layer}"] = column(np.tile(i[A + "q_scale"][layer], 2))
        g[f"ks{layer}"] = column(np.tile(i[A + "k_scale"][layer], 2))
        g[f"lg{layer}"], g[f"lb{layer}"] = column(i[A + "ln_g"][layer]), column(i[A + "ln_b"][layer])
    feature = np.arange(128)
    g["head_sum"] = (feature[:, None] // 64 == feature[None, :] // 64).astype(f)
    g["rot"] = rotation(64, False)
    g["half_ln"] = np.full((128, 1), 0.5 * np.log(TINY_SCALE), f)
    half_idx = np.arange(0, 64, 2, dtype=f)
    inv = (1.0 / 10000.0 ** (half_idx / f(64))).astype(f)
    t = np.arange(SEQ, dtype=f)
    freqs = (t[:, None] * inv[None, :]).astype(f)
    base = ((half_idx + f(0.4 * 64)) / f(1.4 * 64)).astype(f)
    power = ((t - SEQ // 2) / f(32.0)).astype(f)
    scale = (base[None, :] ** power[:, None]).astype(f)

    def table(a):
        return np.tile(np.concatenate([a, a], 1).T, (2, 1)).astype(f)

    g["cos"] = np.concatenate([table(np.cos(freqs) * scale), table(np.cos(freqs) / scale)], 1)
    g["sin"] = np.concatenate([table(np.sin(freqs) * scale), table(np.sin(freqs) / scale)], 1)
    p, c = np.arange(128)[:, None], np.arange(320)[None, :]
    d = np.where(c < 128, p - c, 64 + p - (c - 128))
    band_qk = np.where((d >= 0) & (d <= 64), 0, NEG)
    d = np.where(c < 192, c - p, c - 192 - p)
    band_kq = np.where((d >= 0) & (d <= 64), 0, NEG)
    for n, m in (("band_qk", band_qk), ("band_kq", band_kq)):
        g[n] = bf16_pairs(m)
    return g


FEATURES = 64
RF_EPS = 1e-6


def random_feature_stage(k, name, z, w, out):
    nc = k.nc
    wide = HEADS * FEATURES
    trips = BATCH + 1
    pe_s = Steps(k, "products", ["q", "k", "t0", "v", "t1", "h2", "lk0", "lk1", "n", "mt", "z", "mb", "lq0", "o", "lq1",
                                 "turn"], trips)
    act_s = Steps(k, "lookups", ["eq0", "copy", "q", "k", "k2", "eq1", "t0", "t1", "v", "ek0", "ek1", "out"], trips)
    dve_s = Steps(k, "vectors", ["h2", "mk0", "mk1", "mks", "mk", "nn", "m1", "diag", "eps", "m", "sk0", "sk1", "mq0",
                                 "sq0", "recip", "ctx", "mq1", "sq1"], trips)
    k.arena.reset()
    take = k.arena.take
    zt, qf, kf, k2 = take(SEQ), take(SEQ), take(SEQ), take(SEQ)
    v = take(2 * HEADS * VCOLS).rearrange("p (c h d) -> p c h d", c=2, h=HEADS)
    ak = [take(wide) for _ in range(2)]
    pq = [take(wide) for _ in range(2)]
    pT = [take(wide) for _ in range(2)]
    mk = take(2 * HEADS).rearrange("p (c h) -> p c h", c=2)
    mq = take(2 * HEADS).rearrange("p (c h) -> p c h", c=2)
    h2 = take(2 * HEADS).rearrange("p (c h) -> p c h", c=2)
    m = take(2 * HEADS).rearrange("p (c h) -> p c h", c=2)
    mkb, m1, diag = take(HEADS), take(1), take(HEADS)
    nn = take(8 * 18).rearrange("p (a c) -> p a c", a=8)
    recip = take(2 * HEADS).rearrange("p (c h) -> p c h", c=2)
    ctx = take(SEQ).rearrange("p (c f) -> p c f", c=2)
    bank = [k.psum[:, n, :] for n in range(8)]
    nbank = bank[6][:, 0:144].rearrange("p (a c) -> p a c", a=8)
    zbank = bank[6][:, 144:160]
    hbank = bank[7][:, 288:320].rearrange("p (c h) -> p c h", c=2)
    obank = bank[7][:, 0:288].rearrange("p (c h d) -> p c h d", c=2, h=HEADS)
    sums = nn.rearrange("p a (b c) -> p (a b) c", b=2)[:, :, HEAD_DIM]

    def logits(c):
        return k.psum[:, 2 + 2 * c:4 + 2 * c, :]

    def by_head(ap):
        return ap.rearrange("p (h f) -> p h f", f=FEATURES)

    def logits_by_head(c):
        return logits(c).rearrange("p a (h f) -> p (a h) f", f=FEATURES)

    def spread(ap):
        return ap.unsqueeze(2).to_broadcast([128, HEADS, FEATURES])

    fills = [(v.rearrange("p c h d -> p (c h d)"), 1.0)] + [(buf, 1.0) for buf in ak + pq]
    filled = Count(k, "filled", len(fills))
    with nc.Block() as block:
        @block.vector
        def _(dve):
            for buf, value in fills:
                dve.memset(buf, value).then_inc(filled.sem, 1)
            dve.wait_ge(filled.sem, filled.at(len(fills)))

    with nc.Block() as block:
        @block.tensor
        def _(pe):
            pe_s.prime(pe)

            def feature_logits(x, c):
                for a in range(2):
                    cols = slice(512 * a, 512 * a + 512)
                    last = pe.matmul(logits(c)[:, a, :], x[:, c * 128:(c + 1) * 128], w["wrf"][:, cols],
                                     start=True, stop=True)
                last.then_inc(pe_s.sem, 1)

            def turn_features(c):
                for p in range(8):
                    last = pe.transpose(logits(c)[:, p // 4, (p % 4) * 128:(p % 4 + 1) * 128],
                                        pq[c][:, p * 128:(p + 1) * 128], k.c["ident"])
                last.then_inc(pe_s.sem, 1)

            with pe.Fori(0, trips) as i:
                pe.wait_ge(act_s.sem, act_s.before(i, "k2"))
                pe.wait_ge(dve_s.sem, dve_s.before(i, "m"))
                pe.matmul(bank[0][:, 0:SEQ], w["wq"], z[:, tok(i, SEQ)], start=True, stop=True).then_inc(pe_s.sem, 1)
                pe.matmul(bank[0][:, SEQ:2 * SEQ], w["wk"], z[:, tok(i, SEQ)], start=True, stop=True)\
                    .then_inc(pe_s.sem, 1)
                pe.wait_ge(act_s.sem, act_s.at(i, "eq0"))
                turn_features(0)
                pe.wait_ge(act_s.sem, act_s.at(i, "copy"))
                for c in range(2):
                    to = bank[1][:, c * 128:(c + 1) * 128]
                    pe.matmul(to, zt[:, c * 128:(c + 1) * 128], w["wv"], start=True, stop=False)
                    last = pe.matmul(to, k.c["ones"][0:1, :], w["bv"][0:1, :], start=False, stop=True)
                last.then_inc(pe_s.sem, 1)
                pe.wait_ge(act_s.sem, act_s.at(i, "eq1"))
                turn_features(1)
                for c in range(2):
                    last = pe.matmul(hbank[:, c, :], k2[:, c * 128:(c + 1) * 128], w["half_square"],
                                     start=True, stop=True)
                last.then_inc(pe_s.sem, 1)
                for c in range(2):
                    pe.wait_ge(act_s.sem, act_s.at(i, f"t{c}"))
                    feature_logits(kf, c)
                    pe.wait_ge(act_s.sem, act_s.before(i, "ek1"))
                    for p in range(4 * c, 4 * c + 4):
                        for c2 in range(2):
                            last = pe.matmul(nbank[:, p, :], ak[c2][:, p * 128:(p + 1) * 128],
                                             v[:, c2, 2 * p:2 * p + 2, :].rearrange("p h d -> p (h d)"),
                                             start=(c2 == 0), stop=(c2 == 1))
                last.then_inc(pe_s.sem, 1)
                pe.wait_ge(dve_s.sem, dve_s.at(i, "mk"))
                pe.transpose(bank[0][0:HEADS, 0:128], mkb, k.c["ident"]).then_inc(pe_s.sem, 1)
                pe.wait_ge(dve_s.sem, dve_s.at(i, "nn"))
                pe.matmul(zbank, w["eps_sum"], sums, start=True, stop=True).then_inc(pe_s.sem, 1)
                pe.wait_ge(dve_s.sem, dve_s.at(i, "diag"))
                pe.matmul(bank[0][:, 128:144], k.c["ones"][0:HEADS, :], diag[0:HEADS, :], start=True, stop=True)\
                    .then_inc(pe_s.sem, 1)
                pe.wait_ge(dve_s.sem, dve_s.at(i, "eps"))
                for c in range(2):
                    for p in range(8):
                        last = pe.matmul(obank[:, c, 2 * p:2 * p + 2, :].rearrange("p h d -> p (h d)"),
                                         pT[c][:, p * 128:(p + 1) * 128], nn[:, p, :], start=True, stop=True)
                    if c == 1:
                        last.then_inc(pe_s.sem, 1)
                    pe.wait_ge(dve_s.sem, dve_s.at(i, f"sk{c}"))
                    feature_logits(qf, c)
                pe.wait_ge(dve_s.sem, dve_s.at(i, "ctx"))
                pe.wait_ge(act_s.sem, act_s.at(i, "v"))
                for c in range(2):
                    last = pe.transpose(bank[1][:, SEQ + c * 128:SEQ + (c + 1) * 128], ctx[:, c, :], k.c["ident"])
                last.then_inc(pe_s.sem, 1)

        @block.scalar
        def _(act):
            act_s.prime(act)
            k.load_table(act, EXP_LN)

            def query_features(i, c):
                act.wait_ge(dve_s.sem, dve_s.before(i, f"sq{c}"))
                act.activation(pq[c], pq[c], ACT.Exp).then_inc(act_s.sem, 1)

            with act.Fori(0, trips) as i:
                query_features(i, 0)
                act.wait_ge(pe_s.sem, pe_s.before(i, "v"))
                act.copy(zt, z[:, tok(i, SEQ)]).then_inc(act_s.sem, 1)
                act.wait_ge(pe_s.sem, pe_s.at(i, "k"))
                act.wait_ge(pe_s.sem, pe_s.before(i, "lq1"))
                act.activation(qf, bank[0][:, 0:SEQ], ACT.Identity, bias=w["bq"]).then_inc(act_s.sem, 1)
                act.activation(kf, bank[0][:, SEQ:2 * SEQ], ACT.Identity, bias=w["bk"]).then_inc(act_s.sem, 1)
                act.activation(k2, bank[0][:, SEQ:2 * SEQ], ACT.Square, bias=w["bk"]).then_inc(act_s.sem, 1)
                query_features(i, 1)
                for c in range(2):
                    act.wait_ge(pe_s.sem, pe_s.at(i, f"t{c}"))
                    act.wait_ge(pe_s.sem, pe_s.before(i, "o"))
                    act.copy(pT[c].rearrange("p (a t) -> p a t", a=2), logits(c)).then_inc(act_s.sem, 1)
                act.wait_ge(pe_s.sem, pe_s.at(i, "v"))
                act.wait_ge(pe_s.sem, pe_s.at(i, "n"))
                act.copy(v[:, :, :, 0:HEAD_DIM],
                         bank[1][:, 0:SEQ].rearrange("p (c h d) -> p c h d", c=2, d=HEAD_DIM)).then_inc(act_s.sem, 1)
                for c in range(2):
                    act.wait_ge(dve_s.sem, dve_s.at(i, f"sk{c}"))
                    act.activation(ak[c], ak[c], ACT.Exp).then_inc(act_s.sem, 1)
                act.wait_ge(pe_s.sem, pe_s.at(i, "turn"))
                act.copy(out[:, tok(i, SEQ)], bank[1][:, SEQ:2 * SEQ]).then_inc(act_s.sem, 1)

        @block.vector
        def _(dve):
            dve_s.prime(dve)

            def shift_queries(i, c):
                dve.wait_ge(pe_s.sem, pe_s.at(i, f"lq{c}"))
                dve.tensor_reduce(mq[:, c, :], logits_by_head(c), AX_X, ALU.max).then_inc(dve_s.sem, 1)
                dve.wait_ge(dve_s.sem, dve_s.at(i, f"mq{c}"))
                dve.tensor_tensor(by_head(pq[c]), logits_by_head(c), spread(mq[:, c, :]), ALU.subtract)\
                    .then_inc(dve_s.sem, 1)

            with dve.Fori(0, trips) as i:
                dve.wait_ge(pe_s.sem, pe_s.at(i, "h2"))
                dve.tensor_copy(h2, hbank).then_inc(dve_s.sem, 1)
                for c in range(2):
                    dve.wait_ge(pe_s.sem, pe_s.at(i, f"lk{c}"))
                    dve.tensor_reduce(mk[:, c, :], logits_by_head(c), AX_X, ALU.max).then_inc(dve_s.sem, 1)
                dve.wait_ge(dve_s.sem, dve_s.at(i, "mk1"))
                dve.tensor_tensor(mk, mk, h2, ALU.add).then_inc(dve_s.sem, 1)
                dve.wait_ge(dve_s.sem, dve_s.at(i, "mks"))
                dve.tensor_tensor(mkb, mk[:, 0, :], mk[:, 1, :], ALU.max).then_inc(dve_s.sem, 1)
                dve.wait_ge(pe_s.sem, pe_s.at(i, "n"))
                dve.tensor_tensor(nn, nbank, w["own_head"].unsqueeze(1).to_broadcast([128, 8, 18]), ALU.mult)\
                    .then_inc(dve_s.sem, 1)
                dve.wait_ge(pe_s.sem, pe_s.at(i, "mt"))
                dve.tensor_reduce(m1[0:HEADS, :], bank[0][0:HEADS, 0:128], AX_X, ALU.max).then_inc(dve_s.sem, 1)
                dve.wait_ge(dve_s.sem, dve_s.at(i, "m1"))
                dve.tensor_scalar(diag[0:HEADS, :], k.c["ident"][0:HEADS, 0:HEADS], m1[0:HEADS, :], None, ALU.mult)\
                    .then_inc(dve_s.sem, 1)
                dve.wait_ge(pe_s.sem, pe_s.at(i, "z"))
                dve.tensor_tensor(sums, zbank, sums, ALU.add).then_inc(dve_s.sem, 1)
                dve.wait_ge(pe_s.sem, pe_s.at(i, "mb"))
                dve.tensor_tensor(m, bank[0][:, 128:144].unsqueeze(1).to_broadcast([128, 2, HEADS]), h2,
                                  ALU.subtract).then_inc(dve_s.sem, 1)
                dve.wait_ge(dve_s.sem, dve_s.at(i, "m"))
                for c in range(2):
                    dve.tensor_tensor(by_head(ak[c]), logits_by_head(c), spread(m[:, c, :]), ALU.subtract)\
                        .then_inc(dve_s.sem, 1)
                shift_queries(i, 0)
                dve.wait_ge(pe_s.sem, pe_s.at(i, "o"))
                dve.reciprocal(recip, obank[:, :, :, HEAD_DIM]).then_inc(dve_s.sem, 1)
                dve.wait_ge(dve_s.sem, dve_s.at(i, "recip"))
                dve.wait_ge(pe_s.sem, pe_s.before(i, "turn"))
                for c in range(2):
                    last = dve.tensor_tensor(ctx[:, c, :].rearrange("p (h d) -> p h d", d=HEAD_DIM),
                                             obank[:, c, :, 0:HEAD_DIM],
                                             recip[:, c, :].unsqueeze(2).to_broadcast([128, HEADS, HEAD_DIM]),
                                             ALU.mult)
                last.then_inc(dve_s.sem, 1)
                shift_queries(i, 1)


def l1_attn_b(k, name, w):
    norm_stage(k, f"{name}_ln", k.X, [(k.H, None, None)], True, "eps5")
    zero_stage(k, f"{name}_pad", [(k.H[:, TOKENS:TOKENS + SEQ], 0.0)])
    random_feature_stage(k, name, k.H, w, k.Y_padded)
    output_stage(k, f"{name}_out", [(w["wo"], k.Y, 0)], k.X, k.X, bias=w["bo"])


def l1_attn_b_group(i):
    A, f = "L1_attn_b_", np.float32
    wrf = np.zeros((HEADS, HEAD_DIM, HEADS, FEATURES), f)
    for h in range(HEADS):
        wrf[h, :, h] = i[A + "Wrf"][0, h]
    feature, head = np.arange(128)[:, None], np.arange(HEADS)[None, :]
    half = np.arange(128) // 64
    return {"wq": i[A + "Wq"].T, "wk": i[A + "Wk"].T, "wv": i[A + "Wv"].T, "wo": i[A + "Wo"].T,
            "bq": column(i[A + "bq"]), "bk": column(i[A + "bk"]), "bv": i[A + "bv"].reshape(1, -1),
            "bo": column(i[A + "bo"]), "wrf": wrf.reshape(128, -1),
            "half_square": np.where(feature // HEAD_DIM == head, -0.5, 0).astype(f),
            "eps_sum": np.where(half[:, None] == half[None, :], RF_EPS, 0).astype(f),
            "own_head": (half[:, None] == np.arange(18)[None, :] // VCOLS).astype(f)}


QUARTER = 4 * SEQ
QUARTERS = TOKENS // QUARTER
STATE = 128


def ssm_gates_stage(k, name, xn, w, B, C, U):
    nc = k.nc
    pe_s = Steps(k, "products", ["sel", "b", "c", "imp", "gate"], TILES)
    act_s = Steps(k, "sigmoids", ["sel", "imp", "gate"], TILES)
    dve_s = Steps(k, "gated", ["x2", "b", "c", "u"], TILES)
    take = k.arena.take
    sel, x2, imp, gate = take(TILE), take(TILE), take(TILE), take(TILE)
    sel_bias = take(1)
    ready = Count(k, "filled", 1)
    bank = [k.psum[:, n, :] for n in range(5)]
    with nc.Block() as block:
        @block.vector
        def _(dve):
            dve.tensor_tensor(sel_bias, w["bsel"], w["sel_gate"], ALU.mult).then_inc(ready.sem, 1)
            dve.wait_ge(ready.sem, ready.at(1))

    with nc.Block() as block:
        @block.tensor
        def _(pe):
            pe_s.prime(pe)
            with pe.Fori(0, TILES) as i:
                x = xn[:, tok(i, TILE)]
                pe.wait_ge(act_s.sem, act_s.before(i, "sel"))
                pe.matmul(bank[0], w["wsel"], x, start=True, stop=True).then_inc(pe_s.sem, 1)
                pe.wait_ge(dve_s.sem, dve_s.before(i, "c"))
                pe.matmul(bank[1], w["wx"][:, 64:192], x, start=True, stop=True).then_inc(pe_s.sem, 1)
                pe.matmul(bank[2], w["wx"][:, 192:320], x, start=True, stop=True).then_inc(pe_s.sem, 1)
                pe.wait_ge(dve_s.sem, dve_s.at(i, "x2"))
                pe.wait_ge(act_s.sem, act_s.before(i, "gate"))
                pe.matmul(bank[3], w["wimp"], x2, start=True, stop=True).then_inc(pe_s.sem, 1)
                pe.matmul(bank[4], w["wg"], x2, start=True, stop=True).then_inc(pe_s.sem, 1)

        @block.scalar
        def _(act):
            act_s.prime(act)
            k.load_table(act, SIGMOID_SET)
            with act.Fori(0, TILES) as i:
                act.wait_ge(pe_s.sem, pe_s.at(i, "sel"))
                act.wait_ge(dve_s.sem, dve_s.before(i, "x2"))
                act.activation(sel, bank[0], ACT.Sigmoid, scale=w["sel_gate"], bias=sel_bias).then_inc(act_s.sem, 1)
                act.wait_ge(pe_s.sem, pe_s.at(i, "imp"))
                act.wait_ge(dve_s.sem, dve_s.before(i, "c"))
                act.activation(imp, bank[3], ACT.Sigmoid, bias=w["bimp"]).then_inc(act_s.sem, 1)
                act.wait_ge(pe_s.sem, pe_s.at(i, "gate"))
                act.wait_ge(dve_s.sem, dve_s.before(i, "u"))
                act.activation(gate, bank[4], ACT.Sigmoid, bias=w["bg"]).then_inc(act_s.sem, 1)

        @block.vector
        def _(dve):
            dve_s.prime(dve)
            with dve.Fori(0, TILES) as i:
                dve.wait_ge(act_s.sem, act_s.at(i, "sel"))
                dve.wait_ge(pe_s.sem, pe_s.before(i, "gate"))
                dve.wait_ge(dve_s.sem, dve_s.before(i, "u"))
                dve.tensor_tensor(x2, xn[:, tok(i, TILE)], sel, ALU.mult).then_inc(dve_s.sem, 1)
                dve.wait_ge(act_s.sem, act_s.at(i, "imp"))
                dve.wait_ge(pe_s.sem, pe_s.at(i, "c"))
                dve.tensor_tensor(B[:, tok(i, TILE)], bank[1], imp, ALU.mult).then_inc(dve_s.sem, 1)
                dve.tensor_tensor(C[:, tok(i, TILE)], bank[2], imp, ALU.mult).then_inc(dve_s.sem, 1)
                dve.wait_ge(act_s.sem, act_s.at(i, "gate"))
                dve.wait_ge(dve_s.sem, dve_s.at(i, "x2"))
                dve.tensor_tensor(U[:, tok(i, TILE)], x2, gate, ALU.mult).then_inc(dve_s.sem, 1)


def ssm_delta_stage(k, name, xn, w, U):
    nc = k.nc
    pe_s = Steps(k, "products", ["dr", "dl"], TILES)
    act_s = Steps(k, "lookups", ["dr", "abs", "exp", "ln"], TILES)
    dve_s = Steps(k, "delta", ["max", "delta", "u"], TILES)
    at = k.arena.used
    take = k.arena.take
    dr, small, pos = take(TILE), take(TILE), take(TILE)
    with nc.Block() as block:
        @block.tensor
        def _(pe):
            pe_s.prime(pe)
            with pe.Fori(0, TILES) as i:
                pe.wait_ge(act_s.sem, act_s.before(i, "dr"))
                pe.matmul(k.psum[0:64, 0, :], w["wx"][:, 0:64], xn[:, tok(i, TILE)], start=True, stop=True)\
                    .then_inc(pe_s.sem, 1)
                pe.wait_ge(act_s.sem, act_s.at(i, "dr"))
                pe.wait_ge(dve_s.sem, dve_s.before(i, "max"))
                pe.matmul(k.psum[:, 1, :], w["wdt"][0:64, :], dr[0:64, :], start=True, stop=True)\
                    .then_inc(pe_s.sem, 1)

        @block.scalar
        def _(act):
            act_s.prime(act)
            k.load_table(act, EXP_LN)
            with act.Fori(0, TILES) as i:
                act.wait_ge(pe_s.sem, pe_s.at(i, "dr"))
                act.copy(dr[0:64, :], k.psum[0:64, 0, :]).then_inc(act_s.sem, 1)
                act.wait_ge(pe_s.sem, pe_s.at(i, "dl"))
                act.wait_ge(dve_s.sem, dve_s.before(i, "delta"))
                act.activation(small, k.psum[:, 1, :], ACT.Abs, bias=w["bdt"]).then_inc(act_s.sem, 1)
                act.wait_ge(act_s.sem, act_s.at(i, "abs"))
                act.activation(small, small, ACT.Exp, scale=-1.0).then_inc(act_s.sem, 1)
                act.wait_ge(act_s.sem, act_s.at(i, "exp"))
                act.activation(small, small, ACT.Ln, bias=1.0).then_inc(act_s.sem, 1)

        @block.vector
        def _(dve):
            dve_s.prime(dve)
            with dve.Fori(0, TILES) as i:
                dve.wait_ge(act_s.sem, act_s.at(i, "abs"))
                dve.wait_ge(dve_s.sem, dve_s.before(i, "delta"))
                dve.tensor_scalar(pos, k.psum[:, 1, :], w["bdt"], 0.0, ALU.add, ALU.max).then_inc(dve_s.sem, 1)
                dve.wait_ge(act_s.sem, act_s.at(i, "ln"))
                dve.wait_ge(dve_s.sem, dve_s.at(i, "max"))
                dve.tensor_tensor(xn[:, tok(i, TILE)], pos, small, ALU.add).then_inc(dve_s.sem, 1)
                dve.wait_ge(dve_s.sem, dve_s.at(i, "delta"))
                dve.tensor_tensor(U[:, tok(i, TILE)], U[:, tok(i, TILE)], xn[:, tok(i, TILE)], ALU.mult)\
                    .then_inc(dve_s.sem, 1)
    k.arena.used = at


def scan_stage(k, name, xh, w, cst, delta, B, C, U, big):
    nc = k.nc
    pe_in = Steps(k, "spread", [f"{s}{u}" for u in (0, 1) for s in ("bd", "bu", "y")], 64 * QUARTERS)
    act_in = Steps(k, "decays", ["da0", "da1", "e0", "e1"], 64 * QUARTERS)
    dve_in = Steps(k, "scans", [f"{s}{u}" for u in (0, 1) for s in ("bx", "h")], 64 * QUARTERS)
    pool_in = Steps(k, "read_out", ["hc0", "hc1"], 64 * QUARTERS)
    splits = [f"{s}{n}" for s in ("d", "u") for n in ("t1", "r1", "t2", "r2", "t3", "s")]
    pe_q = Steps(k, "quarter_sums", ["init", "last"], QUARTERS)
    act_q = Steps(k, "quarter_taken", ["c", "y"], QUARTERS)
    dve_q = Steps(k, "quarter_split", splits, QUARTERS)
    pool_q = Steps(k, "quarter_zero", ["zero"], QUARTERS)
    take = k.arena.take
    DS = k.arena.take_bf16(4 * QUARTER)
    US = k.arena.take_bf16(4 * QUARTER)
    da = [take(QUARTER) for _ in range(2)]
    bx = [big.take(QUARTER) for _ in range(2)]
    hc = [big.take(QUARTER) for _ in range(2)]
    cq = big.take(QUARTER)
    onehot = [big.take(128) for _ in range(2)]
    diag, neg_a = big.take(128), big.take(128)
    zero_column = big.take(1)
    nothing = zero_column.to_broadcast([128, QUARTER])
    rest, low = bx[0], bx[1][:, 0:QUARTER // 2].bitcast(BF16)
    pick = cst["pick"].bitcast(BF16)
    delta_bank = [k.psum[:, 0:2, :], k.psum[:, 6:8, :]]
    u_bank, y_bank = k.psum[:, 2:4, :], k.psum[:, 4:6, :]
    prep = Count(k, "prepared", 2)
    with nc.Block() as block:
        @block.scalar
        def _(act):
            k.load_table(act, EXP_LN)
            act.activation(neg_a, w["a_log"], ACT.Exp).then_inc(prep.sem, 1)

        @block.vector
        def _(dve):
            dve.tensor_scalar(diag, k.c["ident"], w["dp"], None, ALU.mult)
            dve.memset(zero_column, 0.0)
            for u in range(2):
                dve.memset(da[u], 0.0)
                dve.memset(onehot[u], 0.0)
            dve.wait_ge(prep.sem, prep.at(1))
            dve.tensor_scalar(neg_a, neg_a, -1.0, None, ALU.mult).then_inc(prep.sem, 1)
            dve.wait_ge(prep.sem, prep.at(2))

    with nc.Block() as block:
        @block.tensor
        def _(pe):
            for s in (pe_in, pe_q):
                s.prime(pe)
            with pe.Fori(0, QUARTERS) as q:
                pe.wait_ge(act_q.sem, act_q.before(q, "y"))
                pe.wait_ge(dve_q.sem, dve_q.at(q, "us"))
                pe.wait_ge(pool_q.sem, pool_q.at(q, "zero"))
                for h in range(2):
                    last = pe.matmul(y_bank[:, h, :], diag, xh[:, bass.ds(q * QUARTER + h * TILE, TILE)],
                                     start=True, stop=True)
                last.then_inc(pe_q.sem, 1)

                def spread(bank, src, u, g, j):
                    for h in range(2):
                        last = pe.matmul(bank[:, h, :], pick[0:96, bass.ds(j * 256 + u * 128, 128)],
                                         src[0:96, bass.ds(g * QUARTER + h * TILE, TILE)], start=True, stop=True)
                    last.then_inc(pe_in.sem, 1)

                def read_out(u):
                    for h in range(2):
                        last = pe.matmul(y_bank[:, h, :], onehot[u], hc[u][:, h * TILE:(h + 1) * TILE],
                                         start=False, stop=True, skip_group_check=True)
                    return last

                with pe.Fori(0, 4) as g:
                    with pe.Fori(0, 16) as j:
                        t = q * 64 + g * 16 + j
                        for u in range(2):
                            pe.wait_ge(act_in.sem, act_in.before(t, f"da{u}"))
                            spread(delta_bank[u], DS, u, g, j)
                            pe.wait_ge(dve_in.sem, dve_in.at(t, "bx0") if u else dve_in.before(t, "bx1"))
                            spread(u_bank, US, u, g, j)
                            pe.wait_ge(pool_in.sem, pool_in.before(t, f"hc{u}"))
                            pe.wait_ge(act_in.sem, act_in.before(t, f"e{u}"))
                            read_out(u).then_inc(pe_in.sem, 1)
                pe.wait_ge(pool_in.sem, pool_in.before(q * 64 + 64, "hc1"))
                pe.wait_ge(act_in.sem, act_in.before(q * 64 + 64, "e1"))
                read_out(0)
                read_out(1).then_inc(pe_q.sem, 1)

        @block.scalar
        def _(act):
            for s in (act_in, act_q):
                s.prime(act)
            k.load_table(act, EXP_LN)
            with act.Fori(0, QUARTERS) as q:
                act.wait_ge(pool_in.sem, pool_in.before(q * 64, "hc1"))
                act.copy(cq, C[:, bass.ds(q * QUARTER, QUARTER)]).then_inc(act_q.sem, 1)
                with act.Fori(0, 4) as g:
                    with act.Fori(0, 16) as j:
                        t = q * 64 + g * 16 + j
                        for u in range(2):
                            act.wait_ge(pe_in.sem, pe_in.at(t, f"bd{u}"))
                            act.wait_ge(dve_in.sem, dve_in.before(t, f"h{u}"))
                            act.activation(da[u].rearrange("p (b t) -> p b t", t=SEQ)[:, :, 1:SEQ],
                                           delta_bank[u].rearrange("p h (b t) -> p (h b) t", t=SEQ)[:, :, 1:SEQ],
                                           ACT.Exp, scale=neg_a[:, bass.ds(g * 32 + j * 2 + u, 1)])\
                                .then_inc(act_in.sem, 1)
                        for u in range(2):
                            act.wait_ge(pe_in.sem, pe_in.at(t, f"y{u}"))
                            act.copy(onehot[u], cst["slide"][:, bass.ds(g * -32 + j * -2 + (127 - u), 128)])\
                                .then_inc(act_in.sem, 1)
                act.wait_ge(pe_q.sem, pe_q.at(q, "last"))
                act.copy(U[:, bass.ds(q * QUARTER, QUARTER)].rearrange("p (h t) -> p h t", h=2), y_bank)\
                    .then_inc(act_q.sem, 1)

        @block.vector
        def _(dve):
            for s in (dve_in, dve_q):
                s.prime(dve)
            with dve.Fori(0, QUARTERS) as q:
                dve.wait_ge(pool_in.sem, pool_in.before(q * 64, "hc1"))
                dve.wait_ge(pe_in.sem, pe_in.before(q * 64, "bu1"))
                for s, src, dst in (("d", delta, DS), ("u", U, US)):
                    value = src[:, bass.ds(q * QUARTER, QUARTER)]
                    for n in (1, 2, 3):
                        dve.tensor_copy(low, value).then_inc(dve_q.sem, 1)
                        dve.wait_ge(dve_q.sem, dve_q.at(q, f"{s}t{n}"))
                        for g in range(4):
                            last = dve.tensor_copy(dst[32 * (n - 1):32 * n, g * QUARTER:(g + 1) * QUARTER],
                                                   low[32 * g:32 * g + 32, :])
                        if n < 3:
                            dve.tensor_tensor(rest, value, low, ALU.subtract).then_inc(dve_q.sem, 1)
                            dve.wait_ge(dve_q.sem, dve_q.at(q, f"{s}r{n}"))
                            value = rest
                        else:
                            last.then_inc(dve_q.sem, 1)
                            if s == "d":
                                dve.wait_ge(dve_q.sem, dve_q.at(q, "ds"))
                with dve.Fori(0, 4) as g:
                    with dve.Fori(0, 16) as j:
                        t = q * 64 + g * 16 + j
                        for u in range(2):
                            dve.wait_ge(pe_in.sem, pe_in.at(t, f"bu{u}"))
                            dve.wait_ge(pool_in.sem, pool_in.before(t, f"hc{u}"))
                            dve.tensor_tensor(bx[u].rearrange("p (h t) -> p h t", h=2),
                                              u_bank, B[:, bass.ds(q * QUARTER, QUARTER)]
                                              .rearrange("p (h t) -> p h t", h=2), ALU.mult).then_inc(dve_in.sem, 1)
                            dve.wait_ge(dve_in.sem, dve_in.at(t, f"bx{u}"))
                            dve.wait_ge(act_in.sem, act_in.at(t, f"da{u}"))
                            dve.tensor_tensor_scan(bx[u], da[u], bx[u], 0.0, ALU.mult, ALU.add)\
                                .then_inc(dve_in.sem, 1)

        @block.gpsimd
        def _(pool):
            for s in (pool_in, pool_q):
                s.prime(pool)
            with pool.Fori(0, QUARTERS) as q:
                pool.wait_ge(pe_q.sem, pe_q.before(q, "last"))
                pool.wait_ge(act_q.sem, act_q.at(q, "c"))
                for u in range(2):
                    last = pool.tensor_tensor(hc[u], nothing, nothing, ALU.mult)
                last.then_inc(pool_q.sem, 1)
                with pool.Fori(0, 64) as j:
                    t = q * 64 + j
                    for u in range(2):
                        pool.wait_ge(pe_in.sem, pe_in.at(t, f"y{u}"))
                        pool.wait_ge(dve_in.sem, dve_in.at(t, f"h{u}"))
                        pool.tensor_tensor(hc[u], bx[u], cq, ALU.mult).then_inc(pool_in.sem, 1)


def l0_attn_a(k, name, w, weights):
    norm_stage(k, f"{name}_ln", k.X, [(k.Z, None, None)], True, "eps5")
    norm_stage(k, f"{name}_rms1", k.Z, [(k.H, w["norm_attn"], None)], False, "eps6")
    softmax_attention(k, f"{name}_attn", k.H, w["wq"], w["wk"], w["wv"], False, qn=w["qn"], kn=w["kn"],
                      rope=(k.c["rot_halves"], k.c["cos_halves"], k.c["sin_halves"]), eps="eps6")
    output_stage(k, f"{name}_o", [(w["wo"], k.H, SEQ)], k.Z, k.Y, factor=0.5)
    norm_stage(k, f"{name}_rms2", k.Z, [(k.H, w["norm_ssm"], None)], False, "eps6")
    k.arena.reset()
    B, C, U = (k.arena.take(TOKENS) for _ in range(3))
    kept = k.arena.used
    ssm_gates_stage(k, f"{name}_gates", k.H, w, B, C, U)
    k.arena.used = kept
    ssm_delta_stage(k, f"{name}_delta", k.H, w, U)
    region = Region(k.wbig, WBIG)
    cst = weights.get("ssm_scan")
    region.take(sum(n for _, n in k.layouts["ssm_scan"].values()))
    scan_stage(k, f"{name}_scan", k.Z, w, cst, k.H, B, C, U, region)
    weights.big_done()
    output_stage(k, f"{name}_so", [(w["wout"], U, 0)], k.Y, k.Y, factor=0.5)
    norm_stage(k, f"{name}_rms3", k.Y, [(k.H, w["norm_ffn"], None)], False, "eps6")
    gated_mlp_stage(k, f"{name}_mlp", k.H, [128] * 4, w["w_lin"], w["w_act"], None, None, w["w_out"], ACT.Silu,
                    SILU_SET, k.Y, k.Y, None)
    add_stage(k, f"{name}_add", k.Y, k.X)


def l0_attn_a_groups(i):
    A, f = "L0_attn_a_", np.float32
    heads = np.repeat(np.arange(4), 4)

    def repeated(m):
        return m.reshape(128, 4, 8)[:, heads].reshape(128, 128)

    w1 = i[A + "W1"]
    g = {"wq": i[A + "Wq"], "wk": repeated(i[A + "Wk"]), "wv": repeated(i[A + "Wv"]), "wo": i[A + "Wo"],
         "wx": i[A + "Wx"], "wdt": i[A + "Wdt"], "a_log": i[A + "A_log"].T, "wsel": i[A + "Wsel"],
         "wimp": i[A + "Wimp"], "wg": i[A + "Wg"], "wout": i[A + "Wout"], "w_act": w1[:, 0:512],
         "w_lin": w1[:, 512:], "w_out": i[A + "W2"].reshape(4, 128, 128).transpose(1, 0, 2)}
    for n, name in (("norm_attn", "norm_attn_w"), ("norm_ssm", "ssm_norm_w"), ("norm_ffn", "norm_ffn_w"),
                    ("bdt", "bdt"), ("dp", "Dp"), ("bsel", "bsel"), ("sel_gate", "sel_gate"), ("bimp", "bimp"),
                    ("bg", "bg")):
        g[n] = column(i[A + name])
    g["qn"], g["kn"] = column(np.tile(i[A + "qn_w"], 16)), column(np.tile(i[A + "kn_w"], 16))
    pick = np.zeros((128, 32, 128), f)
    for d in range(32):
        for part in range(3):
            pick[32 * part + d, d] = 1
    slide = np.zeros((128, 255), f)
    slide[:, 127] = 1
    scan = {"pick": bf16_pairs(pick.reshape(128, -1)), "slide": slide}
    return g, scan
def zero_stage(k, name, fills):
    filled = Count(k, "filled", len(fills))
    with k.nc.Block() as block:
        @block.vector
        def _(dve):
            for ap, value in fills:
                dve.memset(ap, value).then_inc(filled.sem, 1)
            dve.wait_ge(filled.sem, filled.at(len(fills)))


def views(tensor, layout):
    return {name: tensor[:, at:at + n] for name, (at, n) in layout.items()}


def attention_buffers(k):
    k.arena.reset()
    q = k.arena.take((BATCH + 2) * SEQ)
    kk = k.arena.take((BATCH + 2) * SEQ)
    v = k.arena.take((2 * BATCH + 2) * HEADS * VCOLS).rearrange("p (t c) -> p t c", c=HEADS * VCOLS)
    k.arena_kept = k.arena.used
    last = (BATCH + 1) * SEQ
    fills = [(q[:, 0:SEQ], 0.0), (q[:, last:last + SEQ], 0.0), (kk[:, 0:SEQ], 0.0), (kk[:, last:last + SEQ], 0.0),
             (v.rearrange("p t c -> p (t c)"), 1.0)]
    return q, kk, v, fills


def softmax_attention(k, name, src, wq, wk, wv, causal, bv=None, **project):
    q, kk, v, fills = attention_buffers(k)
    zero_stage(k, f"{name}_pad", fills)
    project_stage(k, f"{name}_qkv", src, wq, wk, wv, q, kk, v, **project)
    attention_stage(k, name, q, kk, v, k.H, causal, HEAD_DIM ** -0.5, bv=bv)


def network(nc, stages, arrays, layouts, out):
    with ExitStack() as ctx:
        k = Core(nc, ctx)
        k.X = k.sb("X", [128, TOKENS])
        k.Z = k.sb("Z", [128, TOKENS])
        k.Y_padded = k.sb("Y", [128, SEQ + TOKENS])
        k.Y = k.Y_padded[:, SEQ:SEQ + TOKENS]
        k.H = k.sb("H", [128, TOKENS + SEQ])
        k.arena = Region(k.sb("arena", [128, ARENA]), ARENA)
        k.wbig = k.sb("wbig", [128, WBIG])
        k.wsmall = k.sb("wsmall", [128, WSMALL])
        cst = k.sb("cst", [128, arrays["constants"].shape[1]])
        cstb = k.sb("cstb", [128, arrays["constants_bf16"].shape[1]])
        k.shift = k.sb("shift", [128, SEQ], BF16)
        k.psum = ctx.enter_context(nc.psum_tensor("banks", [128, 8, 512], F32))
        k.c = views(cst, layouts["constants"])
        cb = {n: a.bitcast(BF16) for n, a in views(cstb, layouts["constants_bf16"]).items()}
        cb["pick_head"] = cb["pick_head"].rearrange("p (h m) -> p h m", h=HEADS)
        k.cb = cb

        k.layouts = layouts
        weights = Weights(k, arrays, layouts, stages)
        copy_dram_stage(k, "load", [(k.X[:, :], arrays["x"]), (cst[:, :], arrays["constants"]),
                                    (cstb[:, :], arrays["constants_bf16"])])
        zero_stage(k, "shift", [(k.shift[:, :], 0.0)])
        for n, stage in enumerate(stages):
            run_stage(k, n, stage, weights)
            weights.stage_done(n)
        copy_dram_stage(k, "store", [(out, k.X[:, :])])


SMALL_USERS = ("l0_attn_a", "attn_b", "l1_attn_a", "l1_attn_b")
BIG_USERS = {"l0_attn_a": "ssm_scan", "l0_ffn": "l0_ffn", "l1_ffn": "l1_ffn"}


class Weights:

    def __init__(self, k, arrays, layouts, stages):
        self.k, self.arrays, self.layouts, self.stages = k, arrays, layouts, stages
        self.small = [s for s in stages if s in SMALL_USERS]
        self.big = [BIG_USERS[s] for s in stages if s in BIG_USERS]
        self.coming, self.held = {}, {}
        self.fetch("small", self.small)
        self.fetch("big", self.big)

    def fetch(self, side, queue):
        if not queue:
            return
        which = queue[0]
        while queue and queue[0] == which:
            queue.pop(0)
        tensor = self.k.wsmall if side == "small" else self.k.wbig
        landed = Count(self.k, f"{side}_landed", 16)
        part = tensor[:, 0:self.arrays[which].shape[1]]
        with self.k.nc.Block() as block:
            @block.sync
            def _(sp):
                sp.dma_start(part, self.arrays[which]).then_inc(landed.sem, 16)
        self.coming[which] = landed
        self.held[which] = views(tensor, self.layouts[which])

    def get(self, which):
        if which in self.coming:
            landed = self.coming.pop(which)
            with self.k.nc.Block() as block:
                @block.sync
                def _(sp):
                    sp.wait_ge(landed.sem, landed.at(16))
        return self.held[which]

    def big_done(self):
        self.fetch("big", self.big)

    def stage_done(self, n):
        if self.stages[n] in SMALL_USERS:
            self.fetch("small", self.small)
        later = [BIG_USERS[s] for s in self.stages[n + 1:] if s in BIG_USERS]
        if self.stages[n] in ("l0_ffn", "l1_ffn") and later and later[0] != self.stages[n]:
            self.big_done()


def run_stage(k, n, stage, weights):
    if stage == "attn_b":
        w = weights.get("attn_b")
        norm_stage(k, f"n{n}a", k.X, [(k.Z, None, None)], True, "eps5")
        norm_stage(k, f"n{n}b", k.Z, [(k.H, w["g"], None)], True, "eps5")
        softmax_attention(k, f"attn{n}", k.H, w["wq"], w["wk"], w["wv"], True)
        output_stage(k, f"o{n}", [(w["wo"], k.H, SEQ)], k.X, k.X)
    elif stage == "l1_attn_a":
        w = weights.get("l1_attn_a")
        norm_stage(k, f"n{n}a", k.X, [(k.H, None, None)], True, "eps5")
        softmax_attention(k, f"attn{n}", k.H, w["wq"], w["wk"], w["wv"], True, bv=w["bv"], bq=w["bq"], bk=w["bk"],
                          rope=(k.c["rot_pairs"], k.c["cos_pairs"], k.c["sin_pairs"]))
        output_stage(k, f"o{n}", [(w["wo"], k.H, SEQ)], k.X, k.X, bias=w["bo"])
    elif stage == "l1_ffn":
        l1_ffn(k, f"moe{n}", weights.get("l1_ffn"))
    elif stage == "l0_ffn":
        l0_ffn(k, f"ffn{n}", weights.get("l0_ffn"))
    elif stage == "l1_attn_b":
        l1_attn_b(k, f"rf{n}", weights.get("l1_attn_b"))
    elif stage == "l0_attn_a":
        l0_attn_a(k, f"a{n}", weights.get("l0_attn_a"), weights)
    else:
        raise ValueError(stage)


ARENA = 18944
WBIG = 8704
WSMALL = 3200


def constants():
    f = np.float32
    eye = np.eye(128, dtype=f)
    feature = np.arange(128)
    c = {
        "mean": np.full((128, 128), 1.0 / 128, f),
        "center": (eye - 1.0 / 128).astype(f),
        "ident": eye,
        "ones": np.ones((128, 128), f),
        "head_mean": (feature[:, None] // 8 == feature[None, :] // 8).astype(f) / 8,
        "head_mask": (feature[:, None] // 8 == np.arange(16)[None, :]).astype(f),
        "reverse": np.tile(np.arange(8, 0, -1, dtype=f), (128, 1)),
        "eps5": np.full((128, 1), 1e-5, f),
        "eps6": np.full((128, 1), 1e-6, f),
    }

    inv = (1.0 / 10000.0 ** (np.arange(0, 8, 2, dtype=f) / f(8))).astype(f)
    ang = (np.arange(SEQ, dtype=f)[None, :] * inv[:, None]).astype(f)
    halves = np.tile(np.concatenate([ang, ang], 0), (16, 1))
    pairs = np.tile(np.repeat(ang, 2, axis=0), (16, 1))
    c["rot_halves"], c["cos_halves"], c["sin_halves"] = rotation(8, False), np.cos(halves), np.sin(halves)
    c["rot_pairs"], c["cos_pairs"], c["sin_pairs"] = rotation(8, True), np.cos(pairs), np.sin(pairs)
    token = np.arange(128)
    later = token[None, :] > token[:, None]
    b = {"ident": eye, "causal_qk": np.where(later, NEG, 0), "causal_kq": np.where(later.T, NEG, 0)}
    pick = np.zeros((128, 16, 128), f)
    for h in range(16):
        pick[h, h] = 1
    b["pick_head"] = pick.reshape(128, -1)
    b = {name: bf16_pairs(a) for name, a in b.items()}
    return c, b


def rotation(width, pairs):
    f, feature = np.float32, np.arange(128)
    r = np.zeros((128, 128), f)
    for m in feature:
        base, j = m - m % width, m % width
        if pairs:
            r[m, m + 1 if j % 2 == 0 else m - 1] = -1 if j % 2 == 0 else 1
        else:
            half = width // 2
            r[m, m + half if j < half else m - half] = -1 if j < half else 1
    return np.ascontiguousarray(r.T)


def bf16_pairs(a):
    bits = (np.ascontiguousarray(a, np.float32).view(np.uint32) >> 16).astype(np.uint16)
    return bits.view(np.float32)


def packed(parts):
    layout, at, cols = {}, 0, []
    for name, a in parts.items():
        a = a.reshape(a.shape[0], -1)
        if a.shape[0] < 128:
            a = np.concatenate([a, np.zeros((128 - a.shape[0], a.shape[1]), a.dtype)], 0)
        layout[name] = (at, a.shape[1])
        at += a.shape[1]
        cols.append(a)
    return np.ascontiguousarray(np.concatenate(cols, 1)), layout


def column(a):
    return a.reshape(-1, 1)


STAGES = ['l0_attn_a', 'l0_ffn', 'attn_b', 'l0_ffn', 'l1_attn_a', 'l1_ffn', 'l1_attn_b', 'l1_ffn']


def kernel(**inputs):
    import concourse.bacc as _bacc
    from concourse.bass_utils import run_bass_kernel_spmd as _run

    i = {n: np.asarray(a) for n, a in inputs.items()}
    c, b = constants()
    groups = {"constants": c, "constants_bf16": b}
    A = "L0_attn_b_"
    groups["attn_b"] = {"wq": i[A + "Wq"], "wk": i[A + "Wkv"][:, 0:128], "wv": i[A + "Wkv"][:, 128:256],
                        "wo": i[A + "Wo"], "g": column(i[A + "g_ln"])}
    A = "L1_attn_a_"
    w, bb = i[A + "qkv_w"], i[A + "qkv_b"]
    groups["l1_attn_a"] = {"wq": w[0:128].T, "wk": w[128:256].T, "wv": w[256:384].T, "wo": i[A + "proj_w"].T,
                           "bq": column(bb[0:128]), "bk": column(bb[128:256]), "bv": column(bb[256:384]),
                           "bo": column(i[A + "proj_b"])}
    more_groups(groups, i)
    nc = _bacc.Bacc("TRN2", target_bir_lowering=False, num_devices=1)
    sent = {"x": np.ascontiguousarray(i["L0_attn_a_x"].reshape(TOKENS, DIM).T)}
    layouts = {}
    for name, parts in groups.items():
        sent[name], layouts[name] = packed(parts)
    dram = {n: nc.dram_tensor(f"in_{n}", a.shape, mybir.dt.from_np(a.dtype), kind="ExternalInput").ap()
            for n, a in sent.items()}
    out = nc.dram_tensor("out_x", (DIM, TOKENS), F32, kind="ExternalOutput").ap()
    network(nc, STAGES, dram, layouts, out)
    r = _run(nc, [{f"in_{n}": a for n, a in sent.items()}], core_ids=[0])
    return np.ascontiguousarray(r.results[0]["out_x"].T).reshape(BATCH, SEQ, DIM)
```
